# Optimizing a Trainium2 kernel written in Bass

```python
import numpy as np
import jax
import jax.numpy as jnp

def _softmax(x, axis=-1):
    return jax.nn.softmax(x, axis=axis)

def _gelu(x):
    return jax.nn.gelu(x, approximate=True)

def _silu(x):
    return jax.nn.silu(x)

def _sigmoid(x):
    return jax.nn.sigmoid(x)

def _layernorm(x, axis=-1, eps=1e-05):
    m = jnp.mean(x, axis=axis, keepdims=True)
    v = jnp.var(x, axis=axis, keepdims=True)
    return (x - m) / jnp.sqrt(v + eps)

def _scatter_add(tgt, idx, src, axis=0):
    return tgt.at[idx].add(src)

def _segment_sum(src, seg, n):
    return jax.ops.segment_sum(src, seg, n)
kernel_name = 'mk_seq_preln_d1_jaxref_r4_e858f2'

def setup_inputs(seed: int=0):
    np.random.seed(seed)
    _w = jnp.asarray

    def _L0_attn_setup():
        import jax, jax.numpy as jnp
        import numpy as np
        B, S, DIN, DOUT, H, KVH = (2, 512, 256, 256, 16, 16)
        HD = DOUT // H
        CB = 16
        CS = 16
        SB = 8
        TOPK = 2
        WIN = 64
        SCALE = 1.0 / np.sqrt(HD)

        def _rope(x, hd):
            b, s, d = x.shape
            xh = x.reshape(b, s, d // hd, hd)
            half = hd // 2
            inv = 1.0 / 10000.0 ** (jnp.arange(half, dtype=jnp.float32) * 2.0 / hd)
            ang = jnp.arange(s, dtype=jnp.float32)[:, None] * inv[None, :]
            cos = jnp.cos(ang)[None, :, None, :]
            sin = jnp.sin(ang)[None, :, None, :]
            x1, x2 = (xh[..., 0::2], xh[..., 1::2])
            out = jnp.stack([x1 * cos - x2 * sin, x1 * sin + x2 * cos], axis=-1)
            return out.reshape(b, s, d)

        def _masked_softmax(scores, mask):
            s = jnp.where(mask, scores, -jnp.inf)
            m = jnp.max(s, axis=-1, keepdims=True)
            m = jnp.where(jnp.isfinite(m), m, jnp.zeros_like(m))
            e = jnp.exp(s - m)
            den = jnp.sum(e, axis=-1, keepdims=True)
            return jnp.where(den > 0, e / jnp.where(den > 0, den, 1.0), jnp.zeros_like(e))
        key = jax.random.key(seed)
        ks = jax.random.split(key, 12)
        sc_in = 1.0 / np.sqrt(DIN)
        sc_out = 1.0 / np.sqrt(DOUT)
        return {'x': jax.random.normal(ks[0], (B, S, DIN), jnp.float32), 'Wq': jax.random.normal(ks[1], (DIN, DOUT), jnp.float32) * sc_in, 'Wk': jax.random.normal(ks[2], (DIN, KVH * HD), jnp.float32) * sc_in, 'Wv': jax.random.normal(ks[3], (DIN, KVH * HD), jnp.float32) * sc_in, 'Wo': jax.random.normal(ks[4], (DOUT, DOUT), jnp.float32) * sc_out, 'bo': jnp.zeros((DOUT,), jnp.float32), 'wk_comp': jax.random.normal(ks[5], (CB,), jnp.float32), 'wv_comp': jax.random.normal(ks[6], (CB,), jnp.float32), 'pe': jax.random.normal(ks[7], (CB, KVH * HD), jnp.float32), 'Wg': jax.random.normal(ks[8], (DIN, 3), jnp.float32) * sc_in, 'bg': jnp.zeros((3,), jnp.float32)}
    _L0_attn_in = _L0_attn_setup()

    def _L0_ffn_setup():
        import jax, jax.numpy as jnp
        import numpy as np
        B, S, K, N = (8, 2048, 256, 256)
        key = jax.random.key(seed)
        k1, k2, k3, k4 = jax.random.split(key, 4)
        x = jax.random.normal(k1, (B, S, K), dtype=jnp.float32)
        CB = jnp.clip(jnp.round(jax.random.normal(k2, (N, K), dtype=jnp.float32) * 42.0), -127.0, 127.0)
        SCB = jax.random.uniform(k3, (N,), dtype=jnp.float32, minval=0.5, maxval=2.0)
        bias = jax.random.normal(k4, (N,), dtype=jnp.float32) * 0.02
        return {'x': x, 'CB': CB, 'SCB': SCB, 'bias': bias}
    _L0_ffn_in = _L0_ffn_setup()
    _d = {'L0_attn_x': _L0_attn_in['x'], 'L0_attn_Wq': _L0_attn_in['Wq'], 'L0_attn_Wk': _L0_attn_in['Wk'], 'L0_attn_Wv': _L0_attn_in['Wv'], 'L0_attn_Wo': _L0_attn_in['Wo'], 'L0_attn_bo': _L0_attn_in['bo'], 'L0_attn_wk_comp': _L0_attn_in['wk_comp'], 'L0_attn_wv_comp': _L0_attn_in['wv_comp'], 'L0_attn_pe': _L0_attn_in['pe'], 'L0_attn_Wg': _L0_attn_in['Wg'], 'L0_attn_bg': _L0_attn_in['bg'], 'L0_ffn_CB': _L0_ffn_in['CB'], 'L0_ffn_SCB': _L0_ffn_in['SCB'], 'L0_ffn_bias': _L0_ffn_in['bias']}
    _x0 = _d['L0_attn_x']
    _d['L0_attn_x'] = jax.random.normal(jax.random.fold_in(jax.random.key(seed), 1), (8, 1024, 256), dtype=_x0.dtype)
    del _x0
    return _d

def reference(L0_attn_x, L0_attn_Wq, L0_attn_Wk, L0_attn_Wv, L0_attn_Wo, L0_attn_bo, L0_attn_wk_comp, L0_attn_wv_comp, L0_attn_pe, L0_attn_Wg, L0_attn_bg, L0_ffn_CB, L0_ffn_SCB, L0_ffn_bias):

    def _L0_attn_ref(x, Wq, Wk, Wv, Wo, bo, wk_comp, wv_comp, pe, Wg, bg):
        import jax, jax.numpy as jnp
        import numpy as np
        B, S, DIN, DOUT, H, KVH = (2, 512, 256, 256, 16, 16)
        HD = DOUT // H
        CB = 16
        CS = 16
        SB = 8
        TOPK = 2
        WIN = 64
        SCALE = 1.0 / np.sqrt(HD)

        def _rope(x, hd):
            b, s, d = x.shape
            xh = x.reshape(b, s, d // hd, hd)
            half = hd // 2
            inv = 1.0 / 10000.0 ** (jnp.arange(half, dtype=jnp.float32) * 2.0 / hd)
            ang = jnp.arange(s, dtype=jnp.float32)[:, None] * inv[None, :]
            cos = jnp.cos(ang)[None, :, None, :]
            sin = jnp.sin(ang)[None, :, None, :]
            x1, x2 = (xh[..., 0::2], xh[..., 1::2])
            out = jnp.stack([x1 * cos - x2 * sin, x1 * sin + x2 * cos], axis=-1)
            return out.reshape(b, s, d)

        def _masked_softmax(scores, mask):
            s = jnp.where(mask, scores, -jnp.inf)
            m = jnp.max(s, axis=-1, keepdims=True)
            m = jnp.where(jnp.isfinite(m), m, jnp.zeros_like(m))
            e = jnp.exp(s - m)
            den = jnp.sum(e, axis=-1, keepdims=True)
            return jnp.where(den > 0, e / jnp.where(den > 0, den, 1.0), jnp.zeros_like(e))
        b, s, _ = x.shape
        q = _rope(x @ Wq, HD)
        k = _rope(x @ Wk, HD)
        v = x @ Wv
        nb = (s - CB) // CS + 1
        kb = k[:, :nb * CS].reshape(b, nb, CB, -1) + pe[None, None]
        vb = v[:, :nb * CS].reshape(b, nb, CB, -1) + pe[None, None]
        ck = jnp.einsum('bnkd,k->bnd', kb, wk_comp)
        cv = jnp.einsum('bnkd,k->bnd', vb, wv_comp)
        q4 = q.reshape(b, s, H, HD).transpose(0, 2, 1, 3)
        k4 = k.reshape(b, s, KVH, HD).transpose(0, 2, 1, 3)
        v4 = v.reshape(b, s, KVH, HD).transpose(0, 2, 1, 3)
        ck4 = ck.reshape(b, nb, KVH, HD).transpose(0, 2, 1, 3)
        cv4 = cv.reshape(b, nb, KVH, HD).transpose(0, 2, 1, 3)
        sc = jnp.einsum('bhsd,bhnd->bhsn', q4, ck4) * SCALE
        comp_mask = (jnp.arange(nb) + 1) * CS <= jnp.arange(s)[:, None]
        a_comp = _masked_softmax(sc, comp_mask[None, None])
        out_comp = jnp.einsum('bhsn,bhnd->bhsd', a_comp, cv4).transpose(0, 2, 1, 3).reshape(b, s, DOUT)
        imp = sc.mean(axis=(1, 2))
        _, top_idx = jax.lax.top_k(imp, TOPK)
        pos = (top_idx * CS)[:, :, None] + jnp.arange(SB)[None, None, :]
        pos = pos.reshape(b, TOPK * SB)
        valid = pos < s
        posc = jnp.minimum(pos, s - 1)
        sel_k = jnp.take_along_axis(k, posc[..., None], axis=1) * valid[..., None]
        sel_v = jnp.take_along_axis(v, posc[..., None], axis=1) * valid[..., None]
        M = TOPK * SB
        ks4 = sel_k.reshape(b, M, KVH, HD).transpose(0, 2, 1, 3)
        vs4 = sel_v.reshape(b, M, KVH, HD).transpose(0, 2, 1, 3)
        ss = jnp.einsum('bhsd,bhmd->bhsm', q4, ks4) * SCALE
        causal_sel = jnp.arange(s)[None, :, None] >= pos[:, None, :]
        a_sel = _masked_softmax(ss, (causal_sel & valid[:, None, :])[:, None])
        out_sel = jnp.einsum('bhsm,bhmd->bhsd', a_sel, vs4).transpose(0, 2, 1, 3).reshape(b, s, DOUT)
        sw = jnp.einsum('bhsd,bhtd->bhst', q4, k4) * SCALE
        rows = jnp.arange(s)[:, None]
        cols = jnp.arange(s)[None, :]
        wmask = (cols <= rows) & (cols > rows - WIN)
        a_win = _masked_softmax(sw, wmask[None, None])
        out_win = jnp.einsum('bhst,bhtd->bhsd', a_win, v4).transpose(0, 2, 1, 3).reshape(b, s, DOUT)
        g = jax.nn.softmax(x @ Wg + bg, axis=-1)
        out = g[..., 0:1] * out_comp + g[..., 1:2] * out_sel + g[..., 2:3] * out_win
        return out @ Wo + bo

    def _L0_ffn_ref(x, CB, SCB, bias):
        import jax, jax.numpy as jnp
        import numpy as np
        B, S, K, N = (8, 2048, 256, 256)
        out = jnp.einsum('bsk,nk->bsn', x, CB)
        out = out * (SCB * (1.0 / 127.0)) + bias
        return out
    x = L0_attn_x
    x = x + _L0_attn_ref(_layernorm(x, axis=-1), L0_attn_Wq, L0_attn_Wk, L0_attn_Wv, L0_attn_Wo, L0_attn_bo, L0_attn_wk_comp, L0_attn_wv_comp, L0_attn_pe, L0_attn_Wg, L0_attn_bg)
    x = x + _L0_ffn_ref(_layernorm(x, axis=-1), L0_ffn_CB, L0_ffn_SCB, L0_ffn_bias)
    return x

_drawn_inputs = setup_inputs


def setup_inputs(seed=0):
    import zlib

    import numpy as np

    out = dict(_drawn_inputs(seed))
    spreads = {'L0_attn_bo': (0.0, 0.1), 'L0_attn_bg': (0.0, 0.597)}
    factors = {'L0_ffn_bias': 22.42}
    for name, (base, spread) in spreads.items():
        noise = np.random.default_rng([zlib.crc32(name.encode()), seed]).standard_normal(out[name].shape)
        drawn = base * np.exp(spread * noise) if base else spread * noise
        out[name] = jnp.asarray(drawn.astype(out[name].dtype))
    for name, factor in factors.items():
        out[name] = (out[name] * factor).astype(out[name].dtype)
    return out
```

```python
import numpy as np
import concourse.bass as bass
from concourse import mybir
from contextlib import ExitStack

F32 = mybir.dt.float32
BF16 = mybir.dt.bfloat16
U32 = mybir.dt.uint32
ALU = mybir.AluOpType
ACT = mybir.ActivationFunctionType
AX = mybir.AxisListType
ds = bass.ds

P = 128
B, S, D = 8, 1024, 256
H, HD = 16, 16
T = S // P
PAIRS = T // 2
DC = D // P
NB = S // 16
NSEL = 16
WIN = 64
NCS = NB + NSEL
KW = P + WIN
U = 4
NU = H // U
VC = HD + 1
OC = 3 * VC
NP1 = 3 * D + 3
Q_PARTS = (0, 0, 0, 1, 1, 2)
K_PARTS = (0, 1, 2, 0, 1, 0)
NSLOT = len(Q_PARTS)
KR_ROWS = NSLOT * HD
MASKED = -1e30
LEAST = 1e29
EPS = 1e-5


def shape_constants():
    p = np.arange(P)
    t = np.arange(T)

    def bits(a):
        return (np.ascontiguousarray(a, np.float32).view(np.uint32) >> 16).astype(np.uint16)

    j = np.arange(KW) - WIN
    ok = (j[None, :] <= p[:, None]) & (j[None, :] > p[:, None] - WIN)
    ok = ok[:, None, :] & ((t[None, :2, None] * P + j[None, None, :]) >= 0)
    window_mask = np.where(ok, 0.0, MASKED)
    s = t[None, :, None] * P + p[:, None, None]
    n = np.arange(NB)
    cs_mask = np.zeros((P, T, NCS))
    cs_mask[:, :, :NB] = np.where((n[None, None, :] + 1) * 16 <= s, 0.0, MASKED)
    own_mask = np.where((p[:, None] <= p[None, :]) & (p[:, None] > p[None, :] - WIN), 0.0, MASKED)
    pick_w = np.zeros((P, H, KW))
    for part in range(3):
        for h in range(H):
            pick_w[part * H + h, h, :] = 1.0
    for k in range(WIN):
        pick_w[WIN + k, :, P + k] = 1.0
    rows_w = np.zeros((P, S))
    q = np.arange(S)
    kl = np.arange(WIN)
    rows_w[WIN:] = np.where((kl[:, None] > (q % P)[None, :]) & (q[None, :] >= P), 0.0, MASKED)
    pick_cs = np.zeros((P, T, H, NCS))
    for part in range(3):
        for h in range(H):
            pick_cs[part * H + h, :, h, :NB] = 1.0
            pick_cs[48 + part * H + h, :, h, NB:] = 1.0
    for m in range(NSEL):
        pick_cs[96 + m, :, :, NB + m] = 1.0
    for g in range(8):
        pick_cs[112 + g, :, :, :NB] = np.where(n[None, :] >= 8 * t[:, None] + g, MASKED, 0.0)[:, None, :]
    rows_cs = np.zeros((P, S))
    for g in range(8):
        rows_cs[112 + g] = (q % P) // 16 == g
    b16 = {
        "window_mask": window_mask, "cs_mask": cs_mask, "own_mask": own_mask, "pick_w": pick_w,
        "rows_w": rows_w, "pick_cs": pick_cs, "rows_cs": rows_cs, "ident_b": np.eye(P),
    }
    half = HD // 2
    inv = (1.0 / 10000.0 ** (np.arange(half, dtype=np.float32) * np.float32(2.0) / np.float32(HD))).astype(np.float32)
    ang = np.arange(S, dtype=np.float32)[:, None] * inv[None, :]
    cos = np.repeat(np.cos(ang), 2, axis=1)
    sin = np.stack([-np.sin(ang), np.sin(ang)], -1).reshape(S, HD)
    by_tile = lambda a: a.reshape(T, P, HD).transpose(1, 0, 2)
    r = np.arange(8)
    since = (t[None, :, None] * P + p[:, None, None]) - r[None, None, :]
    since_cols = q[None, :] - (np.arange(NSEL) % 8)[:, None]
    block_of = np.zeros((P, T, NCS))
    for pp in range(P):
        for tt in range(T):
            block_of[pp, tt, 8 * tt + pp // 16] = 1.0
    sel_rows = np.zeros((P, 2, P))
    sel_rows[0, 0, 96:104] = 1.0
    sel_rows[0, 1, 104:112] = 1.0
    f32 = {
        "ident_f": np.eye(P), "cos": by_tile(cos), "sin": by_tile(sin), "since": since,
        "since_cols": since_cols, "block_of": block_of, "sel_rows": sel_rows,
    }
    return (
        {k: np.ascontiguousarray(bits(v).reshape(P, -1)) for k, v in b16.items()},
        {k: np.ascontiguousarray(v.astype(np.float32).reshape(v.shape[0], -1)) for k, v in f32.items()},
    )


def build(nc, x, Wq, Wk, Wv, Wo, bo, wk_comp, wv_comp, pe_, Wg, bg, CB, SCB, bias, consts, out):
    ctx = ExitStack()
    with ctx:
        def sb(name, shape, dt=F32):
            return ctx.enter_context(nc.sbuf_tensor(name, shape, dt))

        def sem(name):
            return ctx.enter_context(nc.semaphore(name))

        ident_f = sb("ident_f", [P, P])
        both = sb("both", [P, T * H * VC])
        values_before = both[0:WIN, :].rearrange("p (t h d) -> p t h d", t=T, h=H)
        since_cols = both[96:112, 0:S]
        pe_sb = both[64:80, 0:D]
        wk_rows = both[64:80, D:D + NB]
        wv_rows = both[64:80, D + NB:D + NB + NCS]
        cos = sb("cos", [P, T, HD])
        sin = sb("sin", [P, T, HD])
        since = sb("since", [P, T, 8])
        sel_rows = sb("sel_rows", [P, 2, P])
        ident_b = sb("ident_b", [P, P], BF16)
        window_mask = sb("window_mask", [P, 2, KW], BF16)
        cs_mask = sb("cs_mask", [P, T, NCS], BF16)
        own_mask = sb("own_mask", [P, P], BF16)
        pick_w = sb("pick_w", [P, H, KW], BF16)
        rows_w = sb("rows_w", [P, S], BF16)
        pick_cs = sb("pick_cs", [P, T, H, NCS], BF16)
        rows_cs = sb("rows_cs", [P, S], BF16)
        w_in = sb("w_in", [P, DC, NP1])
        w_out = sb("w_out", [P, DC, D])
        w_ffn = sb("w_ffn", [P, DC, D])
        ones = sb("ones", [P, P])
        bo_all = sb("bo_all", [P, D])
        bias_all = sb("bias_all", [P, D])
        scb_all = sb("scb_all", [P, D])
        bg_all = sb("bg_all", [P, 3])
        wk_col = sb("wk_col", [P, 1])
        wv_col = sb("wv_col", [P, 1])
        comp_k = sb("comp_k", [P, 8])
        gather = sb("gather", [P, T, NCS])
        minus_half = sb("minus_half", [P, 1])
        x_in = sb("x_in", [P, T, D])
        bn6 = sb("bn6", [P, 2, 6])
        mean_var = sb("mean_var", [P, 2, 2])
        var_eps = sb("var_eps", [P, 2])
        rstd = sb("rstd", [P, 2])
        xn = sb("xn", [P, 2, D])
        xnT = sb("xnT", [P, 2, DC, P])
        qk = sb("qk", [P, 2, 2 * D])
        rope_s = sb("rope_s", [P, 2 * D])
        roped = sb("roped", [P, 2, 2 * D])
        rest = sb("rest", [P, 2, 4, P])
        shared = sb("shared", [P, 6144])
        parts = shared[:, 0:3 * 4 * S // 2].bitcast(BF16).rearrange("p (a c s) -> p a c s", a=3, c=4)
        taken = [0]

        def part_of_shared(rows, *shape):
            n = int(np.prod(shape))
            a = shared[0:rows, taken[0]:taken[0] + n]
            taken[0] += n
            names = "abc"[:len(shape)]
            return a.rearrange(f"p ({' '.join(names)}) -> p {' '.join(names)}", **dict(zip(names, shape)))

        k_tok = sb("k_tok", [P, T, D])
        attn = k_tok
        q_sums = sb("q_sums", [P, T, 2])
        values = sb("values", [P, T, H, VC])
        gate = sb("gate", [P, T, 3])
        q_stack = sb("q_stack", [KR_ROWS, H, S], BF16)
        k_stack = sb("k_stack", [KR_ROWS, H, WIN + S], BF16)
        cs_stack = sb("cs_stack", [KR_ROWS, H, NCS], BF16)
        ck = sb("ck", [P, 2, NCS])
        ck_rest = sb("ck_rest", [P, 2, NCS])
        ck_parts = sb("ck_parts", [P, 3, 2, NCS], BF16)
        q_sum = sb("q_sum", [P, 2])
        imp = sb("imp", [1, NB])
        imp_max = sb("imp_max", [1, 8])
        imp_idx = sb("imp_idx", [1, 8], U32)
        sel_start = sb("sel_start", [1, 8])
        start_all = sb("start_all", [P, 3])
        cs_values = sb("cs_values", [NCS, H, 2 * VC])
        branch_gate = sb("branch_gate", [P, T, 3])
        gate_max = sb("gate_max", [P, T])
        gate_sum = sb("gate_sum", [P, T])
        gate_inv = sb("gate_inv", [P, T])
        neg_max = sb("neg_max", [P, 3, H])
        neg_lim = sb("neg_lim", [P, 3, H])
        neg_rest = sb("neg_rest", [P, 3, H])
        neg_parts = sb("neg_parts", [P, 3, 3, H], BF16)
        block_of = shared[:, 6144 - T * NCS:].rearrange("p (t n) -> p t n", t=T)
        p_own = part_of_shared(P, 2, U * P)
        p_cs = part_of_shared(NCS, 2, U * P)
        p_before = part_of_shared(WIN, 2, U * WIN)
        den = sb("den", [P, H, 3])
        den_inv = sb("den_inv", [P, H, 3])
        weight = sb("weight", [P, H, 3])
        weighted = part_of_shared(P, 8, 3, HD)
        tile_before = part_of_shared(WIN, H, VC)
        taken[0] = 0
        x_res = sb("x_res", [P, 2, D])
        attn_t = part_of_shared(P, 2, D)
        attnT = part_of_shared(P, 2, DC, P)
        x1 = part_of_shared(P, 2, D)
        x1b = part_of_shared(P, 2, D)
        x2n = part_of_shared(P, 2, D)
        x2nT = part_of_shared(P, 2, DC, P)
        ffn = part_of_shared(P, 2, D)
        y = sb("y", [P, 2, D])

        ps = ctx.enter_context(nc.psum_tensor("ps", [P, 8, 512], F32))
        part_dram = nc.dram_tensor("part_dram", [3, 2, H, HD, S], BF16).ap()
        cs_dram = nc.dram_tensor("cs_dram", [3, H, HD, NCS], BF16).ap()

        s_const = sem("constants_in")
        s_settled = sem("waits_settled")
        s_setup = sem("setup_vector")
        s_setup_pe = sem("setup_transposed")
        s_w = sem("setup_done")
        s_x = sem("x_in_loaded")
        s_xused = sem("x_in_used")
        s_bn = sem("bn_stats_done")
        s_mv = sem("mean_var_done")
        s_ve = sem("var_eps_done")
        s_rstd = sem("rstd_done")
        s_xn = sem("xn_done")
        s_xt_ps = sem("xn_transposed")
        s_xt = sem("xnT_done")
        s_proj = sem("projected")
        s_qk = sem("qk_copied")
        s_vg = sem("v_and_gate_copied")
        s_rc = sem("rope_products")
        s_rope = sem("roped_done")
        s_ktok = sem("k_tok_done")
        s_qkt = sem("qk_transposed")
        s_hi = sem("high_part")
        s_rest1 = sem("rest_after_high")
        s_mid = sem("mid_part")
        s_lo = sem("low_part")
        s_part_out = sem("parts_in_dram")
        s_stack = sem("stacks_in")
        s_vb = sem("values_before_in")
        s_ck_ps = sem("compressed_keys_summed")
        s_ck = sem("ck_copied")
        s_qsum = sem("q_sum_done")
        s_imp_ps = sem("importance_summed")
        s_top = sem("top_steps")
        s_start_ps = sem("starts_spread")
        s_start = sem("start_all_done")
        s_onehot = sem("one_hot_done")
        s_smask = sem("selected_masks_done")
        s_sel_ps = sem("selected_gathered")
        s_cks = sem("ck_steps")
        s_ckp = sem("ck_parts_done")
        s_csv = sem("cs_values_done")
        s_cs_out = sem("ck_parts_in_dram")
        s_cs_in = sem("cs_stack_in")
        s_gsub = sem("gate_shifted_steps")
        s_gexp = sem("gate_exp")
        s_gate = sem("gate_done_steps")
        s_a = sem("row_scores")
        s_max = sem("row_scores_reduced")
        s_neg = sem("neg_steps")
        s_mt_ps = sem("maxima_transposed")
        s_mt = sem("maxima_copied")
        s_b = sem("column_scores")
        s_exp = sem("probabilities")
        s_pv = sem("probabilities_used")
        s_tb = sem("tile_before_copied")
        s_den = sem("denominator_steps")
        s_wtd = sem("weighted_half")
        s_attn = sem("attention_half")
        s_xr = [sem("x_res_loaded_0"), sem("x_res_loaded_1")]
        s_xrb = sem("x_res_plus_bo")
        s_at = sem("attn_t_copied")
        s_at_ps = sem("attn_transposed")
        s_atT = sem("attnT_copied")
        s_wo = sem("output_projected")
        s_x1 = sem("x1_done")
        s_x1b = sem("x1_plus_bias")
        s_bn2 = sem("bn_stats_2")
        s_mv2 = sem("mean_var_2")
        s_ve2 = sem("var_eps_2")
        s_rstd2 = sem("rstd_2")
        s_x2n = sem("x2n_done")
        s_x2t_ps = sem("x2n_transposed")
        s_x2t = sem("x2nT_copied")
        s_ffn = sem("ffn_projected")
        s_ffs = sem("ffn_scaled")
        s_y = sem("y_done")
        s_out = [sem("y_stored_0"), sem("y_stored_1")]

        loads = [
            (ident_f[:], consts["ident_f"]), (cos[:], consts["cos"]), (sin[:], consts["sin"]),
            (since[:], consts["since"]), (since_cols, consts["since_cols"]),
            (block_of, consts["block_of"]), (sel_rows[:], consts["sel_rows"]),
        ]
        for dst, name in ((ident_b, "ident_b"), (window_mask, "window_mask"), (cs_mask, "cs_mask"),
                          (own_mask, "own_mask"), (pick_w, "pick_w"), (rows_w, "rows_w"),
                          (pick_cs, "pick_cs"), (rows_cs, "rows_cs")):
            loads.append((dst[:], consts[name].bitcast(BF16)))

        def shaped(dst, src):
            if len(dst.shape) == 3:
                src = src.rearrange("p (a b) -> p a b", a=dst.shape[1])
            elif len(dst.shape) == 4:
                src = src.rearrange("p (a b c) -> p a b c", a=dst.shape[1], b=dst.shape[2])
            return src

        loads = [(dst, shaped(dst, src)) for dst, src in loads]
        for k, w in enumerate((Wq, Wk, Wv)):
            loads.append((w_in[:, :, k * D:(k + 1) * D], w.rearrange("(c p) n -> p c n", p=P)))
        loads.append((w_in[:, :, 3 * D:], Wg.rearrange("(c p) n -> p c n", p=P)))
        loads.append((w_out[:], Wo.rearrange("(c p) n -> p c n", p=P)))
        loads.append((x1[:], CB.rearrange("(c p) k -> p c k", p=P)))
        loads.append((pe_sb, pe_))
        for dst, v in ((bo_all, bo), (bias_all, bias), (scb_all, SCB), (bg_all, bg)):
            loads.append((dst[:], v.partition_broadcast(P)))
        for dst, v in ((wk_col, wk_comp), (wv_col, wv_comp)):
            for g in range(8):
                loads.append((dst[16 * g:16 * g + 16, :], v.rearrange("(p a) -> p a", a=1)))

        def done(eng, s, n):
            eng.wait_ge(s, n + 1)

        def settled(eng):
            eng.sem_inc(s_settled, 1)

        def x_tiles(b):
            return x[ds(b, 1)].rearrange("a (t p) d -> p (a t) d", p=P)

        block = ctx.enter_context(nc.Block())

        @block.sync
        def _(sp):
            for dst, src in loads:
                sp.dma_start(dst, src).then_inc(s_const, 16)
            sp.dma_start(x_in[:], x_tiles(0)).then_inc(s_x, 16)
            with sp.Fori(0, B) as b:
                with sp.Fori(0, PAIRS) as i:
                    pair = b * PAIRS + i
                    done(sp, s_lo, pair * 2 + 1)
                    settled(sp)
                    for part in range(3):
                        sp.dma_start(
                            part_dram[part, :, :, :, ds(i * 2 * P, 2 * P)].rearrange("w (g h) d s -> (h d) (w g) s", g=2),
                            parts[:, part, :, ds(i * 2 * P, 2 * P)],
                        ).then_inc(s_part_out, 16)
                    sp.wait_ge(s_part_out, (pair + 1) * 48)
                    settled(sp)
                    for slot in range(NSLOT):
                        rows = slice(slot * HD, slot * HD + HD)
                        sp.dma_start(
                            q_stack[rows, :, ds(i * 2 * P, 2 * P)],
                            part_dram[Q_PARTS[slot], 0, :, :, ds(i * 2 * P, 2 * P)].rearrange("h d s -> d h s"),
                        ).then_inc(s_stack, 16)
                        sp.dma_start(
                            k_stack[rows, :, ds(i * 2 * P + WIN, 2 * P)],
                            part_dram[K_PARTS[slot], 1, :, :, ds(i * 2 * P, 2 * P)].rearrange("h d s -> d h s"),
                        ).then_inc(s_stack, 16)
                done(sp, s_vg, b * T + T - 1)
                sp.dma_start(values_before[:, 1:T], values[WIN:P, 0:T - 1]).then_inc(s_vb, 16)
                done(sp, s_ckp, b)
                for g in range(2):
                    sp.dma_start(cs_dram[:, 8 * g:8 * g + 8].rearrange("a h d n -> (h d) a n"),
                                 ck_parts[:, :, g, :]).then_inc(s_cs_out, 16)
                sp.wait_ge(s_cs_out, (b + 1) * 32)
                for slot in range(NSLOT):
                    sp.dma_start(cs_stack[slot * HD:slot * HD + HD], cs_dram[K_PARTS[slot]].rearrange("h d n -> d h n")).then_inc(s_cs_in, 16)
                done(sp, s_xused, b)
                settled(sp)
                sp.wait_ge(s_x, (b + 1) * 16)
                settled(sp)
                nxt = (b + 1) % B
                sp.dma_start(x_in[:], x_tiles(nxt)).then_inc(s_x, 16)
                for u in range(2):
                    sp.dma_start(x_res[:, u], x[ds(b, 1), u * P:(u + 1) * P].rearrange("a p d -> p (a d)")).then_inc(s_xr[u], 16)
                with sp.Fori(0, PAIRS) as i:
                    for u in range(2):
                        n = b * T + i * 2 + u
                        done(sp, s_y, n)
                        settled(sp)
                        sp.dma_start(out[ds(b, 1), ds((i * 2 + u) * P, P)].rearrange("a p d -> p (a d)"), y[:, u]).then_inc(s_out[u], 16)
                        nxt_tile = ((i + 1) % PAIRS) * 2 + u
                        sp.wait_ge(s_xr[u], (b * (PAIRS + 1) + i + 1) * 16)
                        settled(sp)
                        sp.dma_start(x_res[:, u], x[ds(b, 1), ds(nxt_tile * P, P)].rearrange("a p d -> p (a d)")).then_inc(s_xr[u], 16)
                for u in range(2):
                    sp.wait_ge(s_out[u], (b + 1) * PAIRS * 16)
                settled(sp)
            sp.wait_ge(s_x, (B + 1) * 16)
            for u in range(2):
                sp.wait_ge(s_out[u], B * PAIRS * 16)
                sp.wait_ge(s_xr[u], B * (PAIRS + 1) * 16)

        @block.tensor
        def _(pe):
            pe.wait_ge(s_const, 16 * len(loads))
            for kc in range(DC):
                for ncn in range(DC):
                    last = pe.transpose(ps[:, kc, ncn * P:(ncn + 1) * P], x1[:, ncn, kc * P:(kc + 1) * P], ident_f[:])
            last.then_inc(s_setup_pe, 1)
            pe.wait_ge(s_w, 3)

            def front(b, i, first):
                for u in range(2):
                    n = b * T + i * 2 + u
                    done(pe, s_xn, n)
                    if not first:
                        pe.wait_ge(s_xt, n - 1)
                    for c in range(DC):
                        last = pe.transpose(ps[:, 4 * u, c * P:(c + 1) * P], xn[:, u, c * P:(c + 1) * P], ident_f[:])
                    last.then_inc(s_xt_ps, 1)
                for u in range(2):
                    n = b * T + i * 2 + u
                    done(pe, s_xt, n)
                    if not first:
                        pe.wait_ge(s_vg, n - 1)
                    for c in range(DC):
                        pe.matmul(ps[:, 4 * u + 1, :], xnT[:, u, c, :], w_in[:, c, 0:2 * D], start=c == 0, stop=c == DC - 1)
                    for c in range(DC):
                        last = pe.matmul(ps[:, 4 * u + 2, 0:D + 3], xnT[:, u, c, :], w_in[:, c, 2 * D:], start=c == 0, stop=c == DC - 1)
                    last.then_inc(s_proj, 1)

            def back(b, i, first):
                for u in range(2):
                    n = b * T + i * 2 + u
                    done(pe, s_rope, n)
                    if not first:
                        pe.wait_ge(s_rest1, n - 1)
                    for c in range(4):
                        last = pe.transpose(ps[:, 4 * u + 3, c * P:(c + 1) * P], roped[:, u, c * P:(c + 1) * P], ident_f[:])
                    last.then_inc(s_qkt, 1)

            def selection(b):
                done(pe, s_ktok, b * T + T - 1)
                done(pe, s_rest1, b * T + T - 1)
                done(pe, s_vg, b * T + T - 1)
                for g in range(2):
                    pe.matmul(ps[:, 0, g * NB:(g + 1) * NB], pe_sb[:, g * P:(g + 1) * P], wk_rows, start=g == 0, stop=False, skip_group_check=True)
                    for t in range(T):
                        last = pe.matmul(ps[:, 0, g * NB + 8 * t:g * NB + 8 * t + 8], k_tok[:, t, g * P:(g + 1) * P], comp_k[:],
                                         start=False, stop=True, skip_group_check=True)
                last.then_inc(s_ck_ps, 1)
                done(pe, s_ck, b)
                done(pe, s_qsum, b)
                for g in range(2):
                    last = pe.matmul(ps[0:1, 1, 0:NB], q_sum[:, g:g + 1], ck[:, g, 0:NB], start=g == 0, stop=g == 1)
                last.then_inc(s_imp_ps, 1)
                done(pe, s_top, b * 4 + 3)
                pe.matmul(ps[:, 2, 0:2], ones[0:1, :], sel_start[0:1, 0:2], start=True, stop=True)
                for j in range(2):
                    last = pe.matmul(ps[:, 2, 2:3], sel_rows[0:1, j, :], sel_start[0:1, j:j + 1], start=j == 0, stop=j == 1)
                last.then_inc(s_start_ps, 1)
                done(pe, s_onehot, b * 2 + 1)
                for g in range(2):
                    for t in range(T):
                        pe.matmul(ps[:, 4, g * NSEL:(g + 1) * NSEL], k_tok[:, t, g * P:(g + 1) * P], gather[:, t, NB:NCS], start=t == 0, stop=t == T - 1)
                for t in range(T):
                    vt = values[:, t, :, 0:HD]
                    pe.matmul(ps[0:NCS, 5, 0:D], gather[:, t, :], vt, start=t == 0, stop=False)
                pe.matmul(ps[0:NCS, 5, 0:D], wv_rows, pe_sb, start=False, stop=True).then_inc(s_sel_ps, 1)

            def row_scores(b, t, c, first, tile_0=False):
                if not first:
                    pe.wait_ge(s_max, (b * T + t) * NU + c)
                if c == 0 and not first:
                    pe.wait_ge(s_mt, 2 * (b * T + t))
                for hh in range(U):
                    h = c * U + hh
                    qs = q_stack[:, h, ds(t * P, P)]
                    pe.matmul(ps[:, hh // 2, (hh % 2) * KW:(hh % 2 + 1) * KW], qs, k_stack[:, h, ds(t * P, KW)],
                              start=hh % 2 == 0, stop=False, skip_group_check=True)
                    pe.matmul(ps[:, 2, hh * NCS:(hh + 1) * NCS], qs, cs_stack[:, h, :], start=hh == 0, stop=False, skip_group_check=True)
                for j in range(2):
                    pe.matmul(ps[:, j, 0:2 * KW].rearrange("p (h k) -> p h k", h=2), ident_b[:],
                              window_mask[:, (0 if tile_0 else 1):(1 if tile_0 else 2), :].broadcast_to([P, 2, KW]), start=False, stop=True, skip_group_check=True)
                pe.matmul(ps[:, 2, 0:U * NCS].rearrange("p (h k) -> p h k", h=U), ident_b[:],
                          cs_mask[:, ds(t, 1), :].broadcast_to([P, U, NCS]), start=False, stop=True, skip_group_check=True).then_inc(s_a, 1)

            def maxima(b, t):
                done(pe, s_neg, (b * T + t) * 5 + 4)
                settled(pe)
                w = ps[0:48, 2, 0:64].bitcast(BF16)
                cs = ps[0:96, 2, 64:128].bitcast(BF16)
                pe.transpose(w, neg_parts[:, 0].rearrange("p a h -> p (a h)"), ident_b[:])
                pe.transpose(cs, neg_parts[:, 1:3].rearrange("p r a h -> p (r a h)"), ident_b[:]).then_inc(s_mt_ps, 1)

            def column_scores(b, t, c, first):
                if not first:
                    pe.wait_ge(s_exp, (b * T + t) * NU + c)
                for hh in range(U):
                    h = c * U + hh
                    qs = q_stack[:, h, ds(t * P, P)]
                    own = ps[:, 3, hh * P:(hh + 1) * P]
                    pe.matmul(own, k_stack[:, h, ds(t * P + WIN, P)], qs, start=hh == 0, stop=False, skip_group_check=True)
                    pe.matmul(own, pick_w[:, h, 0:P], rows_w[:, ds(t * P, P)], start=False, stop=False, skip_group_check=True)
                    cs = ps[0:NCS, 4, hh * P:(hh + 1) * P]
                    pe.matmul(cs, cs_stack[:, h, :], qs, start=hh == 0, stop=False, skip_group_check=True)
                    pe.matmul(cs, pick_cs[:, ds(t, 1), h, :].rearrange("p a n -> p (a n)"), rows_cs[:, ds(t * P, P)], start=False, stop=True, skip_group_check=True)
                    before = ps[0:WIN, 5, hh * WIN:(hh + 1) * WIN]
                    pe.matmul(before, k_stack[:, h, ds(t * P, WIN)], q_stack[:, h, ds(t * P, WIN)], start=hh == 0, stop=False, skip_group_check=True)
                    pe.matmul(before, pick_w[:, h, P:KW], rows_w[:, ds(t * P, WIN)], start=False, stop=True, skip_group_check=True)
                pe.matmul(ps[:, 3, :].rearrange("p (h k) -> p h k", h=U), ident_b[:], own_mask[:].unsqueeze(1).broadcast_to([P, U, P]),
                          start=False, stop=True, skip_group_check=True).then_inc(s_b, 1)

            def with_values(b, t, c, first):
                n = b * T + t
                done(pe, s_exp, n * NU + c)
                if c == 0:
                    done(pe, s_tb, n)
                    if not first:
                        pe.wait_ge(s_wtd, n * 2)
                s = c % 2
                for hh in range(U):
                    h = c * U + hh
                    o = ps[:, 6 + h // 8, (h % 8) * OC:(h % 8 + 1) * OC]
                    pe.matmul(o[:, 0:VC], p_own[:, s, hh * P:(hh + 1) * P], values[:, ds(t, 1), h, :].rearrange("p a n -> p (a n)"),
                              start=h % 8 == 0, stop=False, skip_group_check=True)
                    pe.matmul(o[0:WIN, 0:VC], p_before[:, s, hh * WIN:(hh + 1) * WIN], tile_before[:, h, :],
                              start=False, stop=False, skip_group_check=True)
                    last = pe.matmul(o[:, VC:OC], p_cs[:, s, hh * P:(hh + 1) * P], cs_values[:, h, :], start=False, stop=True, skip_group_check=True)
                last.then_inc(s_pv, 1)

            def tile(b, t, first, ahead):
                n = b * T + t
                pe.wait_ge(s_mt, 2 * (n + 1))
                for c in range(NU):
                    if ahead:
                        row_scores(b, t + 1, c, False)
                    column_scores(b, t, c, first and c == 0)
                    if c:
                        with_values(b, t, c - 1, first)
                if ahead:
                    maxima(b, t + 1)
                with_values(b, t, NU - 1, first)

            def attention(b):
                pe.wait_ge(s_stack, (b + 1) * PAIRS * NSLOT * 2 * 16)
                pe.wait_ge(s_cs_in, (b + 1) * NSLOT * 16)
                pe.wait_ge(s_vb, (b + 1) * 16)
                done(pe, s_smask, b * 3 + 2)
                done(pe, s_csv, b * 2 + 1)
                done(pe, s_cks, b * 4)
                for c in range(NU):
                    row_scores(b, 0, c, c == 0, tile_0=True)
                maxima(b, 0)
                tile(b, 0, True, True)
                with pe.Fori(1, T - 1) as t:
                    tile(b, t, False, True)
                tile(b, T - 1, False, False)

            def output(b, i, first):
                for u in range(2):
                    n = b * T + i * 2 + u
                    done(pe, s_at, n)
                    if not first:
                        pe.wait_ge(s_atT, n - 1)
                    for c in range(DC):
                        last = pe.transpose(ps[:, 4 * u, c * P:(c + 1) * P], attn_t[:, u, c * P:(c + 1) * P], ident_f[:])
                    last.then_inc(s_at_ps, 1)
                for u in range(2):
                    n = b * T + i * 2 + u
                    done(pe, s_atT, n)
                    if not first:
                        pe.wait_ge(s_x1, n - 1)
                    for c in range(DC):
                        last = pe.matmul(ps[:, 4 * u + 1, 0:D], attnT[:, u, c, :], w_out[:, c, :], start=c == 0, stop=c == DC - 1)
                    last.then_inc(s_wo, 1)
                for u in range(2):
                    n = b * T + i * 2 + u
                    done(pe, s_x2n, n)
                    if not first:
                        pe.wait_ge(s_x2t, n - 1)
                    for c in range(DC):
                        last = pe.transpose(ps[:, 4 * u + 2, c * P:(c + 1) * P], x2n[:, u, c * P:(c + 1) * P], ident_f[:])
                    last.then_inc(s_x2t_ps, 1)
                for u in range(2):
                    n = b * T + i * 2 + u
                    done(pe, s_x2t, n)
                    if not first:
                        pe.wait_ge(s_ffs, n - 1)
                    for c in range(DC):
                        last = pe.matmul(ps[:, 4 * u + 3, 0:D], x2nT[:, u, c, :], w_ffn[:, c, :], start=c == 0, stop=c == DC - 1)
                    last.then_inc(s_ffn, 1)

            with pe.Fori(0, B) as b:
                front(b, 0, True)
                with pe.Fori(1, PAIRS) as i:
                    front(b, i, False)
                    back(b, i - 1, True)
                back(b, PAIRS - 1, False)
                selection(b)
                attention(b)
                pe.wait_ge(s_wtd, (b + 1) * T * 2)
                output(b, 0, True)
                with pe.Fori(1, PAIRS) as i:
                    output(b, i, False)

        @block.scalar
        def _(act):
            def copy(o, i):
                return act.activation(o, i, ACT.Copy)

            def front(b, i, first):
                for u in range(2):
                    n = b * T + i * 2 + u
                    done(act, s_xt_ps, n)
                    copy(xnT[:, u], ps[:, 4 * u, 0:D].rearrange("p (c q) -> p c q", c=DC)).then_inc(s_xt, 1)
                for u in range(2):
                    t = i * 2 + u
                    n = b * T + t
                    done(act, s_proj, n)
                    if not first:
                        act.wait_ge(s_rc, 2 * (n - 1))
                    copy(qk[:, u], ps[:, 4 * u + 1, :]).then_inc(s_qk, 1)
                    copy(values[:, ds(t, 1), :, 0:HD].rearrange("p a h d -> p (a h) d"),
                         ps[:, 4 * u + 2, 0:D].rearrange("p (h d) -> p h d", h=H))
                    copy(gate[:, ds(t, 1), :].rearrange("p a c -> p (a c)"), ps[:, 4 * u + 2, D:D + 3]).then_inc(s_vg, 1)

            def back(b, i, first):
                for u in range(2):
                    t = i * 2 + u
                    n = b * T + t
                    done(act, s_qkt, n)
                    copy(parts[:, 0, :, ds(t * P, P)], ps[:, 4 * u + 3, :].rearrange("p (c q) -> p c q", c=4)).then_inc(s_hi, 1)
                for u in range(2):
                    t = i * 2 + u
                    n = b * T + t
                    done(act, s_rest1, n)
                    copy(parts[:, 1, :, ds(t * P, P)], rest[:, u]).then_inc(s_mid, 1)

            def probabilities(b, t, c, first):
                k = (b * T + t) * NU + c
                done(act, s_b, k)
                if not first:
                    act.wait_ge(s_pv, k - 1)
                s = c % 2
                act.activation(p_own[:, s, :], ps[:, 3, :], ACT.Exp)
                act.activation(p_cs[:, s, :], ps[0:NCS, 4, :], ACT.Exp)
                act.activation(p_before[:, s, :], ps[0:WIN, 5, 0:U * WIN], ACT.Exp).then_inc(s_exp, 1)

            def output(b, i, first):
                for u in range(2):
                    t = i * 2 + u
                    n = b * T + t
                    if not first:
                        act.wait_ge(s_at_ps, n - 1)
                    copy(attn_t[:, u], attn[:, ds(t, 1), :].rearrange("p a d -> p (a d)")).then_inc(s_at, 1)
                for u in range(2):
                    n = b * T + i * 2 + u
                    done(act, s_at_ps, n)
                    if not first:
                        act.wait_ge(s_wo, n - 1)
                    copy(attnT[:, u], ps[:, 4 * u, 0:D].rearrange("p (c q) -> p c q", c=DC)).then_inc(s_atT, 1)
                for u in range(2):
                    n = b * T + i * 2 + u
                    done(act, s_x2t_ps, n)
                    if not first:
                        act.wait_ge(s_ffn, n - 1)
                    copy(x2nT[:, u], ps[:, 4 * u + 2, 0:D].rearrange("p (c q) -> p c q", c=DC)).then_inc(s_x2t, 1)

            with act.Fori(0, B) as b:
                front(b, 0, True)
                with act.Fori(1, PAIRS) as i:
                    front(b, i, False)
                    back(b, i - 1, True)
                back(b, PAIRS - 1, False)
                done(act, s_gsub, b * 3 + 2)
                act.activation(gate[:], gate[:], ACT.Exp).then_inc(s_gexp, 1)
                done(act, s_sel_ps, b)
                copy(cs_values[0:NB, :, 0:HD], ps[0:NB, 5, 0:D].rearrange("p (h d) -> p h d", h=H)).then_inc(s_csv, 1)
                copy(cs_values[NB:NCS, :, VC:VC + HD], ps[NB:NCS, 5, 0:D].rearrange("p (h d) -> p h d", h=H)).then_inc(s_csv, 1)
                for c in range(NU):
                    probabilities(b, 0, c, c < 2)
                with act.Fori(1, T) as t:
                    for c in range(NU):
                        probabilities(b, t, c, False)
                done(act, s_attn, (b * T + T - 1) * 2 + 1)
                output(b, 0, True)
                with act.Fori(1, PAIRS) as i:
                    output(b, i, False)

        @block.vector
        def _(dve):
            dve.memset(ones[:], 1.0)
            dve.memset(minus_half[:], -0.5)
            dve.memset(values[:], 1.0)
            dve.memset(values_before, 0.0)
            dve.memset(k_stack[:, :, 0:WIN], 0.0)
            dve.memset(cs_values[:], 0.0).then_inc(s_setup, 1)
            dve.wait_ge(s_setup, 1)
            dve.memset(cs_values[0:NB, :, HD:VC], 1.0)
            dve.memset(cs_values[NB:NCS, :, 2 * VC - 1:2 * VC], 1.0).then_inc(s_w, 1)
            dve.wait_ge(s_const, 16 * len(loads))
            dve.tensor_scalar(w_in[:, :, 0:D], w_in[:, :, 0:D], 1.0 / float(np.sqrt(HD)), None, ALU.mult)
            dve.tensor_scalar(scb_all[:], scb_all[:], 1.0 / 127.0, None, ALU.mult)
            dve.tensor_scalar(comp_k[:], block_of[:, 0, 0:8], wk_col[:, 0:1], None, ALU.mult)
            dve.tensor_scalar(gather[:], block_of[:], wv_col[:, 0:1], None, ALU.mult)
            dve.tensor_scalar(wk_rows, ones[64:80, 0:NB], wk_col[64:80, 0:1], None, ALU.mult)
            dve.memset(wv_rows, 0.0).then_inc(s_setup, 1)
            dve.wait_ge(s_setup, 2)
            dve.tensor_scalar(wv_rows[:, 0:NB], ones[64:80, 0:NB], wv_col[64:80, 0:1], None, ALU.mult).then_inc(s_w, 1)
            dve.wait_ge(s_setup_pe, 1)
            dve.tensor_copy(w_ffn[:], ps[:, 0:DC, 0:D]).then_inc(s_w, 1)

            def layernorm(n, u, src, dst, bn, mv, ve):
                dve.bn_stats(bn6[:, u], src).then_inc(bn, 1)
                done(dve, bn, n)
                settled(dve)
                dve.bn_aggr(mean_var[:, u], bn6[:, u]).then_inc(mv, 1)
                done(dve, mv, n)
                dve.tensor_scalar(var_eps[:, u:u + 1], mean_var[:, u, 1:2], EPS, None, ALU.add).then_inc(ve, 1)

            def front(b, i, first):
                for u in range(2):
                    t = i * 2 + u
                    layernorm(b * T + t, u, x_in[:, ds(t, 1), :].rearrange("p a d -> p (a d)"), None, s_bn, s_mv, s_ve)
                for u in range(2):
                    t = i * 2 + u
                    n = b * T + t
                    done(dve, s_rstd, n)
                    if not first:
                        dve.wait_ge(s_xt_ps, n - 1)
                    dve.tensor_scalar(xn[:, u], x_in[:, ds(t, 1), :].rearrange("p a d -> p (a d)"), mean_var[:, u, 0:1], rstd[:, u:u + 1],
                                      ALU.subtract, ALU.mult).then_inc(s_xn, 1)
                done(dve, s_xn, b * T + i * 2 + 1)
                settled(dve)

            def back(b, i, first):
                for u in range(2):
                    t = i * 2 + u
                    n = b * T + t
                    done(dve, s_hi, n)
                    dve.tensor_reduce(q_sums[:, ds(t, 1), :].rearrange("p a g -> p (a g)"), ps[:, 4 * u + 3, 0:D].rearrange("p (g s) -> p g s", g=2), AX.X, ALU.add)
                    dve.tensor_tensor(rest[:, u], ps[:, 4 * u + 3, :].rearrange("p (c q) -> p c q", c=4), parts[:, 0, :, ds(t * P, P)],
                                      ALU.subtract).then_inc(s_rest1, 1)
                for u in range(2):
                    t = i * 2 + u
                    n = b * T + t
                    done(dve, s_mid, n)
                    dve.tensor_tensor(parts[:, 2, :, ds(t * P, P)], rest[:, u], parts[:, 1, :, ds(t * P, P)], ALU.subtract).then_inc(s_lo, 1)
                done(dve, s_lo, b * T + i * 2 + 1)
                settled(dve)

            def selection(b):
                done(dve, s_ck_ps, b)
                dve.tensor_copy(ck[:, :, 0:NB], ps[:, 0, 0:2 * NB].rearrange("p (g n) -> p g n", g=2)).then_inc(s_ck, 1)
                dve.tensor_reduce(q_sum[:], q_sums[:].rearrange("p t g -> p g t"), AX.X, ALU.add).then_inc(s_qsum, 1)
                done(dve, s_imp_ps, b)
                dve.tensor_copy(imp[:], ps[0:1, 1, 0:NB]).then_inc(s_top, 1)
                done(dve, s_top, b * 4)
                settled(dve)
                dve.max(imp_max[:], imp[:]).then_inc(s_top, 1)
                done(dve, s_top, b * 4 + 1)
                settled(dve)
                dve.max_index(imp_idx[:], imp_max[:], imp[:]).then_inc(s_top, 1)
                done(dve, s_top, b * 4 + 2)
                dve.tensor_scalar(sel_start[:], imp_idx[:], 16.0, None, ALU.mult).then_inc(s_top, 1)
                done(dve, s_start_ps, b)
                dve.tensor_copy(start_all[:], ps[:, 2, 0:3]).then_inc(s_start, 1)
                done(dve, s_start, b)
                for j in range(2):
                    cols = slice(NB + 8 * j, NB + 8 * j + 8)
                    dve.tensor_scalar(gather[:, :, cols], since[:], start_all[:, j:j + 1], None, ALU.is_equal).then_inc(s_onehot, 1)
                for j in range(2):
                    cols = slice(NB + 8 * j, NB + 8 * j + 8)
                    dve.tensor_scalar(cs_mask[:, :, cols], since[:], start_all[:, j:j + 1], MASKED, ALU.is_lt, ALU.mult).then_inc(s_smask, 1)
                dve.tensor_scalar(rows_cs[96:112, :], since_cols, start_all[96:112, 2:3], MASKED, ALU.is_lt, ALU.mult).then_inc(s_smask, 1)
                dve.tensor_tensor(gate[:], gate[:], bg_all[:].unsqueeze(1).broadcast_to([P, T, 3]), ALU.add).then_inc(s_gsub, 1)
                done(dve, s_gsub, b * 3)
                dve.tensor_reduce(gate_max[:], gate[:], AX.X, ALU.max).then_inc(s_gsub, 1)
                done(dve, s_gsub, b * 3 + 1)
                dve.tensor_tensor(gate[:], gate[:], gate_max[:].unsqueeze(2).broadcast_to([P, T, 3]), ALU.subtract).then_inc(s_gsub, 1)
                done(dve, s_sel_ps, b)
                dve.tensor_copy(ck[:, :, NB:NCS], ps[:, 4, 0:2 * NSEL].rearrange("p (g n) -> p g n", g=2)).then_inc(s_cks, 1)
                done(dve, s_cks, b * 4)
                dve.tensor_copy(ck_parts[:, 0], ck[:]).then_inc(s_cks, 1)
                done(dve, s_cks, b * 4 + 1)
                dve.tensor_tensor(ck_rest[:], ck[:], ck_parts[:, 0], ALU.subtract).then_inc(s_cks, 1)
                done(dve, s_cks, b * 4 + 2)
                dve.tensor_copy(ck_parts[:, 1], ck_rest[:]).then_inc(s_cks, 1)
                done(dve, s_cks, b * 4 + 3)
                dve.tensor_tensor(ck_parts[:, 2], ck_rest[:], ck_parts[:, 1], ALU.subtract).then_inc(s_ckp, 1)
                done(dve, s_gexp, b)
                dve.tensor_reduce(gate_sum[:], gate[:], AX.X, ALU.add).then_inc(s_gate, 1)
                done(dve, s_gate, b * 4)
                dve.reciprocal(gate_inv[:], gate_sum[:]).then_inc(s_gate, 1)
                done(dve, s_gate, b * 4 + 1)
                for to, of, n in ((0, 2, 1), (1, 0, 2)):
                    dve.tensor_tensor(branch_gate[:, :, to:to + n], gate[:, :, of:of + n], gate_inv[:].unsqueeze(2).broadcast_to([P, T, n]),
                                      ALU.mult).then_inc(s_gate, 1)
                done(dve, s_gate, b * 4 + 3)

            def reduce_unit(b, t, c):
                done(dve, s_a, (b * T + t) * NU + c)
                hs = slice(c * U, c * U + U)
                dve.tensor_reduce(neg_max[:, 0, hs].rearrange("p (j h) -> p j h", j=2),
                                  ps[:, 0:2, 0:2 * KW].rearrange("p j (h k) -> p j h k", h=2), AX.X, ALU.max, negate=True)
                cs = ps[:, 2, 0:U * NCS].rearrange("p (h k) -> p h k", h=U)
                dve.tensor_reduce(neg_max[:, 1, hs], cs[:, :, 0:NB], AX.X, ALU.max, negate=True)
                dve.tensor_reduce(neg_max[:, 2, hs], cs[:, :, NB:NCS], AX.X, ALU.max, negate=True).then_inc(s_max, 1)

            def split_maxima(b, t):
                n = b * T + t
                done(dve, s_max, n * NU + NU - 1)
                dve.tensor_scalar(neg_lim[:], neg_max[:], LEAST, None, ALU.min).then_inc(s_neg, 1)
                done(dve, s_neg, n * 5)
                dve.tensor_copy(neg_parts[:, :, 0], neg_lim[:]).then_inc(s_neg, 1)
                done(dve, s_neg, n * 5 + 1)
                dve.tensor_tensor(neg_rest[:], neg_lim[:], neg_parts[:, :, 0], ALU.subtract).then_inc(s_neg, 1)
                done(dve, s_neg, n * 5 + 2)
                dve.tensor_copy(neg_parts[:, :, 1], neg_rest[:]).then_inc(s_neg, 1)
                done(dve, s_neg, n * 5 + 3)
                dve.tensor_tensor(neg_parts[:, :, 2], neg_rest[:], neg_parts[:, :, 1], ALU.subtract).then_inc(s_neg, 1)

            def copy_maxima(b, t, fence):
                done(dve, s_mt_ps, b * T + t)
                dve.tensor_copy(rows_w[0:48, ds(t * P, P)], ps[0:48, 2, 0:64].bitcast(BF16)).then_inc(s_mt, 1)
                dve.tensor_copy(rows_cs[0:96, ds(t * P, P)], ps[0:96, 2, 64:128].bitcast(BF16)).then_inc(s_mt, 1)
                done(dve, s_mt, (b * T + t) * 2 + 1)
                settled(dve)

            def combine(b, t):
                n = b * T + t
                done(dve, s_pv, n * NU + NU - 1)
                for j in range(2):
                    o = ps[:, 6 + j, 0:8 * OC].rearrange("p (h r d) -> p h r d", h=8, r=3)
                    dve.tensor_scalar(den[:, 8 * j:8 * j + 8, :].unsqueeze(3), o[:, :, :, HD:VC], 1e-30, None, ALU.max).then_inc(s_den, 1)
                done(dve, s_den, n * 4 + 1)
                dve.reciprocal(den_inv[:], den[:]).then_inc(s_den, 1)
                done(dve, s_den, n * 4 + 2)
                dve.tensor_tensor(weight[:], den_inv[:], branch_gate[:, ds(t, 1), :].broadcast_to([P, H, 3]), ALU.mult).then_inc(s_den, 1)
                done(dve, s_den, n * 4 + 3)
                for j in range(2):
                    o = ps[:, 6 + j, 0:8 * OC].rearrange("p (h r d) -> p h r d", h=8, r=3)
                    dve.tensor_tensor(weighted[:], o[:, :, :, 0:HD], weight[:, 8 * j:8 * j + 8, :].unsqueeze(3).broadcast_to([P, 8, 3, HD]),
                                      ALU.mult).then_inc(s_wtd, 1)
                    done(dve, s_wtd, n * 2 + j)
                    dve.tensor_reduce(attn[:, ds(t, 1), P * j:P * j + P].rearrange("p a (h d) -> p (a h) d", h=8),
                                      weighted[:].rearrange("p h r d -> p h d r"), AX.X, ALU.add).then_inc(s_attn, 1)
                    done(dve, s_attn, n * 2 + j)
                    settled(dve)

            def output(b, i, first):
                for u in range(2):
                    n = b * T + i * 2 + u
                    done(dve, s_wo, n)
                    done(dve, s_xrb, n)
                    dve.tensor_tensor(x1[:, u], ps[:, 4 * u + 1, 0:D], x_res[:, u], ALU.add).then_inc(s_x1, 1)
                    done(dve, s_x1, n)
                    layernorm(n, u, x1[:, u], None, s_bn2, s_mv2, s_ve2)
                for u in range(2):
                    n = b * T + i * 2 + u
                    done(dve, s_rstd2, n)
                    dve.tensor_scalar(x2n[:, u], x1[:, u], mean_var[:, u, 0:1], rstd[:, u:u + 1], ALU.subtract, ALU.mult).then_inc(s_x2n, 1)
                for u in range(2):
                    n = b * T + i * 2 + u
                    done(dve, s_ffn, n)
                    dve.tensor_tensor(ffn[:, u], ps[:, 4 * u + 3, 0:D], scb_all[:], ALU.mult).then_inc(s_ffs, 1)
                    done(dve, s_ffs, n)
                    done(dve, s_x1b, n)
                    if not first:
                        dve.wait_ge(s_out[u], (b * PAIRS + i) * 16)
                    dve.tensor_tensor(y[:, u], ffn[:, u], x1b[:, u], ALU.add).then_inc(s_y, 1)
                done(dve, s_y, b * T + i * 2 + 1)
                settled(dve)

            with dve.Fori(0, B) as b:
                dve.wait_ge(s_x, (b + 1) * 16)
                front(b, 0, True)
                with dve.Fori(1, PAIRS) as i:
                    front(b, i, False)
                    back(b, i - 1, True)
                dve.sem_inc(s_xused, 1)
                back(b, PAIRS - 1, False)
                selection(b)
                for c in range(NU):
                    reduce_unit(b, 0, c)
                split_maxima(b, 0)
                copy_maxima(b, 0, None)
                with dve.Fori(0, T - 1) as t:
                    for c in range(NU):
                        reduce_unit(b, t + 1, c)
                    split_maxima(b, t + 1)
                    copy_maxima(b, t + 1, None)
                    combine(b, t)
                combine(b, T - 1)
                output(b, 0, True)
                with dve.Fori(1, PAIRS) as i:
                    output(b, i, False)

        @block.gpsimd
        def _(pool):
            def swapped(ap):
                return ap.rearrange("p (f two) -> p f two", two=2)

            def front(b, i, first):
                for u in range(2):
                    n = b * T + i * 2 + u
                    done(pool, s_ve, n)
                    pool.tensor_tensor(rstd[:, u:u + 1], var_eps[:, u:u + 1], minus_half[:], ALU.pow).then_inc(s_rstd, 1)
                for u in range(2):
                    t = i * 2 + u
                    n = b * T + t
                    done(pool, s_qk, n)
                    heads = lambda a: a.rearrange("p (h d) -> p h d", d=HD)
                    c = cos[:, ds(t, 1), :].broadcast_to([P, 2 * H, HD])
                    if not first:
                        pool.wait_ge(s_qkt, n - 1)
                    pool.tensor_tensor(heads(roped[:, u]), heads(qk[:, u]), c, ALU.mult).then_inc(s_rc, 1)
                    for e in range(2):
                        s = sin[:, ds(t, 1), e::2].broadcast_to([P, 2 * H, HD // 2])
                        last = pool.tensor_tensor(heads(rope_s[:])[:, :, e::2], heads(qk[:, u])[:, :, 1 - e::2], s, ALU.mult)
                    last.then_inc(s_rc, 1)
                    done(pool, s_rc, 2 * n + 1)
                    pool.tensor_tensor(roped[:, u], roped[:, u], rope_s[:], ALU.add).then_inc(s_rope, 1)
                    done(pool, s_rope, n)
                    settled(pool)
                    pool.tensor_copy(k_tok[:, ds(t, 1), :].rearrange("p a d -> p (a d)"), roped[:, u, D:2 * D]).then_inc(s_ktok, 1)

            def output(b, i):
                for u in range(2):
                    n = b * T + i * 2 + u
                    pool.wait_ge(s_xr[u], (b * (PAIRS + 1) + i + 1) * 16)
                    pool.tensor_tensor(x_res[:, u], x_res[:, u], bo_all[:], ALU.add).then_inc(s_xrb, 1)
                for u in range(2):
                    n = b * T + i * 2 + u
                    done(pool, s_ve2, n)
                    pool.tensor_tensor(rstd[:, u:u + 1], var_eps[:, u:u + 1], minus_half[:], ALU.pow).then_inc(s_rstd2, 1)
                for u in range(2):
                    n = b * T + i * 2 + u
                    pool.tensor_tensor(x1b[:, u], x1[:, u], bias_all[:], ALU.add).then_inc(s_x1b, 1)

            pool.wait_ge(s_const, 16 * len(loads))
            pool.wait_ge(s_w, 1)
            with pool.Fori(0, B) as b:
                front(b, 0, True)
                with pool.Fori(1, PAIRS) as i:
                    front(b, i, False)
                pool.wait_ge(s_vb, (b + 1) * 16)
                pool.wait_ge(s_stack, (b + 1) * PAIRS * NSLOT * 2 * 16)
                settled(pool)
                pool.tensor_copy(tile_before, values_before[:, 0]).then_inc(s_tb, 1)
                with pool.Fori(1, T) as t:
                    pool.wait_ge(s_pv, (b * T + t) * NU)
                    settled(pool)
                    pool.tensor_copy(tile_before, values_before[:, ds(t, 1)].rearrange("p a h d -> p (a h) d")).then_inc(s_tb, 1)
                with pool.Fori(0, PAIRS) as i:
                    output(b, i)


INS = ["L0_attn_x", "L0_attn_Wq", "L0_attn_Wk", "L0_attn_Wv", "L0_attn_Wo", "L0_attn_bo", "L0_attn_wk_comp",
       "L0_attn_wv_comp", "L0_attn_pe", "L0_attn_Wg", "L0_attn_bg", "L0_ffn_CB", "L0_ffn_SCB", "L0_ffn_bias"]


def kernel(**inputs):
    import numpy as _np
    import concourse.bacc as _bacc
    from concourse import mybir as _mybir
    from concourse.bass_utils import run_bass_kernel_spmd as _run

    nc = _bacc.Bacc("TRN2", target_bir_lowering=False, num_devices=1)
    arrays, args = {}, []
    for name in INS:
        a = _np.ascontiguousarray(inputs[name])
        arrays[f"in_{name}"] = a
        args.append(nc.dram_tensor(f"in_{name}", a.shape, _mybir.dt.from_np(a.dtype), kind="ExternalInput").ap())
    consts = {}
    for group in shape_constants():
        for name, a in group.items():
            arrays[f"const_{name}"] = a
            consts[name] = nc.dram_tensor(f"const_{name}", a.shape, _mybir.dt.from_np(a.dtype), kind="ExternalInput").ap()
    out = nc.dram_tensor("out", (B, S, D), _mybir.dt.float32, kind="ExternalOutput").ap()
    build(nc, *args, consts, out)
    r = _run(nc, [arrays], core_ids=[0])
    return r.results[0]["out"]
```

```python
import numpy as np
import concourse.bass as bass
from concourse import mybir
from contextlib import ExitStack

F32 = mybir.dt.float32
BF16 = mybir.dt.bfloat16
F16 = mybir.dt.float16
U32 = mybir.dt.uint32
ALU = mybir.AluOpType
ACT = mybir.ActivationFunctionType
AX = mybir.AxisListType
ds = bass.ds

P = 128
B, S, D = 8, 1024, 256
H, HD = 16, 16
T = S // P
PAIRS = T // 2
DC = D // P
NB = S // 16
NSEL = 16
WIN = 64
NCS = NB + NSEL
KW = P + WIN
U = 4
NU = H // U
VC = HD + 1
V_COLS = (slice(0, VC), slice(VC, VC + HD), slice(VC + HD, VC + 2 * HD))
VPC = VC + 2 * HD
EARLY, LATE = slice(0, H - U), slice(H - U, H)
OC = 3 * VC
NP1 = 3 * D + 3
Q_PARTS = (0, 0, 0, 1, 1, 2)
K_PARTS = (0, 1, 2, 0, 1, 0)
NSLOT = len(Q_PARTS)
KR_ROWS = NSLOT * HD
MASKED = -1e30
LEAST = 1e29
EPS = 1e-5
P_BIAS = 11 * float(np.log(2.0))


def shape_constants():
    p = np.arange(P)
    t = np.arange(T)

    def bits(a):
        return (np.ascontiguousarray(a, np.float32).view(np.uint32) >> 16).astype(np.uint16)

    j = np.arange(KW) - WIN
    ok = (j[None, :] <= p[:, None]) & (j[None, :] > p[:, None] - WIN)
    ok = ok[:, None, :] & ((t[None, :2, None] * P + j[None, None, :]) >= 0)
    window_mask = np.where(ok, 0.0, MASKED)
    s = t[None, :, None] * P + p[:, None, None]
    n = np.arange(NB)
    cs_mask = np.zeros((P, T, NCS))
    cs_mask[:, :, :NB] = np.where((n[None, None, :] + 1) * 16 <= s, 0.0, MASKED)
    own_mask = np.where((p[:, None] <= p[None, :]) & (p[:, None] > p[None, :] - WIN), 0.0, MASKED)
    pick_w = np.zeros((P, H, KW))
    for part in range(3):
        for h in range(H):
            pick_w[part * H + h, h, :] = 1.0
    for k in range(WIN):
        pick_w[WIN + k, :, P + k] = 1.0
    rows_w = np.zeros((P, S))
    q = np.arange(S)
    kl = np.arange(WIN)
    rows_w[WIN:] = np.where((kl[:, None] > (q % P)[None, :]) & (q[None, :] >= P), 0.0, MASKED)
    pick_cs = np.zeros((P, H, NCS))
    for part in range(3):
        for h in range(H):
            pick_cs[part * H + h, h, :NB] = 1.0
            pick_cs[48 + part * H + h, h, NB:] = 1.0
    cs_mask_cols = np.zeros((P, S))
    cs_mask_cols[:NB] = np.where((n[:, None] + 1) * 16 <= q[None, :], 0.0, MASKED)
    b16 = {
        "window_mask": window_mask, "cs_mask": cs_mask, "own_mask": own_mask, "pick_w": pick_w,
        "rows_w": rows_w, "pick_cs": pick_cs, "cs_mask_cols": cs_mask_cols, "ident_b": np.eye(P),
    }
    half = HD // 2
    inv = (1.0 / 10000.0 ** (np.arange(half, dtype=np.float32) * np.float32(2.0) / np.float32(HD))).astype(np.float32)
    ang = np.arange(S, dtype=np.float32)[:, None] * inv[None, :]
    cos = np.repeat(np.cos(ang), 2, axis=1)
    sin = np.stack([-np.sin(ang), np.sin(ang)], -1).reshape(S, HD)
    by_tile = lambda a: a.reshape(T, P, HD).transpose(1, 0, 2)
    r = np.arange(8)
    since = (t[None, :, None] * P + p[:, None, None]) - r[None, None, :]
    since_cols = q[None, :] - (np.arange(NSEL) % 8)[:, None]
    block_of = np.zeros((P, T, NCS))
    for pp in range(P):
        for tt in range(T):
            block_of[pp, tt, 8 * tt + pp // 16] = 1.0
    sel_rows = np.zeros((1, 2, P))
    sel_rows[0, 0, NB:NB + 8] = 1.0
    sel_rows[0, 1, NB + 8:NCS] = 1.0
    f32 = {
        "ident_f": np.eye(P), "cos": by_tile(cos), "sin": by_tile(sin), "since": since,
        "since_cols": since_cols, "block_of": block_of, "sel_rows": sel_rows,
    }
    return (
        {k: np.ascontiguousarray(bits(v).reshape(P, -1)) for k, v in b16.items()},
        {k: np.ascontiguousarray(v.astype(np.float32).reshape(v.shape[0], -1)) for k, v in f32.items()},
    )


def build(nc, x, Wq, Wk, Wv, Wo, bo, wk_comp, wv_comp, pe_, Wg, bg, CB, SCB, bias, consts, out):
    ctx = ExitStack()
    with ctx:
        def sb(name, shape, dt=F32):
            return ctx.enter_context(nc.sbuf_tensor(name, shape, dt))

        def sem(name):
            return ctx.enter_context(nc.semaphore(name))

        ident_f = sb("ident_f", [P, P])
        both = sb("both", [P, S])
        since_cols = both[NB:NCS, :]
        pe_sb = both[0:16, 0:D]
        wk_rows = both[0:16, D:D + NB]
        wv_rows = both[0:16, D + NB:D + NB + NCS]
        cos = sb("cos", [P, T, HD])
        sin = sb("sin", [P, T, HD])
        since = sb("since", [P, T, 8])
        sel_rows = both[0:1, D + NB + NCS:D + NB + NCS + 2 * P].rearrange("p (j n) -> p j n", j=2)
        ident_b = sb("ident_b", [P, P], BF16)
        window_mask = sb("window_mask", [P, 2, KW], BF16)
        cs_mask = sb("cs_mask", [P, T, NCS], BF16)
        own_mask = sb("own_mask", [P, P], BF16)
        pick_w = sb("pick_w", [P, H, KW], BF16)
        rows_w = sb("rows_w", [P, S], BF16)
        pick_cs = sb("pick_cs", [P, H, NCS], BF16)
        rows_cs = sb("rows_cs", [96, S], BF16)
        cs_mask_cols = sb("cs_mask_cols", [P, S], BF16)
        w_in = sb("w_in", [P, DC, NP1])
        w_out = sb("w_out", [P, DC, D])
        w_ffn = sb("w_ffn", [P, DC, D])
        ones = sb("ones", [P, P])
        bo_all = sb("bo_all", [P, D])
        bias_all = sb("bias_all", [P, D])
        scb_all = sb("scb_all", [P, D])
        bg_all = sb("bg_all", [P, 3])
        wk_col = sb("wk_col", [P, 1])
        wv_col = sb("wv_col", [P, 1])
        wk_all = sb("wk_all", [P, NB // 4])
        pe_key = sb("pe_key", [P, 2])
        weighted_k = sb("weighted_k", [P, D])
        gather = sb("gather", [P, T, NCS])
        minus_half = sb("minus_half", [P, 1])
        p_bias = sb("p_bias", [P, 1])
        x_in = sb("x_in", [P, T, D])
        bn6 = sb("bn6", [P, 2, 6])
        mean_var = sb("mean_var", [P, 2, 2])
        var_eps = sb("var_eps", [P, 2])
        rstd = sb("rstd", [P, 2])
        xn = sb("xn", [P, 2, D])
        xnT = sb("xnT", [P, 2, DC, P])
        qk = sb("qk", [P, 2, 2 * D])
        rope_s = sb("rope_s", [P, 2, 2 * D])
        roped = sb("roped", [P, 2, 2 * D])
        rest = sb("rest", [P, 2, 4, P])
        shared = sb("shared", [P, 6144])
        parts = shared[:, 0:3 * 4 * S // 2].bitcast(BF16).rearrange("p (a c s) -> p a c s", a=3, c=4)
        taken = [0]

        def part_of_shared(rows, *shape):
            n = int(np.prod(shape))
            a = shared[0:rows, taken[0]:taken[0] + n]
            taken[0] += n
            names = "abc"[:len(shape)]
            return a.rearrange(f"p ({' '.join(names)}) -> p {' '.join(names)}", **dict(zip(names, shape)))

        k_tok = sb("k_tok", [P, T, D])
        attn = k_tok
        q_sums = sb("q_sums", [P, T, 2])
        values = sb("values", [P, T, D])
        v_rest = sb("v_rest", [P, T, D])
        v_parts = sb("v_parts", [P, T, H, VPC], BF16)
        gate = sb("gate", [P, T, 3])
        q_stack = sb("q_stack", [KR_ROWS, H, S], BF16)
        k_stack = sb("k_stack", [KR_ROWS, H, WIN + S], BF16)
        cs_stack = sb("cs_stack", [KR_ROWS, H, NCS], BF16)
        ck = sb("ck", [P, 2, NCS])
        ck_rest = sb("ck_rest", [P, 2, NCS])
        ck_parts = sb("ck_parts", [P, 3, 2, NCS], BF16)
        q_sum = sb("q_sum", [P, 2])
        imp = sb("imp", [1, NB])
        imp_max = sb("imp_max", [1, 8])
        imp_idx = sb("imp_idx", [1, 8], U32)
        sel_start = sb("sel_start", [1, 8])
        start_all = sb("start_all", [P, 3])
        cs_parts = sb("cs_parts", [NCS, H, 3, 2 * VC], BF16)
        cs_rest = weighted_k[0:NCS].rearrange("p (h d) -> p h d", h=H)
        branch_gate = sb("branch_gate", [P, T, 3])
        gate_max = sb("gate_max", [P, T])
        gate_sum = sb("gate_sum", [P, T])
        gate_inv = sb("gate_inv", [P, T])
        neg_max = sb("neg_max", [P, 3, H])
        neg_lim = sb("neg_lim", [P, 3, H])
        neg_rest = sb("neg_rest", [P, 3, H])
        neg_parts = sb("neg_parts", [P, 3, 3, H], BF16)
        block_of = shared[:, 6144 - T * NCS:].rearrange("p (t n) -> p t n", t=T)
        p_own = part_of_shared(P, 2, U * P)
        p_cs = part_of_shared(NCS, 2, U * P)
        p_before = part_of_shared(WIN, 2, U * WIN)
        weighted = part_of_shared(P, 8, 3, HD)
        halves = lambda a: a.bitcast(F16).rearrange("p (s a k) -> p s a k", s=2, a=2)
        own_parts = halves(qk[:].rearrange("p u n -> p (u n)"))
        csp_parts = halves(roped[0:NCS].rearrange("p u n -> p (u n)"))
        before_parts = halves(rope_s[0:WIN, 0])
        rest_b = rest[:].rearrange("p u c q -> p (u c q)").bitcast(BF16)
        v_tile = rest_b[:, 0:H * VPC].rearrange("p (h v) -> p h v", h=H)
        v_prev = rest_b[0:WIN, H * VPC:2 * H * VPC].rearrange("p (h v) -> p h v", h=H)
        den = sb("den", [P, H, 3])
        den_inv = sb("den_inv", [P, H, 3])
        weight = sb("weight", [P, H, 3])
        taken[0] = 0
        x_res = sb("x_res", [P, 2, D])
        attn_t = part_of_shared(P, 2, D)
        attnT = part_of_shared(P, 2, DC, P)
        x1 = part_of_shared(P, 2, D)
        x1b = part_of_shared(P, 2, D)
        x2n = part_of_shared(P, 2, D)
        x2nT = part_of_shared(P, 2, DC, P)
        ffn = part_of_shared(P, 2, D)
        y = part_of_shared(P, 2, D)

        ps = ctx.enter_context(nc.psum_tensor("ps", [P, 8, 512], F32))
        part_dram = nc.dram_tensor("part_dram", [3, 2, H, HD, S], BF16).ap()
        cs_dram = nc.dram_tensor("cs_dram", [3, H, HD, NCS], BF16).ap()

        s_const = sem("constants_in")
        s_settled = sem("waits_settled")
        s_setup = sem("setup_vector")
        s_setup_pe = sem("setup_transposed")
        s_w = sem("setup_done")
        s_x = sem("x_in_loaded")
        s_xused = sem("x_in_used")
        s_bn = sem("bn_stats_done")
        s_mv = sem("mean_var_done")
        s_ve = sem("var_eps_done")
        s_rstd = sem("rstd_done")
        s_xn = sem("xn_done")
        s_xt_ps = sem("xn_transposed")
        s_xt = sem("xnT_done")
        s_proj = sem("projected")
        s_qk = sem("qk_copied")
        s_vg = sem("v_and_gate_copied")
        s_rc = sem("rope_cos_product")
        s_rs = sem("rope_sin_product")
        s_rope = sem("roped_done")
        s_ktok = sem("k_tok_done")
        s_qkt = sem("qk_transposed")
        s_hi = sem("high_part")
        s_rest1 = sem("rest_after_high")
        s_mid = sem("mid_part")
        s_lo = sem("low_part")
        s_part_out = sem("parts_in_dram")
        s_stack = sem("stacks_in")
        s_vhi = sem("values_high")
        s_vrest = sem("values_rest")
        s_vmid = sem("values_mid")
        s_vlo = sem("values_low")
        s_vt = [sem("tile_values_in"), sem("tile_values_in_last_unit")]
        s_wk = sem("keys_weighted")
        s_ckt = sem("keys_summed")
        s_ck = sem("ck_copied")
        s_qsum = sem("q_sum_done")
        s_imp_ps = sem("importance_summed")
        s_top = sem("top_steps")
        s_start_ps = sem("starts_spread")
        s_start = sem("start_all_done")
        s_onehot = sem("one_hot_done")
        s_smask = sem("selected_masks_done")
        s_selk_ps = sem("selected_keys_gathered")
        s_sel_ps = sem("values_gathered")
        s_cks = sem("ck_steps")
        s_ckp = sem("ck_parts_done")
        s_cvhi = sem("cs_values_high")
        s_cvrest = sem("cs_values_rest")
        s_cvmid = sem("cs_values_mid")
        s_cvlo = sem("cs_values_low")
        s_cs_out = sem("ck_parts_in_dram")
        s_cs_in = sem("cs_stack_in")
        s_gsub = sem("gate_shifted_steps")
        s_gexp = sem("gate_exp")
        s_gate = sem("gate_done_steps")
        s_a = sem("row_scores")
        s_max = sem("row_scores_reduced")
        s_fa = sem("first_window_scores")
        s_fmax = sem("first_window_scores_reduced")
        s_neg = sem("neg_steps")
        s_mt_ps = sem("maxima_transposed")
        s_mt = sem("maxima_copied")
        s_b = sem("column_scores")
        s_exp = sem("probabilities")
        s_pv = sem("probabilities_used")
        s_low = sem("low_probabilities")
        s_low_cs = sem("low_probabilities_cs")
        s_den = sem("denominator_steps")
        s_wtd = sem("weighted_half")
        s_attn = sem("attention_half")
        s_xr = [sem("x_res_loaded_0"), sem("x_res_loaded_1")]
        s_xrb = sem("x_res_plus_bo")
        s_at = sem("attn_t_copied")
        s_at_ps = sem("attn_transposed")
        s_atT = sem("attnT_copied")
        s_wo = sem("output_projected")
        s_x1 = sem("x1_done")
        s_x1b = sem("x1_plus_bias")
        s_bn2 = sem("bn_stats_2")
        s_mv2 = sem("mean_var_2")
        s_ve2 = sem("var_eps_2")
        s_rstd2 = sem("rstd_2")
        s_x2n = sem("x2n_done")
        s_x2t_ps = sem("x2n_transposed")
        s_x2t = sem("x2nT_copied")
        s_ffn = sem("ffn_projected")
        s_ffs = sem("ffn_scaled")
        s_y = sem("y_done")
        s_out = [sem("y_stored_0"), sem("y_stored_1")]

        loads = [
            (ident_f[:], consts["ident_f"]), (cos[:], consts["cos"]), (sin[:], consts["sin"]),
            (since[:], consts["since"]), (since_cols, consts["since_cols"]),
            (block_of, consts["block_of"]), (sel_rows, consts["sel_rows"]),
        ]
        for dst, name in ((ident_b, "ident_b"), (window_mask, "window_mask"), (cs_mask, "cs_mask"),
                          (own_mask, "own_mask"), (pick_w, "pick_w"), (rows_w, "rows_w"),
                          (pick_cs, "pick_cs"), (cs_mask_cols, "cs_mask_cols")):
            loads.append((dst[:], consts[name].bitcast(BF16)))

        def shaped(dst, src):
            if len(dst.shape) == 3:
                src = src.rearrange("p (a b) -> p a b", a=dst.shape[1])
            elif len(dst.shape) == 4:
                src = src.rearrange("p (a b c) -> p a b c", a=dst.shape[1], b=dst.shape[2])
            return src

        loads = [(dst, shaped(dst, src)) for dst, src in loads]
        for k, w in enumerate((Wq, Wk, Wv)):
            loads.append((w_in[:, :, k * D:(k + 1) * D], w.rearrange("(c p) n -> p c n", p=P)))
        loads.append((w_in[:, :, 3 * D:], Wg.rearrange("(c p) n -> p c n", p=P)))
        loads.append((w_out[:], Wo.rearrange("(c p) n -> p c n", p=P)))
        loads.append((x1[:], CB.rearrange("(c p) k -> p c k", p=P)))
        loads.append((pe_sb, pe_))
        for dst, v in ((bo_all, bo), (bias_all, bias), (scb_all, SCB), (bg_all, bg)):
            loads.append((dst[:], v.partition_broadcast(P)))
        loads.append((wk_all[:], wk_comp.partition_broadcast(P)))
        for dst, v in ((wk_col, wk_comp), (wv_col, wv_comp)):
            for g in range(8):
                loads.append((dst[16 * g:16 * g + 16, :], v.rearrange("(p a) -> p a", a=1)))

        def done(eng, s, n):
            eng.wait_ge(s, n + 1)

        def settled(eng):
            eng.sem_inc(s_settled, 1)

        def x_tiles(b):
            return x[ds(b, 1)].rearrange("a (t p) d -> p (a t) d", p=P)

        cs_places = ((slice(0, NB), 0), (slice(NB, NCS), VC))
        block = ctx.enter_context(nc.Block())

        @block.sync
        def _(sp):
            for dst, src in loads:
                sp.dma_start(dst, src).then_inc(s_const, 16)
            sp.dma_start(x_in[:], x_tiles(0)).then_inc(s_x, 16)
            with sp.Fori(0, B) as b:
                with sp.Fori(0, PAIRS) as i:
                    pair = b * PAIRS + i
                    done(sp, s_lo, pair * 2 + 1)
                    settled(sp)
                    for part in range(3):
                        sp.dma_start(
                            part_dram[part, :, :, :, ds(i * 2 * P, 2 * P)].rearrange("w (g h) d s -> (h d) (w g) s", g=2),
                            parts[:, part, :, ds(i * 2 * P, 2 * P)],
                        ).then_inc(s_part_out, 16)
                    sp.wait_ge(s_part_out, (pair + 1) * 48)
                    settled(sp)
                    for slot in range(NSLOT):
                        rows = slice(slot * HD, slot * HD + HD)
                        sp.dma_start(
                            q_stack[rows, :, ds(i * 2 * P, 2 * P)],
                            part_dram[Q_PARTS[slot], 0, :, :, ds(i * 2 * P, 2 * P)].rearrange("h d s -> d h s"),
                        ).then_inc(s_stack, 16)
                        sp.dma_start(
                            k_stack[rows, :, ds(i * 2 * P + WIN, 2 * P)],
                            part_dram[K_PARTS[slot], 1, :, :, ds(i * 2 * P, 2 * P)].rearrange("h d s -> d h s"),
                        ).then_inc(s_stack, 16)
                done(sp, s_ckp, b)
                for g in range(2):
                    sp.dma_start(cs_dram[:, 8 * g:8 * g + 8].rearrange("a h d n -> (h d) a n"),
                                 ck_parts[:, :, g, :]).then_inc(s_cs_out, 16)
                sp.wait_ge(s_cs_out, (b + 1) * 32)
                for slot in range(NSLOT):
                    sp.dma_start(cs_stack[slot * HD:slot * HD + HD], cs_dram[K_PARTS[slot]].rearrange("h d n -> d h n")).then_inc(s_cs_in, 16)
                done(sp, s_xused, b)
                settled(sp)
                sp.wait_ge(s_x, (b + 1) * 16)
                settled(sp)
                nxt = (b + 1) % B
                sp.dma_start(x_in[:], x_tiles(nxt)).then_inc(s_x, 16)
                for u in range(2):
                    sp.dma_start(x_res[:, u], x[ds(b, 1), u * P:(u + 1) * P].rearrange("a p d -> p (a d)")).then_inc(s_xr[u], 16)
                done(sp, s_vlo, b)
                for hs, loaded in ((EARLY, s_vt[0]), (LATE, s_vt[1])):
                    sp.dma_start(v_tile[:, hs], v_parts[:, 0, hs]).then_inc(loaded, 16)
                    sp.dma_start(v_prev[:, hs], v_parts[WIN:P, T - 1, hs]).then_inc(loaded, 16)
                with sp.Fori(1, T) as t:
                    for hs, loaded, left in ((EARLY, s_vt[0], 1), (LATE, s_vt[1], 0)):
                        sp.wait_ge(s_pv, (b * T + t) * NU - left)
                        settled(sp)
                        sp.wait_ge(loaded, (b * T + t) * 32)
                        settled(sp)
                        sp.dma_start(v_tile[:, hs], v_parts[:, ds(t, 1), hs].rearrange("p a h d -> p (a h) d")).then_inc(loaded, 16)
                        sp.dma_start(v_prev[:, hs], v_parts[WIN:P, ds(t - 1, 1), hs].rearrange("p a h d -> p (a h) d")).then_inc(loaded, 16)
                with sp.Fori(0, PAIRS) as i:
                    for u in range(2):
                        done(sp, s_x1, b * T + i * 2 + u)
                        settled(sp)
                        sp.wait_ge(s_xr[u], (b * (PAIRS + 1) + i + 1) * 16)
                        settled(sp)
                        nxt_tile = ((i + 1) % PAIRS) * 2 + u
                        sp.dma_start(x_res[:, u], x[ds(b, 1), ds(nxt_tile * P, P)].rearrange("a p d -> p (a d)")).then_inc(s_xr[u], 16)
                    for u in range(2):
                        done(sp, s_y, b * T + i * 2 + u)
                        settled(sp)
                        sp.dma_start(out[ds(b, 1), ds((i * 2 + u) * P, P)].rearrange("a p d -> p (a d)"), y[:, u]).then_inc(s_out[u], 16)
                for u in range(2):
                    sp.wait_ge(s_out[u], (b + 1) * PAIRS * 16)
                settled(sp)
            sp.wait_ge(s_x, (B + 1) * 16)
            for u in range(2):
                sp.wait_ge(s_out[u], B * PAIRS * 16)
                sp.wait_ge(s_xr[u], B * (PAIRS + 1) * 16)

        @block.tensor
        def _(pe):
            pe.wait_ge(s_const, 16 * len(loads))
            for kc in range(DC):
                for ncn in range(DC):
                    last = pe.transpose(ps[:, kc, ncn * P:(ncn + 1) * P], x1[:, ncn, kc * P:(kc + 1) * P], ident_f[:])
            last.then_inc(s_setup_pe, 1)
            pe.wait_ge(s_w, 2)
            for g in range(2):
                last = pe.matmul(ps[:, 2, g:g + 1], pe_sb[:, g * P:(g + 1) * P], wk_rows[:, 0:1], start=True, stop=True)
            last.then_inc(s_setup_pe, 1)
            pe.wait_ge(s_w, 4)

            def front(b, i, first):
                for u in range(2):
                    n = b * T + i * 2 + u
                    done(pe, s_xn, n)
                    if not first:
                        pe.wait_ge(s_xt, n - 1)
                    for c in range(DC):
                        last = pe.transpose(ps[:, 4 * u, c * P:(c + 1) * P], xn[:, u, c * P:(c + 1) * P], ident_f[:])
                    last.then_inc(s_xt_ps, 1)
                for u in range(2):
                    n = b * T + i * 2 + u
                    done(pe, s_xt, n)
                    if not first:
                        pe.wait_ge(s_vg, n - 1)
                    for c in range(DC):
                        pe.matmul(ps[:, 4 * u + 1, :], xnT[:, u, c, :], w_in[:, c, 0:2 * D], start=c == 0, stop=c == DC - 1)
                    for c in range(DC):
                        last = pe.matmul(ps[:, 4 * u + 2, 0:D + 3], xnT[:, u, c, :], w_in[:, c, 2 * D:], start=c == 0, stop=c == DC - 1)
                    last.then_inc(s_proj, 1)

            def back(b, i, first):
                for u in range(2):
                    n = b * T + i * 2 + u
                    done(pe, s_rope, n)
                    if not first:
                        pe.wait_ge(s_rest1, n - 1)
                    for c in range(4):
                        last = pe.transpose(ps[:, 4 * u + 3, c * P:(c + 1) * P], roped[:, u, c * P:(c + 1) * P], ident_f[:])
                    last.then_inc(s_qkt, 1)

            def selection(b):
                done(pe, s_ktok, b * T + T - 1)
                done(pe, s_rest1, b * T + T - 1)
                done(pe, s_vg, b * T + T - 1)
                done(pe, s_ck, b)
                done(pe, s_qsum, b)
                for g in range(2):
                    last = pe.matmul(ps[0:1, 1, 0:NB], q_sum[:, g:g + 1], ck[:, g, 0:NB], start=g == 0, stop=g == 1)
                last.then_inc(s_imp_ps, 1)
                done(pe, s_top, b * 4 + 3)
                pe.matmul(ps[:, 2, 0:2], ones[0:1, :], sel_start[0:1, 0:2], start=True, stop=True)
                for j in range(2):
                    last = pe.matmul(ps[:, 2, 2:3], sel_rows[0:1, j, :], sel_start[0:1, j:j + 1], start=j == 0, stop=j == 1)
                last.then_inc(s_start_ps, 1)
                done(pe, s_onehot, b * 2 + 1)
                for g in range(2):
                    for t in range(T):
                        last = pe.matmul(ps[:, 4, g * NSEL:(g + 1) * NSEL], k_tok[:, t, g * P:(g + 1) * P], gather[:, t, NB:NCS], start=t == 0, stop=t == T - 1)
                last.then_inc(s_selk_ps, 1)
                pe.wait_ge(s_stack, (b * PAIRS + 1) * NSLOT * 2 * 16)
                done(pe, s_start, b)
                first_window_scores(b)
                for t in range(T):
                    pe.matmul(ps[0:NCS, 5, 0:D], gather[:, t, :], values[:, t, :], start=t == 0, stop=False)
                pe.matmul(ps[0:NCS, 5, 0:D], wv_rows, pe_sb, start=False, stop=True).then_inc(s_sel_ps, 1)

            def first_window_scores(b):
                for c in range(NU):
                    if c > 1:
                        done(pe, s_fmax, b * NU + c - 2)
                    banks = 2 * (c % 2)
                    for hh in range(U):
                        h = c * U + hh
                        pe.matmul(ps[:, banks + hh // 2, (hh % 2) * KW:(hh % 2 + 1) * KW], q_stack[:, h, 0:P], k_stack[:, h, 0:KW],
                                  start=hh % 2 == 0, stop=False, skip_group_check=True)
                    for j in range(2):
                        last = pe.matmul(ps[:, banks + j, 0:2 * KW].rearrange("p (h k) -> p h k", h=2), ident_b[:],
                                         window_mask[:, 0:1, :].broadcast_to([P, 2, KW]), start=False, stop=True, skip_group_check=True)
                    last.then_inc(s_fa, 1)

            def first_cs_scores(b):
                done(pe, s_fmax, b * NU + NU - 1)
                for c in range(NU):
                    for hh in range(U):
                        h = c * U + hh
                        pe.matmul(ps[:, c, hh * NCS:(hh + 1) * NCS], q_stack[:, h, 0:P], cs_stack[:, h, :], start=hh == 0, stop=False, skip_group_check=True)
                    pe.matmul(ps[:, c, 0:U * NCS].rearrange("p (h k) -> p h k", h=U), ident_b[:],
                              cs_mask[:, 0:1, :].broadcast_to([P, U, NCS]), start=False, stop=True, skip_group_check=True).then_inc(s_a, 1)

            def row_scores(b, t, c):
                pe.wait_ge(s_max, (b * T + t) * NU + c)
                for hh in range(U):
                    h = c * U + hh
                    pe.matmul(ps[:, hh // 2, (hh % 2) * KW:(hh % 2 + 1) * KW], q_stack[:, h, ds(t * P, P)], k_stack[:, h, ds(t * P, KW)],
                              start=hh % 2 == 0, stop=False, skip_group_check=True)
                for j in range(2):
                    pe.matmul(ps[:, j, 0:2 * KW].rearrange("p (h k) -> p h k", h=2), ident_b[:],
                              window_mask[:, 1:2, :].broadcast_to([P, 2, KW]), start=False, stop=True, skip_group_check=True)
                if c == 0:
                    pe.wait_ge(s_mt, 2 * (b * T + t))
                for hh in range(U):
                    h = c * U + hh
                    pe.matmul(ps[:, 2, hh * NCS:(hh + 1) * NCS], q_stack[:, h, ds(t * P, P)], cs_stack[:, h, :], start=hh == 0, stop=False, skip_group_check=True)
                pe.matmul(ps[:, 2, 0:U * NCS].rearrange("p (h k) -> p h k", h=U), ident_b[:],
                          cs_mask[:, ds(t, 1), :].broadcast_to([P, U, NCS]), start=False, stop=True, skip_group_check=True).then_inc(s_a, 1)

            def maxima(b, t):
                done(pe, s_neg, (b * T + t) * 5 + 4)
                settled(pe)
                w = ps[0:48, 2, 0:64].bitcast(BF16)
                cs = ps[0:96, 2, 64:128].bitcast(BF16)
                pe.transpose(w, neg_parts[:, 0].rearrange("p a h -> p (a h)"), ident_b[:])
                pe.transpose(cs, neg_parts[:, 1:3].rearrange("p r a h -> p (r a h)"), ident_b[:]).then_inc(s_mt_ps, 1)

            def column_scores(b, t, c, first):
                k = (b * T + t) * NU + c
                hs = range(c * U, c * U + U)
                if not first:
                    pe.wait_ge(s_exp, k * 3 - 2)
                for hh, h in enumerate(hs):
                    own = ps[:, 3, hh * P:(hh + 1) * P]
                    pe.matmul(own, k_stack[:, h, ds(t * P + WIN, P)], q_stack[:, h, ds(t * P, P)], start=hh == 0, stop=False, skip_group_check=True)
                    pe.matmul(own, pick_w[:, h, 0:P], rows_w[:, ds(t * P, P)], start=False, stop=False, skip_group_check=True)
                pe.matmul(ps[:, 3, :].rearrange("p (h k) -> p h k", h=U), ident_b[:], own_mask[:].unsqueeze(1).broadcast_to([P, U, P]),
                          start=False, stop=True, skip_group_check=True).then_inc(s_b, 1)
                if not first:
                    pe.wait_ge(s_exp, k * 3 - 1)
                for hh, h in enumerate(hs):
                    cs = ps[0:NCS, 4, hh * P:(hh + 1) * P]
                    pe.matmul(cs, cs_stack[:, h, :], q_stack[:, h, ds(t * P, P)], start=hh == 0, stop=False, skip_group_check=True)
                    pe.matmul(cs, pick_cs[0:96, h, :], rows_cs[:, ds(t * P, P)], start=False, stop=False, skip_group_check=True)
                pe.matmul(ps[0:NCS, 4, :].rearrange("p (h k) -> p h k", h=U), ident_b[:, 0:NCS],
                          cs_mask_cols[:, ds(t * P, P)].unsqueeze(1).broadcast_to([P, U, P]), start=False, stop=True, skip_group_check=True).then_inc(s_b, 1)
                if not first:
                    pe.wait_ge(s_exp, k * 3)
                for hh, h in enumerate(hs):
                    before = ps[0:WIN, 5, hh * WIN:(hh + 1) * WIN]
                    pe.matmul(before, k_stack[:, h, ds(t * P, WIN)], q_stack[:, h, ds(t * P, WIN)], start=hh == 0, stop=False, skip_group_check=True)
                    last = pe.matmul(before, pick_w[:, h, P:KW], rows_w[:, ds(t * P, WIN)], start=False, stop=True, skip_group_check=True)
                last.then_inc(s_b, 1)

            def with_values(b, t, c, first):
                n = b * T + t
                if c == 0:
                    pe.wait_ge(s_vt[0], (n + 1) * 32)
                if c == NU - 1:
                    pe.wait_ge(s_vt[1], (n + 1) * 32)
                if c % 2 == 0 and not first:
                    pe.wait_ge(s_wtd, n * 2 - 1 + c // 2)
                s = c % 2
                heads = [(hh, c * U + hh, ps[:, 6 + c // 2, ((c * U + hh) % 8) * OC:((c * U + hh) % 8 + 1) * OC]) for hh in range(U)]
                products = [(0, 0), (0, 1), (0, 2), (1, 0), (1, 1)]
                done(pe, s_low, (n * NU + c) * 2)
                for hh, h, o in heads:
                    for pp, vp in products:
                        w = VC if vp == 0 else HD
                        pe.matmul(o[:, 0:w], own_parts[:, s, pp, hh * P:(hh + 1) * P], v_tile[:, h, V_COLS[vp]],
                                  start=h % 8 == 0 and (pp, vp) == (0, 0), stop=False, skip_group_check=True)
                done(pe, s_low_cs, n * NU + c)
                for hh, h, o in heads:
                    for pp, vp in products:
                        pe.matmul(o[:, VC:OC], csp_parts[:, s, pp, hh * P:(hh + 1) * P], cs_parts[:, h, vp, :], start=False, stop=True, skip_group_check=True)
                done(pe, s_low, (n * NU + c) * 2 + 1)
                settled(pe)
                for hh, h, o in heads:
                    for pp, vp in products:
                        w = VC if vp == 0 else HD
                        last = pe.matmul(o[0:WIN, 0:w], before_parts[:, s, pp, hh * WIN:(hh + 1) * WIN], v_prev[:, h, V_COLS[vp]],
                                         start=False, stop=True, skip_group_check=True)
                last.then_inc(s_pv, 1)

            def tile(b, t, first, ahead):
                n = b * T + t
                for c in range(NU):
                    if ahead:
                        row_scores(b, t + 1, c)
                    if c == 0:
                        pe.wait_ge(s_mt, 2 * (n + 1))
                    column_scores(b, t, c, first and c == 0)
                    if c:
                        with_values(b, t, c - 1, first)
                    elif not first:
                        with_values(b, t - 1, NU - 1, False)
                if ahead:
                    maxima(b, t + 1)

            def attention(b):
                pe.wait_ge(s_cs_in, (b + 1) * NSLOT * 16)
                done(pe, s_smask, b * 3 + 2)
                first_cs_scores(b)
                done(pe, s_cks, b * 4)
                done(pe, s_cvlo, b * 2 + 1)
                maxima(b, 0)
                pe.wait_ge(s_stack, (b + 1) * PAIRS * NSLOT * 2 * 16)
                tile(b, 0, True, True)
                with pe.Fori(1, T - 1) as t:
                    tile(b, t, False, True)
                tile(b, T - 1, False, False)
                with_values(b, T - 1, NU - 1, False)

            def turn_attn(b, i, first):
                for u in range(2):
                    n = b * T + i * 2 + u
                    done(pe, s_at, n)
                    if not first:
                        pe.wait_ge(s_atT, n - 1)
                    for c in range(DC):
                        last = pe.transpose(ps[:, 4 * u, c * P:(c + 1) * P], attn_t[:, u, c * P:(c + 1) * P], ident_f[:])
                    last.then_inc(s_at_ps, 1)

            def project_out(b, i, first):
                for u in range(2):
                    n = b * T + i * 2 + u
                    done(pe, s_atT, n)
                    if not first:
                        pe.wait_ge(s_x1, n - 1)
                    for c in range(DC):
                        last = pe.matmul(ps[:, 4 * u + 1, 0:D], attnT[:, u, c, :], w_out[:, c, :], start=c == 0, stop=c == DC - 1)
                    last.then_inc(s_wo, 1)

            def turn_x2n(b, i, first):
                for u in range(2):
                    n = b * T + i * 2 + u
                    done(pe, s_x2n, n)
                    if not first:
                        pe.wait_ge(s_x2t, n - 1)
                    for c in range(DC):
                        last = pe.transpose(ps[:, 4 * u + 2, c * P:(c + 1) * P], x2n[:, u, c * P:(c + 1) * P], ident_f[:])
                    last.then_inc(s_x2t_ps, 1)

            def feed_forward(b, i, first):
                for u in range(2):
                    n = b * T + i * 2 + u
                    done(pe, s_x2t, n)
                    if not first:
                        pe.wait_ge(s_ffs, n - 1)
                    for c in range(DC):
                        last = pe.matmul(ps[:, 4 * u + 3, 0:D], x2nT[:, u, c, :], w_ffn[:, c, :], start=c == 0, stop=c == DC - 1)
                    last.then_inc(s_ffn, 1)

            with pe.Fori(0, B) as b:
                front(b, 0, True)
                with pe.Fori(1, PAIRS) as i:
                    front(b, i, False)
                    back(b, i - 1, True)
                back(b, PAIRS - 1, False)
                selection(b)
                attention(b)
                pe.wait_ge(s_wtd, (b + 1) * T * 2)
                turn_attn(b, 0, True)
                project_out(b, 0, True)
                for i in range(1, PAIRS):
                    turn_attn(b, i, False)
                    turn_x2n(b, i - 1, i == 1)
                    project_out(b, i, False)
                    feed_forward(b, i - 1, i == 1)
                turn_x2n(b, PAIRS - 1, False)
                feed_forward(b, PAIRS - 1, False)

        @block.scalar
        def _(act):
            def copy(o, i):
                return act.activation(o, i, ACT.Copy)

            def front(b, i, first):
                for u in range(2):
                    n = b * T + i * 2 + u
                    done(act, s_xt_ps, n)
                    copy(xnT[:, u], ps[:, 4 * u, 0:D].rearrange("p (c q) -> p c q", c=DC)).then_inc(s_xt, 1)
                for u in range(2):
                    t = i * 2 + u
                    n = b * T + t
                    done(act, s_proj, n)
                    if not first:
                        act.wait_ge(s_rc, n - 1)
                        act.wait_ge(s_rs, n - 1)
                    copy(qk[:, u], ps[:, 4 * u + 1, :]).then_inc(s_qk, 1)
                    copy(values[:, ds(t, 1), :].rearrange("p a d -> p (a d)"), ps[:, 4 * u + 2, 0:D])
                    copy(gate[:, ds(t, 1), :].rearrange("p a c -> p (a c)"), ps[:, 4 * u + 2, D:D + 3]).then_inc(s_vg, 1)

            def back(b, i, first):
                for u in range(2):
                    t = i * 2 + u
                    n = b * T + t
                    done(act, s_rope, n)
                    copy(k_tok[:, ds(t, 1), :].rearrange("p a d -> p (a d)"), roped[:, u, D:2 * D]).then_inc(s_ktok, 1)
                for u in range(2):
                    t = i * 2 + u
                    n = b * T + t
                    done(act, s_qkt, n)
                    copy(parts[:, 0, :, ds(t * P, P)], ps[:, 4 * u + 3, :].rearrange("p (c q) -> p c q", c=4)).then_inc(s_hi, 1)
                for u in range(2):
                    t = i * 2 + u
                    n = b * T + t
                    done(act, s_rest1, n)
                    copy(parts[:, 1, :, ds(t * P, P)], rest[:, u]).then_inc(s_mid, 1)

            def probabilities(b, t, c, first):
                k = (b * T + t) * NU + c
                if not first:
                    act.wait_ge(s_pv, k - 1)
                s = c % 2
                for j, (full, halves, scores) in enumerate((
                    (p_own[:, s, :], own_parts[:, s, 0, :], ps[:, 3, :]),
                    (p_cs[:, s, :], csp_parts[:, s, 0, :], ps[0:NCS, 4, :]),
                    (p_before[:, s, :], before_parts[:, s, 0, :], ps[0:WIN, 5, 0:U * WIN]),
                )):
                    done(act, s_b, k * 3 + j)
                    bias = p_bias[0:full.shape[0], :]
                    act.activation(full, scores, ACT.Exp, bias=bias)
                    act.activation(halves, scores, ACT.Exp, bias=bias).then_inc(s_exp, 1)

            def first_half(b, i, first):
                for u in range(2):
                    t = i * 2 + u
                    n = b * T + t
                    if not first:
                        act.wait_ge(s_at_ps, n - 1)
                    copy(attn_t[:, u], attn[:, ds(t, 1), :].rearrange("p a d -> p (a d)")).then_inc(s_at, 1)
                for u in range(2):
                    n = b * T + i * 2 + u
                    done(act, s_at_ps, n)
                    if not first:
                        act.wait_ge(s_wo, n - 1)
                    copy(attnT[:, u], ps[:, 4 * u, 0:D].rearrange("p (c q) -> p c q", c=DC)).then_inc(s_atT, 1)

            def second_half(b, i, first):
                for u in range(2):
                    n = b * T + i * 2 + u
                    done(act, s_x2t_ps, n)
                    if not first:
                        act.wait_ge(s_ffn, n - 1)
                    copy(x2nT[:, u], ps[:, 4 * u + 2, 0:D].rearrange("p (c q) -> p c q", c=DC)).then_inc(s_x2t, 1)

            with act.Fori(0, B) as b:
                front(b, 0, True)
                with act.Fori(1, PAIRS) as i:
                    front(b, i, False)
                    back(b, i - 1, True)
                back(b, PAIRS - 1, False)
                done(act, s_vg, b * T + T - 1)
                by_head = lambda a: a.rearrange("p t (h d) -> p t h d", h=H)
                copy(v_parts[:, :, :, 0:HD], by_head(values[:])).then_inc(s_vhi, 1)
                done(act, s_vrest, b)
                copy(v_parts[:, :, :, V_COLS[1]], by_head(v_rest[:])).then_inc(s_vmid, 1)
                done(act, s_gsub, b * 3 + 2)
                act.activation(gate[:], gate[:], ACT.Exp).then_inc(s_gexp, 1)
                done(act, s_sel_ps, b)
                for rows, at in cs_places:
                    copy(cs_parts[rows, :, 0, at:at + HD], ps[rows, 5, 0:D].rearrange("p (h d) -> p h d", h=H)).then_inc(s_cvhi, 1)
                for k, (rows, at) in enumerate(cs_places):
                    done(act, s_cvrest, b * 2 + k)
                    copy(cs_parts[rows, :, 1, at:at + HD], cs_rest[rows]).then_inc(s_cvmid, 1)
                for c in range(NU):
                    probabilities(b, 0, c, c < 2)
                with act.Fori(1, T) as t:
                    for c in range(NU):
                        probabilities(b, t, c, False)
                done(act, s_attn, (b * T + T - 1) * 2 + 1)
                first_half(b, 0, True)
                for i in range(1, PAIRS):
                    first_half(b, i, False)
                    second_half(b, i - 1, i == 1)
                second_half(b, PAIRS - 1, False)
                for u in range(2):
                    act.wait_ge(s_out[u], (b + 1) * PAIRS * 16)

        @block.vector
        def _(dve):
            dve.memset(ones[:], 1.0)
            dve.memset(minus_half[:], -0.5)
            dve.memset(p_bias[:], P_BIAS)
            dve.memset(v_parts[:, :, :, HD:VC], 1.0)
            dve.memset(k_stack[:, :, 0:WIN], 0.0)
            dve.memset(cs_parts[:], 0.0).then_inc(s_setup, 1)
            dve.wait_ge(s_setup, 1)
            dve.memset(cs_parts[0:NB, :, 0, HD:VC], 1.0)
            dve.memset(cs_parts[NB:NCS, :, 0, 2 * VC - 1:2 * VC], 1.0).then_inc(s_w, 1)
            dve.wait_ge(s_const, 16 * len(loads))
            dve.tensor_scalar(w_in[:, :, 0:D], w_in[:, :, 0:D], 1.0 / float(np.sqrt(HD)), None, ALU.mult)
            dve.tensor_scalar(scb_all[:], scb_all[:], 1.0 / 127.0, None, ALU.mult)
            dve.tensor_scalar(gather[:], block_of[:], wv_col[:, 0:1], None, ALU.mult)
            dve.tensor_scalar(wk_rows, ones[0:16, 0:NB], wk_col[0:16, 0:1], None, ALU.mult)
            dve.memset(wv_rows, 0.0).then_inc(s_setup, 1)
            dve.wait_ge(s_setup, 2)
            dve.tensor_scalar(wv_rows[:, 0:NB], ones[0:16, 0:NB], wv_col[0:16, 0:1], None, ALU.mult).then_inc(s_w, 1)
            dve.wait_ge(s_setup_pe, 1)
            dve.tensor_copy(w_ffn[:], ps[:, 0:DC, 0:D]).then_inc(s_w, 1)
            dve.wait_ge(s_setup_pe, 2)
            dve.tensor_copy(pe_key[:], ps[:, 2, 0:2]).then_inc(s_w, 1)

            def layernorm(n, u, src, bn, mv, ve):
                dve.bn_stats(bn6[:, u], src).then_inc(bn, 1)
                done(dve, bn, n)
                settled(dve)
                dve.bn_aggr(mean_var[:, u], bn6[:, u]).then_inc(mv, 1)
                done(dve, mv, n)
                dve.tensor_scalar(var_eps[:, u:u + 1], mean_var[:, u, 1:2], EPS, None, ALU.add).then_inc(ve, 1)

            def front(b, i, first):
                for u in range(2):
                    t = i * 2 + u
                    layernorm(b * T + t, u, x_in[:, ds(t, 1), :].rearrange("p a d -> p (a d)"), s_bn, s_mv, s_ve)
                for u in range(2):
                    t = i * 2 + u
                    n = b * T + t
                    done(dve, s_rstd, n)
                    if not first:
                        dve.wait_ge(s_xt_ps, n - 1)
                    dve.tensor_scalar(xn[:, u], x_in[:, ds(t, 1), :].rearrange("p a d -> p (a d)"), mean_var[:, u, 0:1], rstd[:, u:u + 1],
                                      ALU.subtract, ALU.mult).then_inc(s_xn, 1)
                done(dve, s_xn, b * T + i * 2 + 1)
                settled(dve)

            def rope(b, i, first):
                heads = lambda a: a.rearrange("p (h d) -> p h d", d=HD)
                for u in range(2):
                    t = i * 2 + u
                    n = b * T + t
                    done(dve, s_qk, n)
                    if not first:
                        dve.wait_ge(s_qkt, n - 1)
                        dve.wait_ge(s_ktok, n - 1)
                    dve.tensor_tensor(heads(roped[:, u]), heads(qk[:, u]), cos[:, ds(t, 1), :].broadcast_to([P, 2 * H, HD]), ALU.mult).then_inc(s_rc, 1)
                for u in range(2):
                    n = b * T + i * 2 + u
                    done(dve, s_rc, n)
                    done(dve, s_rs, n)
                    dve.tensor_tensor(roped[:, u], roped[:, u], rope_s[:, u], ALU.add).then_inc(s_rope, 1)

            def back(b, i, first):
                for u in range(2):
                    t = i * 2 + u
                    n = b * T + t
                    done(dve, s_hi, n)
                    if not first:
                        dve.wait_ge(s_lo, n - 1)
                    dve.tensor_tensor(weighted_k[:].rearrange("p (n k) -> p n k", k=16), ps[:, 4 * u + 3, D:2 * D].rearrange("p (n k) -> p n k", k=16),
                                      wk_all[:].unsqueeze(1).broadcast_to([P, 16, 16]), ALU.mult).then_inc(s_wk, 1)
                    dve.tensor_reduce(q_sums[:, ds(t, 1), :].rearrange("p a g -> p (a g)"), ps[:, 4 * u + 3, 0:D].rearrange("p (g s) -> p g s", g=2), AX.X, ALU.add)
                    dve.tensor_tensor(rest[:, u], ps[:, 4 * u + 3, :].rearrange("p (c q) -> p c q", c=4), parts[:, 0, :, ds(t * P, P)],
                                      ALU.subtract).then_inc(s_rest1, 1)
                    done(dve, s_wk, n)
                    dve.tensor_reduce(ck[:, :, ds(t * 8, 8)], weighted_k[:].rearrange("p (g n k) -> p g n k", g=2, k=16), AX.X, ALU.add).then_inc(s_ckt, 1)
                    done(dve, s_ckt, n)
                    settled(dve)

            def selection(b):
                dve.tensor_tensor(ck[:, :, 0:NB], ck[:, :, 0:NB], pe_key[:].unsqueeze(2).broadcast_to([P, 2, NB]), ALU.add).then_inc(s_ck, 1)
                dve.tensor_reduce(q_sum[:], q_sums[:].rearrange("p t g -> p g t"), AX.X, ALU.add).then_inc(s_qsum, 1)
                by_head = lambda a: a.rearrange("p t (h d) -> p t h d", h=H)
                done(dve, s_vhi, b)
                dve.tensor_tensor(by_head(v_rest[:]), by_head(values[:]), v_parts[:, :, :, 0:HD], ALU.subtract).then_inc(s_vrest, 1)
                done(dve, s_imp_ps, b)
                dve.tensor_copy(imp[:], ps[0:1, 1, 0:NB]).then_inc(s_top, 1)
                done(dve, s_top, b * 4)
                settled(dve)
                dve.max(imp_max[:], imp[:]).then_inc(s_top, 1)
                done(dve, s_top, b * 4 + 1)
                settled(dve)
                dve.max_index(imp_idx[:], imp_max[:], imp[:]).then_inc(s_top, 1)
                done(dve, s_top, b * 4 + 2)
                dve.tensor_scalar(sel_start[:], imp_idx[:], 16.0, None, ALU.mult).then_inc(s_top, 1)
                done(dve, s_start_ps, b)
                dve.tensor_copy(start_all[:], ps[:, 2, 0:3]).then_inc(s_start, 1)
                done(dve, s_start, b)
                for j in range(2):
                    cols = slice(NB + 8 * j, NB + 8 * j + 8)
                    dve.tensor_scalar(gather[:, :, cols], since[:], start_all[:, j:j + 1], None, ALU.is_equal).then_inc(s_onehot, 1)
                for j in range(2):
                    cols = slice(NB + 8 * j, NB + 8 * j + 8)
                    dve.tensor_scalar(cs_mask[:, :, cols], since[:], start_all[:, j:j + 1], MASKED, ALU.is_lt, ALU.mult).then_inc(s_smask, 1)
                dve.tensor_scalar(cs_mask_cols[NB:NCS, :], since_cols, start_all[NB:NCS, 2:3], MASKED, ALU.is_lt, ALU.mult).then_inc(s_smask, 1)
                dve.tensor_tensor(gate[:], gate[:], bg_all[:].unsqueeze(1).broadcast_to([P, T, 3]), ALU.add).then_inc(s_gsub, 1)
                done(dve, s_gsub, b * 3)
                dve.tensor_reduce(gate_max[:], gate[:], AX.X, ALU.max).then_inc(s_gsub, 1)
                done(dve, s_gsub, b * 3 + 1)
                dve.tensor_tensor(gate[:], gate[:], gate_max[:].unsqueeze(2).broadcast_to([P, T, 3]), ALU.subtract).then_inc(s_gsub, 1)
                done(dve, s_vmid, b)
                dve.tensor_tensor(v_parts[:, :, :, V_COLS[2]], by_head(v_rest[:]), v_parts[:, :, :, V_COLS[1]], ALU.subtract).then_inc(s_vlo, 1)
                done(dve, s_selk_ps, b)
                dve.tensor_copy(ck[:, :, NB:NCS], ps[:, 4, 0:2 * NSEL].rearrange("p (g n) -> p g n", g=2)).then_inc(s_cks, 1)
                done(dve, s_cks, b * 4)
                dve.tensor_copy(ck_parts[:, 0], ck[:]).then_inc(s_cks, 1)
                done(dve, s_cks, b * 4 + 1)
                dve.tensor_tensor(ck_rest[:], ck[:], ck_parts[:, 0], ALU.subtract).then_inc(s_cks, 1)
                done(dve, s_cks, b * 4 + 2)
                dve.tensor_copy(ck_parts[:, 1], ck_rest[:]).then_inc(s_cks, 1)
                done(dve, s_cks, b * 4 + 3)
                dve.tensor_tensor(ck_parts[:, 2], ck_rest[:], ck_parts[:, 1], ALU.subtract).then_inc(s_ckp, 1)
                reduce_first_windows(b)
                done(dve, s_sel_ps, b)
                for k, (rows, at) in enumerate(cs_places):
                    done(dve, s_cvhi, b * 2 + k)
                    dve.tensor_tensor(cs_rest[rows], ps[rows, 5, 0:D].rearrange("p (h d) -> p h d", h=H), cs_parts[rows, :, 0, at:at + HD],
                                      ALU.subtract).then_inc(s_cvrest, 1)
                done(dve, s_gexp, b)
                dve.tensor_reduce(gate_sum[:], gate[:], AX.X, ALU.add).then_inc(s_gate, 1)
                done(dve, s_gate, b * 4)
                dve.reciprocal(gate_inv[:], gate_sum[:]).then_inc(s_gate, 1)
                done(dve, s_gate, b * 4 + 1)
                for to, of, n in ((0, 2, 1), (1, 0, 2)):
                    dve.tensor_tensor(branch_gate[:, :, to:to + n], gate[:, :, of:of + n], gate_inv[:].unsqueeze(2).broadcast_to([P, T, n]),
                                      ALU.mult).then_inc(s_gate, 1)
                for k, (rows, at) in enumerate(cs_places):
                    done(dve, s_cvmid, b * 2 + k)
                    dve.tensor_tensor(cs_parts[rows, :, 2, at:at + HD], cs_rest[rows], cs_parts[rows, :, 1, at:at + HD], ALU.subtract).then_inc(s_cvlo, 1)
                done(dve, s_gate, b * 4 + 3)

            def reduce_unit(b, t, c):
                done(dve, s_a, (b * T + t) * NU + c)
                hs = slice(c * U, c * U + U)
                dve.tensor_reduce(neg_max[:, 0, hs].rearrange("p (j h) -> p j h", j=2),
                                  ps[:, 0:2, 0:2 * KW].rearrange("p j (h k) -> p j h k", h=2), AX.X, ALU.max, negate=True)
                cs = ps[:, 2, 0:U * NCS].rearrange("p (h k) -> p h k", h=U)
                dve.tensor_reduce(neg_max[:, 1, hs], cs[:, :, 0:NB], AX.X, ALU.max, negate=True)
                dve.tensor_reduce(neg_max[:, 2, hs], cs[:, :, NB:NCS], AX.X, ALU.max, negate=True).then_inc(s_max, 1)

            def reduce_first_windows(b):
                for c in range(NU):
                    done(dve, s_fa, b * NU + c)
                    banks = 2 * (c % 2)
                    dve.tensor_reduce(neg_max[:, 0, c * U:c * U + U].rearrange("p (j h) -> p j h", j=2),
                                      ps[:, banks:banks + 2, 0:2 * KW].rearrange("p j (h k) -> p j h k", h=2), AX.X, ALU.max, negate=True).then_inc(s_fmax, 1)

            def reduce_first_cs(b):
                for c in range(NU):
                    done(dve, s_a, b * T * NU + c)
                    cs = ps[:, c, 0:U * NCS].rearrange("p (h k) -> p h k", h=U)
                    dve.tensor_reduce(neg_max[:, 1, c * U:c * U + U], cs[:, :, 0:NB], AX.X, ALU.max, negate=True)
                    dve.tensor_reduce(neg_max[:, 2, c * U:c * U + U], cs[:, :, NB:NCS], AX.X, ALU.max, negate=True).then_inc(s_max, 1)

            def split_maxima(b, t):
                n = b * T + t
                done(dve, s_max, n * NU + NU - 1)
                dve.tensor_scalar(neg_lim[:], neg_max[:], LEAST, None, ALU.min).then_inc(s_neg, 1)
                done(dve, s_neg, n * 5)
                dve.tensor_copy(neg_parts[:, :, 0], neg_lim[:]).then_inc(s_neg, 1)
                done(dve, s_neg, n * 5 + 1)
                dve.tensor_tensor(neg_rest[:], neg_lim[:], neg_parts[:, :, 0], ALU.subtract).then_inc(s_neg, 1)
                done(dve, s_neg, n * 5 + 2)
                dve.tensor_copy(neg_parts[:, :, 1], neg_rest[:]).then_inc(s_neg, 1)
                done(dve, s_neg, n * 5 + 3)
                dve.tensor_tensor(neg_parts[:, :, 2], neg_rest[:], neg_parts[:, :, 1], ALU.subtract).then_inc(s_neg, 1)

            def copy_maxima(b, t):
                done(dve, s_mt_ps, b * T + t)
                dve.tensor_copy(rows_w[0:48, ds(t * P, P)], ps[0:48, 2, 0:64].bitcast(BF16)).then_inc(s_mt, 1)
                dve.tensor_copy(rows_cs[0:96, ds(t * P, P)], ps[0:96, 2, 64:128].bitcast(BF16)).then_inc(s_mt, 1)
                done(dve, s_mt, (b * T + t) * 2 + 1)
                settled(dve)

            def low_parts(b, t, c):
                k = (b * T + t) * NU + c
                s = c % 2
                done(dve, s_exp, k * 3)
                dve.tensor_tensor(own_parts[:, s, 1, :], p_own[:, s, :], own_parts[:, s, 0, :], ALU.subtract).then_inc(s_low, 1)
                done(dve, s_exp, k * 3 + 2)
                dve.tensor_tensor(before_parts[:, s, 1, :], p_before[:, s, :], before_parts[:, s, 0, :], ALU.subtract).then_inc(s_low, 1)

            def combine(b, t, j):
                m = (b * T + t) * 2 + j
                done(dve, s_pv, (b * T + t) * NU + 2 * j + 1)
                hs = slice(8 * j, 8 * j + 8)
                o = ps[:, 6 + j, 0:8 * OC].rearrange("p (h r d) -> p h r d", h=8, r=3)
                dve.tensor_scalar(den[:, hs, :].unsqueeze(3), o[:, :, :, HD:VC], 1e-30, None, ALU.max).then_inc(s_den, 1)
                done(dve, s_den, m * 3)
                dve.reciprocal(den_inv[:, hs], den[:, hs]).then_inc(s_den, 1)
                done(dve, s_den, m * 3 + 1)
                dve.tensor_tensor(weight[:, hs], den_inv[:, hs], branch_gate[:, ds(t, 1), :].broadcast_to([P, 8, 3]), ALU.mult).then_inc(s_den, 1)
                done(dve, s_den, m * 3 + 2)
                dve.tensor_tensor(weighted[:], o[:, :, :, 0:HD], weight[:, hs].unsqueeze(3).broadcast_to([P, 8, 3, HD]),
                                  ALU.mult).then_inc(s_wtd, 1)
                done(dve, s_wtd, m)
                dve.tensor_reduce(attn[:, ds(t, 1), P * j:P * j + P].rearrange("p a (h d) -> p (a h) d", h=8),
                                  weighted[:].rearrange("p h r d -> p h d r"), AX.X, ALU.add).then_inc(s_attn, 1)
                done(dve, s_attn, m)
                settled(dve)

            def attend(b, t, first, ahead):
                for c in range(NU):
                    if c:
                        low_parts(b, t, c - 1)
                    elif not first:
                        low_parts(b, t - 1, NU - 1)
                    if ahead:
                        reduce_unit(b, t + 1, c)
                    if c < 2 and not first:
                        combine(b, t - 1, c)
                if ahead:
                    split_maxima(b, t + 1)
                    copy_maxima(b, t + 1)

            def residual(b, i, first):
                for u in range(2):
                    n = b * T + i * 2 + u
                    done(dve, s_wo, n)
                    done(dve, s_xrb, n)
                    if not first:
                        dve.wait_ge(s_x1b, n - 1)
                    dve.tensor_tensor(x1[:, u], ps[:, 4 * u + 1, 0:D], x_res[:, u], ALU.add).then_inc(s_x1, 1)
                    done(dve, s_x1, n)
                    layernorm(n, u, x1[:, u], s_bn2, s_mv2, s_ve2)

            def normalise(b, i, first):
                for u in range(2):
                    n = b * T + i * 2 + u
                    done(dve, s_rstd2, n)
                    if not first:
                        dve.wait_ge(s_x2t_ps, n - 1)
                    dve.tensor_scalar(x2n[:, u], x1[:, u], mean_var[:, u, 0:1], rstd[:, u:u + 1], ALU.subtract, ALU.mult).then_inc(s_x2n, 1)
                done(dve, s_x2n, b * T + i * 2 + 1)
                settled(dve)

            def result(b, i, first):
                for u in range(2):
                    n = b * T + i * 2 + u
                    done(dve, s_ffn, n)
                    dve.tensor_tensor(ffn[:, u], ps[:, 4 * u + 3, 0:D], scb_all[:], ALU.mult).then_inc(s_ffs, 1)
                    done(dve, s_ffs, n)
                    done(dve, s_x1b, n)
                    if not first:
                        dve.wait_ge(s_out[u], (b * PAIRS + i) * 16)
                    dve.tensor_tensor(y[:, u], ffn[:, u], x1b[:, u], ALU.add).then_inc(s_y, 1)
                done(dve, s_y, b * T + i * 2 + 1)
                settled(dve)

            with dve.Fori(0, B) as b:
                dve.wait_ge(s_x, (b + 1) * 16)
                front(b, 0, True)
                front(b, 1, False)
                rope(b, 0, True)
                front(b, 2, False)
                back(b, 0, True)
                rope(b, 1, False)
                with dve.Fori(2, PAIRS - 1) as i:
                    front(b, i + 1, False)
                    back(b, i - 1, False)
                    rope(b, i, False)
                dve.sem_inc(s_xused, 1)
                rope(b, PAIRS - 1, False)
                back(b, PAIRS - 2, False)
                back(b, PAIRS - 1, False)
                selection(b)
                reduce_first_cs(b)
                split_maxima(b, 0)
                copy_maxima(b, 0)
                attend(b, 0, True, True)
                with dve.Fori(1, T - 1) as t:
                    attend(b, t, False, True)
                attend(b, T - 1, False, False)
                combine(b, T - 1, 0)
                low_parts(b, T - 1, NU - 1)
                combine(b, T - 1, 1)
                residual(b, 0, True)
                normalise(b, 0, True)
                for i in range(1, PAIRS):
                    residual(b, i, False)
                    result(b, i - 1, i == 1)
                    normalise(b, i, False)
                result(b, PAIRS - 1, False)

        @block.gpsimd
        def _(pool):
            def deviations(b, i, ve, out_sem):
                for u in range(2):
                    n = b * T + i * 2 + u
                    done(pool, ve, n)
                    pool.tensor_tensor(rstd[:, u:u + 1], var_eps[:, u:u + 1], minus_half[:], ALU.pow).then_inc(out_sem, 1)

            def sin_products(b, i, first):
                heads = lambda a: a.rearrange("p (h d) -> p h d", d=HD)
                for u in range(2):
                    t = i * 2 + u
                    n = b * T + t
                    done(pool, s_qk, n)
                    if not first:
                        pool.wait_ge(s_rope, n - 1)
                    for e in range(2):
                        s = sin[:, ds(t, 1), e::2].broadcast_to([P, 2 * H, HD // 2])
                        last = pool.tensor_tensor(heads(rope_s[:, u])[:, :, e::2], heads(qk[:, u])[:, :, 1 - e::2], s, ALU.mult)
                    last.then_inc(s_rs, 1)

            def low_parts(b, i):
                for u in range(2):
                    t = i * 2 + u
                    n = b * T + t
                    done(pool, s_mid, n)
                    pool.tensor_tensor(parts[:, 2, :, ds(t * P, P)], rest[:, u], parts[:, 1, :, ds(t * P, P)], ALU.subtract).then_inc(s_lo, 1)

            def output(b, i, first):
                for u in range(2):
                    n = b * T + i * 2 + u
                    pool.wait_ge(s_xr[u], (b * (PAIRS + 1) + i + 1) * 16)
                    pool.tensor_tensor(x_res[:, u], x_res[:, u], bo_all[:], ALU.add).then_inc(s_xrb, 1)
                deviations(b, i, s_ve2, s_rstd2)
                for u in range(2):
                    n = b * T + i * 2 + u
                    if not first:
                        pool.wait_ge(s_y, n - 1)
                    pool.tensor_tensor(x1b[:, u], x1[:, u], bias_all[:], ALU.add).then_inc(s_x1b, 1)

            pool.wait_ge(s_const, 16 * len(loads))
            pool.wait_ge(s_w, 1)
            with pool.Fori(0, B) as b:
                deviations(b, 0, s_ve, s_rstd)
                deviations(b, 1, s_ve, s_rstd)
                sin_products(b, 0, True)
                with pool.Fori(1, PAIRS - 1) as i:
                    deviations(b, i + 1, s_ve, s_rstd)
                    sin_products(b, i, False)
                    low_parts(b, i - 1)
                sin_products(b, PAIRS - 1, False)
                low_parts(b, PAIRS - 2)
                low_parts(b, PAIRS - 1)
                with pool.Fori(0, T) as t:
                    for c in range(NU):
                        k = (b * T + t) * NU + c
                        done(pool, s_exp, k * 3 + 1)
                        pool.tensor_tensor(csp_parts[:, c % 2, 1, :], p_cs[:, c % 2, :], csp_parts[:, c % 2, 0, :], ALU.subtract).then_inc(s_low_cs, 1)
                output(b, 0, True)
                for i in range(1, PAIRS):
                    output(b, i, False)


INS = ["L0_attn_x", "L0_attn_Wq", "L0_attn_Wk", "L0_attn_Wv", "L0_attn_Wo", "L0_attn_bo", "L0_attn_wk_comp",
       "L0_attn_wv_comp", "L0_attn_pe", "L0_attn_Wg", "L0_attn_bg", "L0_ffn_CB", "L0_ffn_SCB", "L0_ffn_bias"]


def kernel(**inputs):
    import numpy as _np
    import concourse.bacc as _bacc
    from concourse import mybir as _mybir
    from concourse.bass_utils import run_bass_kernel_spmd as _run

    nc = _bacc.Bacc("TRN2", target_bir_lowering=False, num_devices=1)
    arrays, args = {}, []
    for name in INS:
        a = _np.ascontiguousarray(inputs[name])
        arrays[f"in_{name}"] = a
        args.append(nc.dram_tensor(f"in_{name}", a.shape, _mybir.dt.from_np(a.dtype), kind="ExternalInput").ap())
    consts = {}
    for group in shape_constants():
        for name, a in group.items():
            arrays[f"const_{name}"] = a
            consts[name] = nc.dram_tensor(f"const_{name}", a.shape, _mybir.dt.from_np(a.dtype), kind="ExternalInput").ap()
    out = nc.dram_tensor("out", (B, S, D), _mybir.dt.float32, kind="ExternalOutput").ap()
    build(nc, *args, consts, out)
    r = _run(nc, [arrays], core_ids=[0])
    return r.results[0]["out"]
```

```python
import numpy as np
import concourse.bass as bass
from concourse import mybir
from contextlib import ExitStack

F32 = mybir.dt.float32
BF16 = mybir.dt.bfloat16
F16 = mybir.dt.float16
U32 = mybir.dt.uint32
ALU = mybir.AluOpType
ACT = mybir.ActivationFunctionType
AX = mybir.AxisListType
ds = bass.ds

P = 128
B, S, D = 8, 1024, 256
H, HD = 16, 16
T = S // P
PAIRS = T // 2
DC = D // P
NB = S // 16
NSEL = 16
WIN = 64
NCS = NB + NSEL
KW = P + WIN
U = 4
NU = H // U
VC = HD + 1
V_COLS = (slice(0, VC), slice(VC, VC + HD), slice(VC + HD, VC + 2 * HD))
VPC = VC + 2 * HD
EARLY, LATE = slice(0, H - U), slice(H - U, H)
OC = 3 * VC
NP1 = 3 * D + 3
Q_PARTS = (0, 0, 0, 1, 1, 2)
K_PARTS = (0, 1, 2, 0, 1, 0)
NSLOT = len(Q_PARTS)
KR_ROWS = NSLOT * HD
MASKED = -1e30
LEAST = 1e29
EPS = 1e-5
P_BIAS = 11 * float(np.log(2.0))


def shape_constants():
    p = np.arange(P)
    t = np.arange(T)

    def bits(a):
        return (np.ascontiguousarray(a, np.float32).view(np.uint32) >> 16).astype(np.uint16)

    j = np.arange(KW) - WIN
    ok = (j[None, :] <= p[:, None]) & (j[None, :] > p[:, None] - WIN)
    ok = ok[:, None, :] & ((t[None, :2, None] * P + j[None, None, :]) >= 0)
    window_mask = np.where(ok, 0.0, MASKED)
    s = t[None, :, None] * P + p[:, None, None]
    n = np.arange(NB)
    cs_mask = np.zeros((P, T, NCS))
    cs_mask[:, :, :NB] = np.where((n[None, None, :] + 1) * 16 <= s, 0.0, MASKED)
    own_mask = np.where((p[:, None] <= p[None, :]) & (p[:, None] > p[None, :] - WIN), 0.0, MASKED)
    pick_w = np.zeros((P, H, KW))
    for part in range(3):
        for h in range(H):
            pick_w[part * H + h, h, :] = 1.0
    for k in range(WIN):
        pick_w[WIN + k, :, P + k] = 1.0
    rows_w = np.zeros((P, S))
    q = np.arange(S)
    kl = np.arange(WIN)
    rows_w[WIN:] = np.where((kl[:, None] > (q % P)[None, :]) & (q[None, :] >= P), 0.0, MASKED)
    pick_cs = np.zeros((P, H, NCS))
    for part in range(3):
        for h in range(H):
            pick_cs[part * H + h, h, :NB] = 1.0
            pick_cs[48 + part * H + h, h, NB:] = 1.0
    cs_mask_cols = np.zeros((P, S))
    cs_mask_cols[:NB] = np.where((n[:, None] + 1) * 16 <= q[None, :], 0.0, MASKED)
    b16 = {
        "window_mask": window_mask, "cs_mask": cs_mask, "own_mask": own_mask, "pick_w": pick_w,
        "rows_w": rows_w, "pick_cs": pick_cs, "cs_mask_cols": cs_mask_cols, "ident_b": np.eye(P),
    }
    half = HD // 2
    inv = (1.0 / 10000.0 ** (np.arange(half, dtype=np.float32) * np.float32(2.0) / np.float32(HD))).astype(np.float32)
    ang = np.arange(S, dtype=np.float32)[:, None] * inv[None, :]
    cos = np.repeat(np.cos(ang), 2, axis=1)
    sin = np.stack([-np.sin(ang), np.sin(ang)], -1).reshape(S, HD)
    by_tile = lambda a: a.reshape(T, P, HD).transpose(1, 0, 2)
    r = np.arange(8)
    since = (t[None, :, None] * P + p[:, None, None]) - r[None, None, :]
    since_cols = q[None, :] - (np.arange(NSEL) % 8)[:, None]
    block_of = np.zeros((P, T, NCS))
    for pp in range(P):
        for tt in range(T):
            block_of[pp, tt, 8 * tt + pp // 16] = 1.0
    sel_rows = np.zeros((1, 2, P))
    sel_rows[0, 0, NB:NB + 8] = 1.0
    sel_rows[0, 1, NB + 8:NCS] = 1.0
    f32 = {
        "ident_f": np.eye(P), "cos": by_tile(cos), "sin": by_tile(sin), "since": since,
        "since_cols": since_cols, "block_of": block_of, "sel_rows": sel_rows,
    }
    return (
        {k: np.ascontiguousarray(bits(v).reshape(P, -1)) for k, v in b16.items()},
        {k: np.ascontiguousarray(v.astype(np.float32).reshape(v.shape[0], -1)) for k, v in f32.items()},
    )


def build(nc, x, Wq, Wk, Wv, Wo, bo, wk_comp, wv_comp, pe_, Wg, bg, CB, SCB, bias, consts, out):
    ctx = ExitStack()
    with ctx:
        def sb(name, shape, dt=F32):
            return ctx.enter_context(nc.sbuf_tensor(name, shape, dt))

        def sem(name):
            return ctx.enter_context(nc.semaphore(name))

        ident_f = sb("ident_f", [P, P])
        both = sb("both", [P, S])
        since_cols = both[NB:NCS, :]
        pe_sb = both[0:16, 0:D]
        wk_rows = both[0:16, D:D + NB]
        wv_rows = both[0:16, D + NB:D + NB + NCS]
        cos = sb("cos", [P, T, HD])
        sin = sb("sin", [P, T, HD])
        since = sb("since", [P, T, 8])
        sel_rows = both[0:1, D + NB + NCS:D + NB + NCS + 2 * P].rearrange("p (j n) -> p j n", j=2)
        ident_b = sb("ident_b", [P, P], BF16)
        window_mask = sb("window_mask", [P, 2, KW], BF16)
        cs_mask = sb("cs_mask", [P, T, NCS], BF16)
        own_mask = sb("own_mask", [P, P], BF16)
        pick_w = sb("pick_w", [P, H, KW], BF16)
        rows_w = sb("rows_w", [P, S], BF16)
        pick_cs = sb("pick_cs", [P, H, NCS], BF16)
        rows_cs = sb("rows_cs", [96, S], BF16)
        cs_mask_cols = sb("cs_mask_cols", [P, S], BF16)
        w_in = sb("w_in", [P, DC, NP1])
        w_out = sb("w_out", [P, DC, D])
        w_ffn = sb("w_ffn", [P, DC, D])
        ones = sb("ones", [P, P])
        bo_all = sb("bo_all", [P, D])
        bias_all = sb("bias_all", [P, D])
        scb_all = sb("scb_all", [P, D])
        bg_all = sb("bg_all", [P, 3])
        wk_col = sb("wk_col", [P, 1])
        wv_col = sb("wv_col", [P, 1])
        wk_all = sb("wk_all", [P, NB // 4])
        pe_key = sb("pe_key", [P, 2])
        weighted_k = sb("weighted_k", [P, D])
        gather = sb("gather", [P, T, NCS])
        minus_half = sb("minus_half", [P, 1])
        p_bias = sb("p_bias", [P, 1])
        x_in = sb("x_in", [P, T, D])
        bn6 = sb("bn6", [P, 2, 2, 6])
        mean_var = sb("mean_var", [P, 2, 2, 2])
        var_eps = sb("var_eps", [P, 2, 2])
        rstd = sb("rstd", [P, 2, 2])
        xn = sb("xn", [P, 2, D])
        xnT = sb("xnT", [P, 2, DC, P])
        qk = sb("qk", [P, 2, 2 * D])
        rope_s = sb("rope_s", [P, 2, 2 * D])
        roped = sb("roped", [P, 2, 2 * D])
        rest = sb("rest", [P, 2, 4, P])
        shared = sb("shared", [P, 6144])
        parts = shared[:, 0:3 * 4 * 2 * P].bitcast(BF16).rearrange("p (a c s) -> p a c s", a=3, c=4)
        taken = [0]

        def part_of_shared(rows, *shape):
            n = int(np.prod(shape))
            a = shared[0:rows, taken[0]:taken[0] + n]
            taken[0] += n
            names = "abc"[:len(shape)]
            return a.rearrange(f"p ({' '.join(names)}) -> p {' '.join(names)}", **dict(zip(names, shape)))

        k_tok = sb("k_tok", [P, T, D])
        attn = k_tok
        q_sums = sb("q_sums", [P, T, 2])
        values = sb("values", [P, T, D])
        v_rest = sb("v_rest", [P, T, D])
        v_parts = sb("v_parts", [P, T, H, VPC], BF16)
        gate = sb("gate", [P, T, 3])
        q_stack = sb("q_stack", [KR_ROWS, H, S], BF16)
        k_stack = sb("k_stack", [KR_ROWS, H, WIN + S], BF16)
        cs_stack = sb("cs_stack", [KR_ROWS, H, NCS], BF16)
        ck = sb("ck", [P, 2, NCS])
        ck_rest = sb("ck_rest", [P, 2, NCS])
        ck_parts = sb("ck_parts", [P, 3, 2, NCS], BF16)
        q_sum = sb("q_sum", [P, 2])
        imp = sb("imp", [1, NB])
        imp_max = sb("imp_max", [1, 8])
        imp_idx = sb("imp_idx", [1, 8], U32)
        sel_start = sb("sel_start", [1, 8])
        start_all = sb("start_all", [P, 3])
        cs_parts = sb("cs_parts", [NCS, H, 3, 2 * VC], BF16)
        cs_rest = weighted_k[0:NCS].rearrange("p (h d) -> p h d", h=H)
        branch_gate = sb("branch_gate", [P, T, 3])
        gate_max = sb("gate_max", [P, T])
        gate_sum = sb("gate_sum", [P, T])
        gate_inv = sb("gate_inv", [P, T])
        neg_max = sb("neg_max", [P, 3, H])
        neg_lim = sb("neg_lim", [P, 3, H])
        neg_rest = sb("neg_rest", [P, 3, H])
        neg_parts = sb("neg_parts", [P, 3, 3, H], BF16)
        block_of = shared[:, 6144 - T * NCS:].rearrange("p (t n) -> p t n", t=T)
        p_own = part_of_shared(P, 2, U * P)
        p_cs = part_of_shared(NCS, 2, U * P)
        p_before = part_of_shared(WIN, 2, U * WIN)
        weighted = part_of_shared(P, 8, 3, HD)
        halves = lambda a: a.bitcast(F16).rearrange("p (s a k) -> p s a k", s=2, a=2)
        own_parts = halves(qk[:].rearrange("p u n -> p (u n)"))
        csp_parts = halves(roped[0:NCS].rearrange("p u n -> p (u n)"))
        before_parts = rope_s[:, 0, 0:U * WIN].bitcast(F16).rearrange("p (s k) -> p s k", s=2)
        rest_b = rest[:].rearrange("p u c q -> p (u c q)").bitcast(BF16)
        v_tile = rest_b[:, 0:H * VPC].rearrange("p (h v) -> p h v", h=H)
        v_prev = rest_b[:, H * VPC:2 * H * VPC].rearrange("p (h v) -> p h v", h=H)
        den = sb("den", [P, H, 3])
        den_inv = sb("den_inv", [P, H, 3])
        weight = sb("weight", [P, H, 3])
        taken[0] = 3072
        x1 = part_of_shared(P, 2, D)
        x1b = part_of_shared(P, 2, D)
        y = part_of_shared(P, 2, D)
        attn_t = part_of_shared(P, D)
        attnT = part_of_shared(P, DC, P)
        x2n = part_of_shared(P, D)
        x2nT = part_of_shared(P, DC, P)
        ffn = part_of_shared(P, D)
        x_res = sb("x_res", [P, 2, D])

        ps = ctx.enter_context(nc.psum_tensor("ps", [P, 8, 512], F32))
        part_dram = nc.dram_tensor("part_dram", [3, 2, H, HD, S], BF16).ap()
        cs_dram = nc.dram_tensor("cs_dram", [3, H, HD, NCS], BF16).ap()

        s_const = sem("constants_in")
        s_settled = sem("waits_settled")
        s_setup = sem("setup_vector")
        s_setup_pe = sem("setup_transposed")
        s_w = sem("setup_done")
        s_x = sem("x_in_loaded")
        s_xused = sem("x_in_used")
        s_bn = sem("bn_stats_done")
        s_mv = sem("mean_var_done")
        s_ve = sem("var_eps_done")
        s_rstd = sem("rstd_done")
        s_xn = sem("xn_done")
        s_xt_ps = sem("xn_transposed")
        s_xt = sem("xnT_done")
        s_proj = sem("projected")
        s_qk = sem("qk_copied")
        s_vg = sem("v_and_gate_copied")
        s_rc = sem("rope_cos_product")
        s_rs = sem("rope_sin_product")
        s_rope = sem("roped_done")
        s_ktok = sem("k_tok_done")
        s_qkt = sem("qk_transposed")
        s_hi = sem("high_part")
        s_rest = sem("rest_after_high")
        s_rest1 = sem("qk_transposes_read")
        s_mid = sem("mid_part")
        s_lo = sem("low_part")
        s_part_out = sem("parts_in_dram")
        s_stack = sem("stacks_in")
        s_vhi = sem("values_high")
        s_vrest = sem("values_rest")
        s_vmid = sem("values_mid")
        s_vlo = sem("values_low")
        s_vt = [sem("tile_values_in"), sem("tile_values_in_last_unit")]
        s_wk = sem("keys_weighted")
        s_ckt = sem("keys_summed")
        s_ck = sem("ck_copied")
        s_qsum = sem("q_sum_done")
        s_imp_ps = sem("importance_summed")
        s_top = sem("top_steps")
        s_start_ps = sem("starts_spread")
        s_start = sem("start_all_done")
        s_onehot = sem("one_hot_done")
        s_smask = sem("selected_masks_done")
        s_selk_ps = sem("selected_keys_gathered")
        s_sel_ps = sem("values_gathered")
        s_cks = sem("ck_steps")
        s_ckp = sem("ck_parts_done")
        s_cvhi = sem("cs_values_high")
        s_cvrest = sem("cs_values_rest")
        s_cvmid = sem("cs_values_mid")
        s_cvlo = sem("cs_values_low")
        s_cs_out = sem("ck_parts_in_dram")
        s_cs_in = sem("cs_stack_in")
        s_gsub = sem("gate_shifted_steps")
        s_gexp = sem("gate_exp")
        s_gate = sem("gate_done_steps")
        s_a = sem("row_scores")
        s_max = sem("row_scores_reduced")
        s_fa = sem("first_window_scores")
        s_fmax = sem("first_window_scores_reduced")
        s_neg = sem("neg_steps")
        s_mt_ps = sem("maxima_transposed")
        s_mt = sem("maxima_copied")
        s_b = sem("column_scores")
        s_exp = sem("probabilities")
        s_pv = sem("probabilities_used")
        s_low = sem("low_probabilities")
        s_low_cs = sem("low_probabilities_cs")
        s_den = sem("denominator_steps")
        s_wtd = sem("weighted_half")
        s_attn = sem("attention_half")
        s_xr = [sem("x_res_loaded_0"), sem("x_res_loaded_1")]
        s_xrb = sem("x_res_plus_bo")
        s_at = sem("attn_t_copied")
        s_at_ps = sem("attn_transposed")
        s_atT = sem("attnT_copied")
        s_wo = sem("output_projected")
        s_x1 = sem("x1_done")
        s_x1b = sem("x1_plus_bias")
        s_bn2 = sem("bn_stats_2")
        s_mv2 = sem("mean_var_2")
        s_ve2 = sem("var_eps_2")
        s_rstd2 = sem("rstd_2")
        s_x2n = sem("x2n_done")
        s_x2t_ps = sem("x2n_transposed")
        s_x2t = sem("x2nT_copied")
        s_ffn = sem("ffn_projected")
        s_ffs = sem("ffn_scaled")
        s_y = sem("y_done")
        s_out = [sem("y_stored_0"), sem("y_stored_1")]

        loads = [
            (ident_f[:], consts["ident_f"]), (cos[:], consts["cos"]), (sin[:], consts["sin"]),
            (since[:], consts["since"]), (since_cols, consts["since_cols"]),
            (block_of, consts["block_of"]), (sel_rows, consts["sel_rows"]),
        ]
        for dst, name in ((ident_b, "ident_b"), (window_mask, "window_mask"), (cs_mask, "cs_mask"),
                          (own_mask, "own_mask"), (pick_w, "pick_w"), (rows_w, "rows_w"),
                          (pick_cs, "pick_cs"), (cs_mask_cols, "cs_mask_cols")):
            loads.append((dst[:], consts[name].bitcast(BF16)))

        def shaped(dst, src):
            if len(dst.shape) == 3:
                src = src.rearrange("p (a b) -> p a b", a=dst.shape[1])
            elif len(dst.shape) == 4:
                src = src.rearrange("p (a b c) -> p a b c", a=dst.shape[1], b=dst.shape[2])
            return src

        loads = [(dst, shaped(dst, src)) for dst, src in loads]
        for k, w in enumerate((Wq, Wk, Wv)):
            loads.append((w_in[:, :, k * D:(k + 1) * D], w.rearrange("(c p) n -> p c n", p=P)))
        loads.append((w_in[:, :, 3 * D:], Wg.rearrange("(c p) n -> p c n", p=P)))
        loads.append((w_out[:], Wo.rearrange("(c p) n -> p c n", p=P)))
        loads.append((x1[:], CB.rearrange("(c p) k -> p c k", p=P)))
        loads.append((pe_sb, pe_))
        for dst, v in ((bo_all, bo), (bias_all, bias), (scb_all, SCB), (bg_all, bg)):
            loads.append((dst[:], v.partition_broadcast(P)))
        loads.append((wk_all[:], wk_comp.partition_broadcast(P)))
        for dst, v in ((wk_col, wk_comp), (wv_col, wv_comp)):
            for g in range(8):
                loads.append((dst[16 * g:16 * g + 16, :], v.rearrange("(p a) -> p a", a=1)))

        def done(eng, s, n):
            eng.wait_ge(s, n + 1)

        def settled(eng):
            eng.sem_inc(s_settled, 1)

        class Tile:
            def __init__(self, t, slot, pair, alone, first_two):
                self.t, self.u, self.i = t, slot, pair
                self.alone = alone
                self.first_two = first_two
                self.last = isinstance(t, int) and t == T - 1

        def qk_bank(k):
            return 0 if k.last else 3

        def here(k):
            return ds((k.i % 2) * 2 * P + k.u * P, P)

        def known(t):
            return Tile(t, t % 2, t // 2, t == 0, t < 2)

        def over_tiles(eng, step):
            step(known(0), known(1), None, None)
            step(known(1), known(2), known(0), None)
            step(known(2), known(3), known(1), known(0))
            with eng.Fori(1, PAIRS - 1) as i:
                c, d, e, f, g = (Tile(i * 2 + k, k % 2, i + k // 2, False, False) for k in range(-1, 4))
                step(e, f, d, c)
                step(f, g, e, d)
            step(known(T - 1), None, known(T - 2), known(T - 3))

        def x_tiles(b):
            return x[ds(b, 1)].rearrange("a (t p) d -> p (a t) d", p=P)

        cs_places = ((slice(0, NB), 0), (slice(NB, NCS), VC))
        block = ctx.enter_context(nc.Block())

        @block.sync
        def _(sp):
            for dst, src in loads:
                sp.dma_start(dst, src).then_inc(s_const, 16)
            sp.dma_start(x_in[:], x_tiles(0)).then_inc(s_x, 16)

            def next_residual(b, i):
                for u in range(2):
                    done(sp, s_x1, b * T + i * 2 + u)
                    settled(sp)
                    sp.wait_ge(s_xr[u], (b * (PAIRS + 1) + i + 1) * 16)
                    settled(sp)
                    t = ((i + 1) % PAIRS) * 2 + u
                    sp.dma_start(x_res[:, u], x[ds(b, 1), t * P:(t + 1) * P].rearrange("a p d -> p (a d)")).then_inc(s_xr[u], 16)

            def store(b, i):
                for u in range(2):
                    t = i * 2 + u
                    done(sp, s_y, b * T + t)
                    settled(sp)
                    sp.dma_start(out[ds(b, 1), t * P:(t + 1) * P].rearrange("a p d -> p (a d)"), y[:, u]).then_inc(s_out[u], 16)

            def parts_out(b, i):
                if i % 2:
                    sp.wait_ge(s_part_out, (b * PAIRS + i) * 48 + 1)
                    settled(sp)
                done(sp, s_lo, b * T + i * 2 + 1)
                settled(sp)
                for part in range(3):
                    sp.dma_start(
                        part_dram[part, :, :, :, i * 2 * P:(i + 1) * 2 * P].rearrange("w (g h) d s -> (h d) (w g) s", g=2),
                        parts[:, part, :, (i % 2) * 2 * P:(i % 2 + 1) * 2 * P],
                    ).then_inc(s_part_out, 16)

            def stacks_in(b, half):
                sp.wait_ge(s_part_out, (b * PAIRS + half * 2 + 2) * 48 + 1)
                settled(sp)
                cols = slice(half * 4 * P, (half + 1) * 4 * P)
                for slot in range(NSLOT):
                    rows = slice(slot * HD, slot * HD + HD)
                    sp.dma_start(q_stack[rows, :, cols], part_dram[Q_PARTS[slot], 0, :, :, cols].rearrange("h d s -> d h s")).then_inc(s_stack, 16)
                    sp.dma_start(k_stack[rows, :, half * 4 * P + WIN:(half + 1) * 4 * P + WIN],
                                 part_dram[K_PARTS[slot], 1, :, :, cols].rearrange("h d s -> d h s")).then_inc(s_stack, 16)

            def side_pass(ob, pb):
                for i in range(PAIRS):
                    if ob is not None:
                        next_residual(ob, i)
                    if pb is not None and i == 2:
                        stacks_in(pb, 0)
                    if ob is not None:
                        store(ob, i)
                    if pb is not None:
                        parts_out(pb, i)
                if pb is not None:
                    stacks_in(pb, 1)

            def side_attention(b, last):
                done(sp, s_ckp, b)
                for g in range(2):
                    sp.dma_start(cs_dram[:, 8 * g:8 * g + 8].rearrange("a h d n -> (h d) a n"),
                                 ck_parts[:, :, g, :]).then_inc(s_cs_out, 16)
                sp.wait_ge(s_cs_out, (b + 1) * 32)
                for slot in range(NSLOT):
                    sp.dma_start(cs_stack[slot * HD:slot * HD + HD], cs_dram[K_PARTS[slot]].rearrange("h d n -> d h n")).then_inc(s_cs_in, 16)
                done(sp, s_vlo, b)
                for hs, loaded in ((EARLY, s_vt[0]), (LATE, s_vt[1])):
                    sp.dma_start(v_tile[:, hs], v_parts[:, 0, hs]).then_inc(loaded, 16)
                    for rows in (slice(0, WIN), slice(WIN, P)):
                        sp.dma_start(v_prev[rows, hs], v_parts[WIN:P, T - 1, hs]).then_inc(loaded, 16)
                if not last:
                    done(sp, s_xused, b)
                    settled(sp)
                    sp.wait_ge(s_x, (b + 1) * 16)
                    settled(sp)
                    sp.dma_start(x_in[:], x_tiles(b + 1)).then_inc(s_x, 16)
                for u in range(2):
                    sp.dma_start(x_res[:, u], x[ds(b, 1), u * P:(u + 1) * P].rearrange("a p d -> p (a d)")).then_inc(s_xr[u], 16)
                with sp.Fori(1, T) as t:
                    for hs, loaded, left in ((EARLY, s_vt[0], 1), (LATE, s_vt[1], 0)):
                        sp.wait_ge(s_pv, (b * T + t) * NU - left)
                        settled(sp)
                        sp.wait_ge(loaded, (b * T + t) * 48)
                        settled(sp)
                        sp.dma_start(v_tile[:, hs], v_parts[:, ds(t, 1), hs].rearrange("p a h d -> p (a h) d")).then_inc(loaded, 16)
                        for rows in (slice(0, WIN), slice(WIN, P)):
                            sp.dma_start(v_prev[rows, hs], v_parts[WIN:P, ds(t - 1, 1), hs].rearrange("p a h d -> p (a h) d")).then_inc(loaded, 16)

            sp.sem_inc(s_part_out, 1)
            side_pass(None, 0)
            with sp.Fori(0, B - 1) as b:
                side_attention(b, False)
                side_pass(b, b + 1)
                for u in range(2):
                    sp.wait_ge(s_xr[u], (b + 1) * (PAIRS + 1) * 16)
                settled(sp)
            side_attention(B - 1, True)
            side_pass(B - 1, None)
            sp.wait_ge(s_x, B * 16)
            for u in range(2):
                sp.wait_ge(s_out[u], B * PAIRS * 16)
                sp.wait_ge(s_xr[u], B * (PAIRS + 1) * 16)

        @block.tensor
        def _(pe):
            pe.wait_ge(s_const, 16 * len(loads))
            for kc in range(DC):
                for ncn in range(DC):
                    last = pe.transpose(ps[:, kc, ncn * P:(ncn + 1) * P], x1[:, ncn, kc * P:(kc + 1) * P], ident_f[:])
            last.then_inc(s_setup_pe, 1)
            pe.wait_ge(s_w, 2)
            for g in range(2):
                last = pe.matmul(ps[:, 2, g:g + 1], pe_sb[:, g * P:(g + 1) * P], wk_rows[:, 0:1], start=True, stop=True)
            last.then_inc(s_setup_pe, 1)
            pe.wait_ge(s_w, 4)

            def turned(bank, src, waited_by):
                for c in range(DC):
                    last = pe.transpose(ps[:, bank, c * P:(c + 1) * P], src[:, c * P:(c + 1) * P], ident_f[:])
                last.then_inc(waited_by, 1)

            def turn_xn(b, k):
                n = b * T + k.t
                done(pe, s_xn, n)
                if not k.alone:
                    pe.wait_ge(s_xt, n)
                turned(0, xn[:, k.u], s_xt_ps)

            def project(b, k):
                n = b * T + k.t
                done(pe, s_xt, n)
                if not k.alone:
                    pe.wait_ge(s_vg, n)
                for c in range(DC):
                    pe.matmul(ps[:, 1, :], xnT[:, k.u, c, :], w_in[:, c, 0:2 * D], start=c == 0, stop=c == DC - 1)
                for c in range(DC):
                    last = pe.matmul(ps[:, 2, 0:D + 3], xnT[:, k.u, c, :], w_in[:, c, 2 * D:], start=c == 0, stop=c == DC - 1)
                last.then_inc(s_proj, 1)

            def turn_qk(b, k):
                n = b * T + k.t
                done(pe, s_rope, n)
                if not k.alone and not k.last:
                    pe.wait_ge(s_rest1, n)
                for c in range(4):
                    last = pe.transpose(ps[:, qk_bank(k), c * P:(c + 1) * P], roped[:, k.u, c * P:(c + 1) * P], ident_f[:])
                last.then_inc(s_qkt, 1)

            def turn_attn(b, k):
                n = b * T + k.t
                done(pe, s_at, n)
                if not k.alone:
                    pe.wait_ge(s_atT, n)
                turned(4, attn_t, s_at_ps)

            def project_out(b, k):
                n = b * T + k.t
                done(pe, s_atT, n)
                if not k.alone:
                    pe.wait_ge(s_x1, n)
                for c in range(DC):
                    last = pe.matmul(ps[:, 5, 0:D], attnT[:, c, :], w_out[:, c, :], start=c == 0, stop=c == DC - 1)
                last.then_inc(s_wo, 1)

            def turn_x2n(b, k):
                n = b * T + k.t
                done(pe, s_x2n, n)
                if not k.alone:
                    pe.wait_ge(s_x2t, n)
                turned(6, x2n, s_x2t_ps)

            def feed_forward(b, k):
                n = b * T + k.t
                done(pe, s_x2t, n)
                if not k.alone:
                    pe.wait_ge(s_ffs, n)
                for c in range(DC):
                    last = pe.matmul(ps[:, 7, 0:D], x2nT[:, c, :], w_ffn[:, c, :], start=c == 0, stop=c == DC - 1)
                last.then_inc(s_ffn, 1)

            def projections_and_output(ob, pb):
                def step(k, after, before, older):
                    if pb is not None:
                        turn_xn(pb, k)
                    if ob is not None:
                        turn_attn(ob, k)
                    if pb is not None:
                        project(pb, k)
                    if ob is not None:
                        if before:
                            turn_x2n(ob, before)
                        project_out(ob, k)
                    if before:
                        if pb is not None:
                            turn_qk(pb, before)
                        if ob is not None:
                            feed_forward(ob, before)

                over_tiles(pe, step)
                if ob is not None:
                    turn_x2n(ob, known(T - 1))
                if pb is not None:
                    turn_qk(pb, known(T - 1))
                if ob is not None:
                    feed_forward(ob, known(T - 1))

            def selection(b):
                done(pe, s_ktok, b * T + T - 1)
                done(pe, s_rest1, b * T + T - 1)
                done(pe, s_vg, b * T + T - 1)
                done(pe, s_ck, b)
                done(pe, s_qsum, b)
                for g in range(2):
                    last = pe.matmul(ps[0:1, 1, 0:NB], q_sum[:, g:g + 1], ck[:, g, 0:NB], start=g == 0, stop=g == 1)
                last.then_inc(s_imp_ps, 1)
                done(pe, s_top, b * 4 + 3)
                pe.matmul(ps[:, 2, 0:2], ones[0:1, :], sel_start[0:1, 0:2], start=True, stop=True)
                for j in range(2):
                    last = pe.matmul(ps[:, 2, 2:3], sel_rows[0:1, j, :], sel_start[0:1, j:j + 1], start=j == 0, stop=j == 1)
                last.then_inc(s_start_ps, 1)
                done(pe, s_onehot, b * 2 + 1)
                for g in range(2):
                    for t in range(T):
                        last = pe.matmul(ps[:, 4, g * NSEL:(g + 1) * NSEL], k_tok[:, t, g * P:(g + 1) * P], gather[:, t, NB:NCS], start=t == 0, stop=t == T - 1)
                last.then_inc(s_selk_ps, 1)
                pe.wait_ge(s_stack, (b * 2 + 1) * NSLOT * 2 * 16)
                done(pe, s_start, b)
                first_window_scores(b)
                for t in range(T):
                    pe.matmul(ps[0:NCS, 5, 0:D], gather[:, t, :], values[:, t, :], start=t == 0, stop=False)
                pe.matmul(ps[0:NCS, 5, 0:D], wv_rows, pe_sb, start=False, stop=True).then_inc(s_sel_ps, 1)

            def first_window_scores(b):
                for c in range(NU):
                    if c > 1:
                        done(pe, s_fmax, b * NU + c - 2)
                    banks = 2 * (c % 2)
                    for hh in range(U):
                        h = c * U + hh
                        pe.matmul(ps[:, banks + hh // 2, (hh % 2) * KW:(hh % 2 + 1) * KW], q_stack[:, h, 0:P], k_stack[:, h, 0:KW],
                                  start=hh % 2 == 0, stop=False, skip_group_check=True)
                    for j in range(2):
                        last = pe.matmul(ps[:, banks + j, 0:2 * KW].rearrange("p (h k) -> p h k", h=2), ident_b[:],
                                         window_mask[:, 0:1, :].broadcast_to([P, 2, KW]), start=False, stop=True, skip_group_check=True)
                    last.then_inc(s_fa, 1)

            def first_cs_scores(b):
                done(pe, s_fmax, b * NU + NU - 1)
                for c in range(NU):
                    for hh in range(U):
                        h = c * U + hh
                        pe.matmul(ps[:, c, hh * NCS:(hh + 1) * NCS], q_stack[:, h, 0:P], cs_stack[:, h, :], start=hh == 0, stop=False, skip_group_check=True)
                    pe.matmul(ps[:, c, 0:U * NCS].rearrange("p (h k) -> p h k", h=U), ident_b[:],
                              cs_mask[:, 0:1, :].broadcast_to([P, U, NCS]), start=False, stop=True, skip_group_check=True).then_inc(s_a, 1)

            def row_scores(b, t, c):
                pe.wait_ge(s_max, (b * T + t) * NU + c)
                for hh in range(U):
                    h = c * U + hh
                    pe.matmul(ps[:, hh // 2, (hh % 2) * KW:(hh % 2 + 1) * KW], q_stack[:, h, ds(t * P, P)], k_stack[:, h, ds(t * P, KW)],
                              start=hh % 2 == 0, stop=False, skip_group_check=True)
                for j in range(2):
                    pe.matmul(ps[:, j, 0:2 * KW].rearrange("p (h k) -> p h k", h=2), ident_b[:],
                              window_mask[:, 1:2, :].broadcast_to([P, 2, KW]), start=False, stop=True, skip_group_check=True)
                if c == 0:
                    pe.wait_ge(s_mt, 2 * (b * T + t))
                for hh in range(U):
                    h = c * U + hh
                    pe.matmul(ps[:, 2, hh * NCS:(hh + 1) * NCS], q_stack[:, h, ds(t * P, P)], cs_stack[:, h, :], start=hh == 0, stop=False, skip_group_check=True)
                pe.matmul(ps[:, 2, 0:U * NCS].rearrange("p (h k) -> p h k", h=U), ident_b[:],
                          cs_mask[:, ds(t, 1), :].broadcast_to([P, U, NCS]), start=False, stop=True, skip_group_check=True).then_inc(s_a, 1)

            def maxima(b, t):
                done(pe, s_neg, (b * T + t) * 5 + 4)
                settled(pe)
                w = ps[0:48, 2, 0:64].bitcast(BF16)
                cs = ps[0:96, 2, 64:128].bitcast(BF16)
                pe.transpose(w, neg_parts[:, 0].rearrange("p a h -> p (a h)"), ident_b[:])
                pe.transpose(cs, neg_parts[:, 1:3].rearrange("p r a h -> p (r a h)"), ident_b[:]).then_inc(s_mt_ps, 1)

            def column_scores(b, t, c, first):
                k = (b * T + t) * NU + c
                hs = range(c * U, c * U + U)
                if not first:
                    pe.wait_ge(s_exp, k * 3 - 2)
                for hh, h in enumerate(hs):
                    own = ps[:, 3, hh * P:(hh + 1) * P]
                    pe.matmul(own, k_stack[:, h, ds(t * P + WIN, P)], q_stack[:, h, ds(t * P, P)], start=hh == 0, stop=False, skip_group_check=True)
                    pe.matmul(own, pick_w[:, h, 0:P], rows_w[:, ds(t * P, P)], start=False, stop=False, skip_group_check=True)
                pe.matmul(ps[:, 3, :].rearrange("p (h k) -> p h k", h=U), ident_b[:], own_mask[:].unsqueeze(1).broadcast_to([P, U, P]),
                          start=False, stop=True, skip_group_check=True).then_inc(s_b, 1)
                if not first:
                    pe.wait_ge(s_exp, k * 3 - 1)
                for hh, h in enumerate(hs):
                    cs = ps[0:NCS, 4, hh * P:(hh + 1) * P]
                    pe.matmul(cs, cs_stack[:, h, :], q_stack[:, h, ds(t * P, P)], start=hh == 0, stop=False, skip_group_check=True)
                    pe.matmul(cs, pick_cs[0:96, h, :], rows_cs[:, ds(t * P, P)], start=False, stop=False, skip_group_check=True)
                pe.matmul(ps[0:NCS, 4, :].rearrange("p (h k) -> p h k", h=U), ident_b[:, 0:NCS],
                          cs_mask_cols[:, ds(t * P, P)].unsqueeze(1).broadcast_to([P, U, P]), start=False, stop=True, skip_group_check=True).then_inc(s_b, 1)
                if not first:
                    pe.wait_ge(s_exp, k * 3)
                for hh, h in enumerate(hs):
                    before = ps[0:WIN, 5, hh * WIN:(hh + 1) * WIN]
                    pe.matmul(before, k_stack[:, h, ds(t * P, WIN)], q_stack[:, h, ds(t * P, WIN)], start=hh == 0, stop=False, skip_group_check=True)
                    last = pe.matmul(before, pick_w[:, h, P:KW], rows_w[:, ds(t * P, WIN)], start=False, stop=True, skip_group_check=True)
                last.then_inc(s_b, 1)

            def with_values(b, t, c, first):
                n = b * T + t
                if c == 0:
                    pe.wait_ge(s_vt[0], (n + 1) * 48)
                if c == NU - 1:
                    pe.wait_ge(s_vt[1], (n + 1) * 48)
                if c % 2 == 0 and not first:
                    pe.wait_ge(s_wtd, n * 2 - 1 + c // 2)
                s = c % 2
                heads = [(hh, c * U + hh, ps[:, 6 + c // 2, ((c * U + hh) % 8) * OC:((c * U + hh) % 8 + 1) * OC]) for hh in range(U)]
                products = [(0, 0), (0, 1), (0, 2), (1, 0), (1, 1)]
                done(pe, s_low, (n * NU + c) * 2)
                for hh, h, o in heads:
                    for pp, vp in products:
                        w = VC if vp == 0 else HD
                        pe.matmul(o[:, 0:w], own_parts[:, s, pp, hh * P:(hh + 1) * P], v_tile[:, h, V_COLS[vp]],
                                  start=h % 8 == 0 and (pp, vp) == (0, 0), stop=False, skip_group_check=True)
                done(pe, s_low_cs, n * NU + c)
                if first and c == 0:
                    done(pe, s_cvlo, b * 2 + 1)
                for hh, h, o in heads:
                    for pp, vp in products:
                        pe.matmul(o[:, VC:OC], csp_parts[:, s, pp, hh * P:(hh + 1) * P], cs_parts[:, h, vp, :], start=False, stop=True, skip_group_check=True)
                done(pe, s_low, (n * NU + c) * 2 + 1)
                settled(pe)
                for hh, h, o in heads:
                    for vp, rows in ((0, P), (1, P), (2, WIN)):
                        w = VC if vp == 0 else HD
                        last = pe.matmul(o[0:WIN, 0:w], before_parts[0:rows, s, hh * WIN:(hh + 1) * WIN], v_prev[0:rows, h, V_COLS[vp]],
                                         start=False, stop=True, skip_group_check=True)
                last.then_inc(s_pv, 1)

            def tile(b, t, first, ahead):
                n = b * T + t
                for c in range(NU):
                    if ahead:
                        row_scores(b, t + 1, c)
                    if c == 0:
                        pe.wait_ge(s_mt, 2 * (n + 1))
                    column_scores(b, t, c, first and c == 0)
                    if c:
                        with_values(b, t, c - 1, first)
                    elif not first:
                        with_values(b, t - 1, NU - 1, False)
                if ahead:
                    maxima(b, t + 1)

            def attention(b):
                pe.wait_ge(s_cs_in, (b + 1) * NSLOT * 16)
                done(pe, s_smask, b * 3 + 2)
                first_cs_scores(b)
                maxima(b, 0)
                done(pe, s_cks, b * 4)
                done(pe, s_cvrest, b * 2 + 1)
                pe.wait_ge(s_stack, (b + 1) * 2 * NSLOT * 2 * 16)
                tile(b, 0, True, True)
                with pe.Fori(1, T - 1) as t:
                    tile(b, t, False, True)
                tile(b, T - 1, False, False)
                with_values(b, T - 1, NU - 1, False)

            projections_and_output(None, 0)
            with pe.Fori(0, B - 1) as b:
                selection(b)
                attention(b)
                projections_and_output(b, b + 1)
            selection(B - 1)
            attention(B - 1)
            projections_and_output(B - 1, None)

        @block.scalar
        def _(act):
            def copy(o, i):
                return act.activation(o, i, ACT.Copy)

            def chunks(a):
                return a.rearrange("p (c q) -> p c q", c=DC)

            def copy_attention(b, k):
                copy(attn_t, attn[:, ds(k.t, 1), :].rearrange("p a d -> p (a d)")).then_inc(s_at, 1)

            def projections_and_output(ob, pb):
                def step(k, after, before, older):
                    if pb is not None:
                        n = pb * T + k.t
                        done(act, s_xt_ps, n)
                        copy(xnT[:, k.u], chunks(ps[:, 0, 0:D])).then_inc(s_xt, 1)
                    if ob is not None:
                        n = ob * T + k.t
                        done(act, s_at_ps, n)
                        if not k.alone:
                            act.wait_ge(s_wo, n)
                        copy(attnT, chunks(ps[:, 4, 0:D])).then_inc(s_atT, 1)
                    if pb is not None:
                        if older:
                            middle(pb, older)
                        n = pb * T + k.t
                        done(act, s_proj, n)
                        if not k.first_two:
                            act.wait_ge(s_rc, n - 1)
                            act.wait_ge(s_rs, n - 1)
                        copy(qk[:, k.u], ps[:, 1, :]).then_inc(s_qk, 1)
                        copy(values[:, ds(k.t, 1), :].rearrange("p a d -> p (a d)"), ps[:, 2, 0:D])
                        copy(gate[:, ds(k.t, 1), :].rearrange("p a c -> p (a c)"), ps[:, 2, D:D + 3]).then_inc(s_vg, 1)
                    if ob is not None:
                        if before:
                            turn_copied(ob, before)
                        if after:
                            copy_attention(ob, after)
                    if pb is not None and before:
                        high(ob, pb, before)

                def turn_copied(b, k):
                    n = b * T + k.t
                    done(act, s_x2t_ps, n)
                    if not k.alone:
                        act.wait_ge(s_ffn, n)
                    copy(x2nT, chunks(ps[:, 6, 0:D])).then_inc(s_x2t, 1)

                def high(ob, pb, k):
                    n = pb * T + k.t
                    done(act, s_rope, n)
                    if ob is not None:
                        done(act, s_at, ob * T + k.t)
                    copy(k_tok[:, ds(k.t, 1), :].rearrange("p a d -> p (a d)"), roped[:, k.u, D:2 * D]).then_inc(s_ktok, 1)
                    done(act, s_qkt, n)
                    if not k.first_two:
                        act.wait_ge(s_part_out, (pb * PAIRS + k.i - 1) * 48 + 1)
                    copy(parts[:, 0, :, here(k)], ps[:, qk_bank(k), :].rearrange("p (c q) -> p c q", c=4)).then_inc(s_hi, 1)

                def middle(pb, k):
                    done(act, s_rest, pb * T + k.t)
                    copy(parts[:, 1, :, here(k)], rest[:, k.u]).then_inc(s_mid, 1)

                if ob is not None:
                    done(act, s_attn, (ob * T + T - 1) * 2 + 1)
                    copy_attention(ob, known(0))
                over_tiles(act, step)
                if ob is not None:
                    turn_copied(ob, known(T - 1))
                if pb is not None:
                    high(ob, pb, known(T - 1))
                    middle(pb, known(T - 2))
                    middle(pb, known(T - 1))

            def probabilities(b, t, c, first):
                k = (b * T + t) * NU + c
                if not first:
                    act.wait_ge(s_pv, k - 1)
                s = c % 2
                for j, (full, halves, scores) in enumerate((
                    (p_own[:, s, :], own_parts[:, s, 0, :], ps[:, 3, :]),
                    (p_cs[:, s, :], csp_parts[:, s, 0, :], ps[0:NCS, 4, :]),
                    (p_before[:, s, :], before_parts[0:WIN, s, :], ps[0:WIN, 5, 0:U * WIN]),
                )):
                    done(act, s_b, k * 3 + j)
                    bias = p_bias[0:full.shape[0], :]
                    act.activation(full, scores, ACT.Exp, bias=bias)
                    act.activation(halves, scores, ACT.Exp, bias=bias).then_inc(s_exp, 1)

            def selection_and_attention(b):
                done(act, s_vg, b * T + T - 1)
                by_head = lambda a: a.rearrange("p t (h d) -> p t h d", h=H)
                copy(v_parts[:, :, :, 0:HD], by_head(values[:])).then_inc(s_vhi, 1)
                done(act, s_vrest, b)
                copy(v_parts[:, :, :, V_COLS[1]], by_head(v_rest[:])).then_inc(s_vmid, 1)
                done(act, s_gsub, b * 3 + 2)
                act.activation(gate[:], gate[:], ACT.Exp).then_inc(s_gexp, 1)
                done(act, s_sel_ps, b)
                for rows, at in cs_places:
                    copy(cs_parts[rows, :, 0, at:at + HD], ps[rows, 5, 0:D].rearrange("p (h d) -> p h d", h=H)).then_inc(s_cvhi, 1)
                for k, (rows, at) in enumerate(cs_places):
                    done(act, s_cvrest, b * 2 + k)
                    copy(cs_parts[rows, :, 1, at:at + HD], cs_rest[rows]).then_inc(s_cvmid, 1)
                for c in range(NU):
                    probabilities(b, 0, c, c < 2)
                with act.Fori(1, T) as t:
                    for c in range(NU):
                        probabilities(b, t, c, False)

            projections_and_output(None, 0)
            with act.Fori(0, B - 1) as b:
                selection_and_attention(b)
                projections_and_output(b, b + 1)
            selection_and_attention(B - 1)
            projections_and_output(B - 1, None)

        @block.vector
        def _(dve):
            dve.memset(ones[:], 1.0)
            dve.memset(minus_half[:], -0.5)
            dve.memset(p_bias[:], P_BIAS)
            dve.memset(v_parts[:, :, :, HD:VC], 1.0)
            dve.memset(k_stack[:, :, 0:WIN], 0.0)
            dve.memset(cs_parts[:], 0.0).then_inc(s_setup, 1)
            dve.wait_ge(s_setup, 1)
            dve.memset(cs_parts[0:NB, :, 0, HD:VC], 1.0)
            dve.memset(cs_parts[NB:NCS, :, 0, 2 * VC - 1:2 * VC], 1.0).then_inc(s_w, 1)
            dve.wait_ge(s_const, 16 * len(loads))
            dve.tensor_scalar(w_in[:, :, 0:D], w_in[:, :, 0:D], 1.0 / float(np.sqrt(HD)), None, ALU.mult)
            dve.tensor_scalar(scb_all[:], scb_all[:], 1.0 / 127.0, None, ALU.mult)
            dve.tensor_scalar(gather[:], block_of[:], wv_col[:, 0:1], None, ALU.mult)
            dve.tensor_scalar(wk_rows, ones[0:16, 0:NB], wk_col[0:16, 0:1], None, ALU.mult)
            dve.memset(wv_rows, 0.0).then_inc(s_setup, 1)
            dve.wait_ge(s_setup, 2)
            dve.tensor_scalar(wv_rows[:, 0:NB], ones[0:16, 0:NB], wv_col[0:16, 0:1], None, ALU.mult).then_inc(s_w, 1)
            dve.wait_ge(s_setup_pe, 1)
            dve.tensor_copy(w_ffn[:], ps[:, 0:DC, 0:D]).then_inc(s_w, 1)
            dve.wait_ge(s_setup_pe, 2)
            dve.tensor_copy(pe_key[:], ps[:, 2, 0:2]).then_inc(s_w, 1)

            def statistics(n, which, u, src, bn, mv, ve):
                dve.bn_stats(bn6[:, which, u], src).then_inc(bn, 1)
                done(dve, bn, n)
                settled(dve)
                dve.bn_aggr(mean_var[:, which, u], bn6[:, which, u]).then_inc(mv, 1)
                done(dve, mv, n)
                dve.tensor_scalar(var_eps[:, which, u:u + 1], mean_var[:, which, u, 1:2], EPS, None, ALU.add).then_inc(ve, 1)

            def x_tile(k):
                return x_in[:, ds(k.t, 1), :].rearrange("p a d -> p (a d)")

            def normalise_x(b, k):
                n = b * T + k.t
                done(dve, s_rstd, n)
                if not k.first_two:
                    dve.wait_ge(s_xt_ps, n - 1)
                dve.tensor_scalar(xn[:, k.u], x_tile(k), mean_var[:, 0, k.u, 0:1], rstd[:, 0, k.u:k.u + 1],
                                  ALU.subtract, ALU.mult).then_inc(s_xn, 1)

            def by_16(a):
                return a.rearrange("p (h d) -> p h d", d=HD)

            def rope_cos(b, k):
                n = b * T + k.t
                done(dve, s_qk, n)
                if not k.first_two:
                    dve.wait_ge(s_qkt, n - 1)
                    dve.wait_ge(s_ktok, n - 1)
                dve.tensor_tensor(by_16(roped[:, k.u]), by_16(qk[:, k.u]), cos[:, ds(k.t, 1), :].broadcast_to([P, 2 * H, HD]), ALU.mult).then_inc(s_rc, 1)

            def rope_add(b, k):
                n = b * T + k.t
                done(dve, s_rc, n)
                done(dve, s_rs, n)
                dve.tensor_tensor(roped[:, k.u], roped[:, k.u], rope_s[:, k.u], ALU.add).then_inc(s_rope, 1)

            def split(b, k):
                n = b * T + k.t
                done(dve, s_hi, n)
                if not k.first_two:
                    done(dve, s_lo, n - 2)
                if not k.alone:
                    done(dve, s_ckt, n - 1)
                    settled(dve)
                dve.tensor_tensor(rest[:, k.u], ps[:, qk_bank(k), :].rearrange("p (c q) -> p c q", c=4), parts[:, 0, :, here(k)], ALU.subtract).then_inc(s_rest, 1)
                dve.tensor_tensor(by_16(weighted_k[:]), by_16(ps[:, qk_bank(k), D:2 * D]), wk_all[:].unsqueeze(1).broadcast_to([P, 16, 16]), ALU.mult).then_inc(s_wk, 1)
                dve.tensor_reduce(q_sums[:, ds(k.t, 1), :].rearrange("p a g -> p (a g)"), ps[:, qk_bank(k), 0:D].rearrange("p (g s) -> p g s", g=2), AX.X, ALU.add).then_inc(s_rest1, 1)
                done(dve, s_wk, n)
                dve.tensor_reduce(ck[:, :, ds(k.t * 8, 8)], weighted_k[:].rearrange("p (g n k) -> p g n k", g=2, k=16), AX.X, ALU.add).then_inc(s_ckt, 1)

            def low(b, k):
                n = b * T + k.t
                done(dve, s_mid, n)
                settled(dve)
                dve.tensor_tensor(parts[:, 2, :, here(k)], rest[:, k.u], parts[:, 1, :, here(k)], ALU.subtract).then_inc(s_lo, 1)

            def selection(b):
                done(dve, s_ckt, b * T + T - 1)
                done(dve, s_rest1, b * T + T - 1)
                dve.tensor_tensor(ck[:, :, 0:NB], ck[:, :, 0:NB], pe_key[:].unsqueeze(2).broadcast_to([P, 2, NB]), ALU.add).then_inc(s_ck, 1)
                dve.tensor_reduce(q_sum[:], q_sums[:].rearrange("p t g -> p g t"), AX.X, ALU.add).then_inc(s_qsum, 1)
                low(b, known(T - 2))
                low(b, known(T - 1))
                done(dve, s_imp_ps, b)
                dve.tensor_copy(imp[:], ps[0:1, 1, 0:NB]).then_inc(s_top, 1)
                done(dve, s_top, b * 4)
                settled(dve)
                dve.max(imp_max[:], imp[:]).then_inc(s_top, 1)
                done(dve, s_top, b * 4 + 1)
                settled(dve)
                dve.max_index(imp_idx[:], imp_max[:], imp[:]).then_inc(s_top, 1)
                done(dve, s_top, b * 4 + 2)
                dve.tensor_scalar(sel_start[:], imp_idx[:], 16.0, None, ALU.mult).then_inc(s_top, 1)
                done(dve, s_start_ps, b)
                dve.tensor_copy(start_all[:], ps[:, 2, 0:3]).then_inc(s_start, 1)
                done(dve, s_start, b)
                for j in range(2):
                    cols = slice(NB + 8 * j, NB + 8 * j + 8)
                    dve.tensor_scalar(gather[:, :, cols], since[:], start_all[:, j:j + 1], None, ALU.is_equal).then_inc(s_onehot, 1)
                for j in range(2):
                    cols = slice(NB + 8 * j, NB + 8 * j + 8)
                    dve.tensor_scalar(cs_mask[:, :, cols], since[:], start_all[:, j:j + 1], MASKED, ALU.is_lt, ALU.mult).then_inc(s_smask, 1)
                dve.tensor_scalar(cs_mask_cols[NB:NCS, :], since_cols, start_all[NB:NCS, 2:3], MASKED, ALU.is_lt, ALU.mult).then_inc(s_smask, 1)
                by_head = lambda a: a.rearrange("p t (h d) -> p t h d", h=H)
                done(dve, s_vhi, b)
                dve.tensor_tensor(by_head(v_rest[:]), by_head(values[:]), v_parts[:, :, :, 0:HD], ALU.subtract).then_inc(s_vrest, 1)
                dve.tensor_tensor(gate[:], gate[:], bg_all[:].unsqueeze(1).broadcast_to([P, T, 3]), ALU.add).then_inc(s_gsub, 1)
                done(dve, s_gsub, b * 3)
                dve.tensor_reduce(gate_max[:], gate[:], AX.X, ALU.max).then_inc(s_gsub, 1)
                done(dve, s_gsub, b * 3 + 1)
                dve.tensor_tensor(gate[:], gate[:], gate_max[:].unsqueeze(2).broadcast_to([P, T, 3]), ALU.subtract).then_inc(s_gsub, 1)
                done(dve, s_selk_ps, b)
                dve.tensor_copy(ck[:, :, NB:NCS], ps[:, 4, 0:2 * NSEL].rearrange("p (g n) -> p g n", g=2)).then_inc(s_cks, 1)
                done(dve, s_cks, b * 4)
                dve.tensor_copy(ck_parts[:, 0], ck[:]).then_inc(s_cks, 1)
                done(dve, s_cks, b * 4 + 1)
                dve.tensor_tensor(ck_rest[:], ck[:], ck_parts[:, 0], ALU.subtract).then_inc(s_cks, 1)
                done(dve, s_cks, b * 4 + 2)
                dve.tensor_copy(ck_parts[:, 1], ck_rest[:]).then_inc(s_cks, 1)
                done(dve, s_cks, b * 4 + 3)
                dve.tensor_tensor(ck_parts[:, 2], ck_rest[:], ck_parts[:, 1], ALU.subtract).then_inc(s_ckp, 1)
                done(dve, s_vmid, b)
                dve.tensor_tensor(v_parts[:, :, :, V_COLS[2]], by_head(v_rest[:]), v_parts[:, :, :, V_COLS[1]], ALU.subtract).then_inc(s_vlo, 1)
                reduce_first_windows(b)

            def selected_values(b):
                done(dve, s_sel_ps, b)
                for k, (rows, at) in enumerate(cs_places):
                    done(dve, s_cvhi, b * 2 + k)
                    dve.tensor_tensor(cs_rest[rows], ps[rows, 5, 0:D].rearrange("p (h d) -> p h d", h=H), cs_parts[rows, :, 0, at:at + HD],
                                      ALU.subtract).then_inc(s_cvrest, 1)
                done(dve, s_gexp, b)
                dve.tensor_reduce(gate_sum[:], gate[:], AX.X, ALU.add).then_inc(s_gate, 1)
                done(dve, s_gate, b * 4)
                dve.reciprocal(gate_inv[:], gate_sum[:]).then_inc(s_gate, 1)
                done(dve, s_gate, b * 4 + 1)
                for to, of, n in ((0, 2, 1), (1, 0, 2)):
                    dve.tensor_tensor(branch_gate[:, :, to:to + n], gate[:, :, of:of + n], gate_inv[:].unsqueeze(2).broadcast_to([P, T, n]),
                                      ALU.mult).then_inc(s_gate, 1)
                for k, (rows, at) in enumerate(cs_places):
                    done(dve, s_cvmid, b * 2 + k)
                    dve.tensor_tensor(cs_parts[rows, :, 2, at:at + HD], cs_rest[rows], cs_parts[rows, :, 1, at:at + HD], ALU.subtract).then_inc(s_cvlo, 1)
                done(dve, s_gate, b * 4 + 3)

            def reduce_unit(b, t, c):
                done(dve, s_a, (b * T + t) * NU + c)
                hs = slice(c * U, c * U + U)
                dve.tensor_reduce(neg_max[:, 0, hs].rearrange("p (j h) -> p j h", j=2),
                                  ps[:, 0:2, 0:2 * KW].rearrange("p j (h k) -> p j h k", h=2), AX.X, ALU.max, negate=True)
                cs = ps[:, 2, 0:U * NCS].rearrange("p (h k) -> p h k", h=U)
                dve.tensor_reduce(neg_max[:, 1, hs], cs[:, :, 0:NB], AX.X, ALU.max, negate=True)
                dve.tensor_reduce(neg_max[:, 2, hs], cs[:, :, NB:NCS], AX.X, ALU.max, negate=True).then_inc(s_max, 1)

            def reduce_first_windows(b):
                for c in range(NU):
                    done(dve, s_fa, b * NU + c)
                    banks = 2 * (c % 2)
                    dve.tensor_reduce(neg_max[:, 0, c * U:c * U + U].rearrange("p (j h) -> p j h", j=2),
                                      ps[:, banks:banks + 2, 0:2 * KW].rearrange("p j (h k) -> p j h k", h=2), AX.X, ALU.max, negate=True).then_inc(s_fmax, 1)

            def reduce_first_cs(b):
                for c in range(NU):
                    done(dve, s_a, b * T * NU + c)
                    cs = ps[:, c, 0:U * NCS].rearrange("p (h k) -> p h k", h=U)
                    dve.tensor_reduce(neg_max[:, 1, c * U:c * U + U], cs[:, :, 0:NB], AX.X, ALU.max, negate=True)
                    dve.tensor_reduce(neg_max[:, 2, c * U:c * U + U], cs[:, :, NB:NCS], AX.X, ALU.max, negate=True).then_inc(s_max, 1)

            def split_maxima(b, t):
                n = b * T + t
                done(dve, s_max, n * NU + NU - 1)
                dve.tensor_scalar(neg_lim[:], neg_max[:], LEAST, None, ALU.min).then_inc(s_neg, 1)
                done(dve, s_neg, n * 5)
                dve.tensor_copy(neg_parts[:, :, 0], neg_lim[:]).then_inc(s_neg, 1)
                done(dve, s_neg, n * 5 + 1)
                dve.tensor_tensor(neg_rest[:], neg_lim[:], neg_parts[:, :, 0], ALU.subtract).then_inc(s_neg, 1)
                done(dve, s_neg, n * 5 + 2)
                dve.tensor_copy(neg_parts[:, :, 1], neg_rest[:]).then_inc(s_neg, 1)
                done(dve, s_neg, n * 5 + 3)
                dve.tensor_tensor(neg_parts[:, :, 2], neg_rest[:], neg_parts[:, :, 1], ALU.subtract).then_inc(s_neg, 1)

            def copy_maxima(b, t):
                done(dve, s_mt_ps, b * T + t)
                dve.tensor_copy(rows_w[0:48, ds(t * P, P)], ps[0:48, 2, 0:64].bitcast(BF16)).then_inc(s_mt, 1)
                dve.tensor_copy(rows_cs[0:96, ds(t * P, P)], ps[0:96, 2, 64:128].bitcast(BF16)).then_inc(s_mt, 1)
                done(dve, s_mt, (b * T + t) * 2 + 1)
                settled(dve)

            def low_parts(b, t, c):
                k = (b * T + t) * NU + c
                s = c % 2
                done(dve, s_exp, k * 3)
                dve.tensor_tensor(own_parts[:, s, 1, :], p_own[:, s, :], own_parts[:, s, 0, :], ALU.subtract).then_inc(s_low, 1)
                done(dve, s_exp, k * 3 + 2)
                dve.tensor_tensor(before_parts[WIN:P, s, :], p_before[:, s, :], before_parts[0:WIN, s, :], ALU.subtract).then_inc(s_low, 1)

            def combine(b, t, j):
                m = (b * T + t) * 2 + j
                done(dve, s_pv, (b * T + t) * NU + 2 * j + 1)
                hs = slice(8 * j, 8 * j + 8)
                o = ps[:, 6 + j, 0:8 * OC].rearrange("p (h r d) -> p h r d", h=8, r=3)
                dve.tensor_scalar(den[:, hs, :].unsqueeze(3), o[:, :, :, HD:VC], 1e-30, None, ALU.max).then_inc(s_den, 1)
                done(dve, s_den, m * 3)
                dve.reciprocal(den_inv[:, hs], den[:, hs]).then_inc(s_den, 1)
                done(dve, s_den, m * 3 + 1)
                dve.tensor_tensor(weight[:, hs], den_inv[:, hs], branch_gate[:, ds(t, 1), :].broadcast_to([P, 8, 3]), ALU.mult).then_inc(s_den, 1)
                done(dve, s_den, m * 3 + 2)
                dve.tensor_tensor(weighted[:], o[:, :, :, 0:HD], weight[:, hs].unsqueeze(3).broadcast_to([P, 8, 3, HD]),
                                  ALU.mult).then_inc(s_wtd, 1)
                done(dve, s_wtd, m)
                dve.tensor_reduce(attn[:, ds(t, 1), P * j:P * j + P].rearrange("p a (h d) -> p (a h) d", h=8),
                                  weighted[:].rearrange("p h r d -> p h d r"), AX.X, ALU.add).then_inc(s_attn, 1)
                done(dve, s_attn, m)
                settled(dve)

            def attend(b, t, first, ahead):
                for c in range(NU):
                    if c:
                        low_parts(b, t, c - 1)
                    elif not first:
                        low_parts(b, t - 1, NU - 1)
                    if ahead:
                        reduce_unit(b, t + 1, c)
                    if c < 2 and not first:
                        combine(b, t - 1, c)
                if ahead:
                    split_maxima(b, t + 1)
                    copy_maxima(b, t + 1)

            def residual(b, k):
                n = b * T + k.t
                done(dve, s_wo, n)
                done(dve, s_xrb, n)
                if not k.first_two:
                    dve.wait_ge(s_x1b, n - 1)
                dve.tensor_tensor(x1[:, k.u], ps[:, 5, 0:D], x_res[:, k.u], ALU.add).then_inc(s_x1, 1)
                done(dve, s_x1, n)
                statistics(n, 1, k.u, x1[:, k.u], s_bn2, s_mv2, s_ve2)

            def normalise_x1(b, k):
                n = b * T + k.t
                done(dve, s_rstd2, n)
                if not k.alone:
                    dve.wait_ge(s_x2t_ps, n)
                dve.tensor_scalar(x2n, x1[:, k.u], mean_var[:, 1, k.u, 0:1], rstd[:, 1, k.u:k.u + 1], ALU.subtract, ALU.mult).then_inc(s_x2n, 1)

            def result(b, k):
                n = b * T + k.t
                done(dve, s_ffn, n)
                if not k.alone:
                    done(dve, s_y, n - 1)
                dve.tensor_tensor(ffn, ps[:, 7, 0:D], scb_all[:], ALU.mult).then_inc(s_ffs, 1)
                done(dve, s_ffs, n)
                done(dve, s_x1b, n)
                if not k.first_two:
                    dve.wait_ge(s_out[k.u], (b * PAIRS + k.i) * 16)
                dve.tensor_tensor(y[:, k.u], ffn, x1b[:, k.u], ALU.add).then_inc(s_y, 1)

            def projections_and_output(ob, pb):
                def step(k, after, before, older):
                    ahead = pb is not None and after is not None
                    if ahead:
                        if not after.first_two:
                            done(dve, s_xn, pb * T + after.t - 2)
                        statistics(pb * T + after.t, 0, after.u, x_tile(after), s_bn, s_mv, s_ve)
                    if pb is not None and older:
                        low(pb, older)
                    if ahead:
                        normalise_x(pb, after)
                    if pb is not None:
                        rope_cos(pb, k)
                    if ob is not None:
                        if not k.first_two:
                            done(dve, s_x2n, ob * T + k.t - 2)
                        residual(ob, k)
                    if pb is not None:
                        rope_add(pb, k)
                    if ob is not None:
                        if before:
                            result(ob, before)
                        normalise_x1(ob, k)
                    if pb is not None and before:
                        split(pb, before)

                if pb is not None:
                    dve.wait_ge(s_x, (pb + 1) * 16)
                    statistics(pb * T, 0, 0, x_tile(known(0)), s_bn, s_mv, s_ve)
                    normalise_x(pb, known(0))
                over_tiles(dve, step)
                if pb is not None:
                    done(dve, s_xn, pb * T + T - 1)
                    settled(dve)
                    dve.sem_inc(s_xused, 1)
                    split(pb, known(T - 1))
                if ob is not None:
                    result(ob, known(T - 1))

            def attention(b):
                reduce_first_cs(b)
                split_maxima(b, 0)
                copy_maxima(b, 0)
                selected_values(b)
                attend(b, 0, True, True)
                with dve.Fori(1, T - 1) as t:
                    attend(b, t, False, True)
                attend(b, T - 1, False, False)
                combine(b, T - 1, 0)
                low_parts(b, T - 1, NU - 1)
                combine(b, T - 1, 1)

            projections_and_output(None, 0)
            with dve.Fori(0, B - 1) as b:
                selection(b)
                attention(b)
                projections_and_output(b, b + 1)
            selection(B - 1)
            attention(B - 1)
            projections_and_output(B - 1, None)

        @block.gpsimd
        def _(pool):
            def deviation(n, which, u, ve, out_sem):
                done(pool, ve, n)
                pool.tensor_tensor(rstd[:, which, u:u + 1], var_eps[:, which, u:u + 1], minus_half[:], ALU.pow).then_inc(out_sem, 1)

            def sin_products(b, k):
                n = b * T + k.t
                heads = lambda a: a.rearrange("p (h d) -> p h d", d=HD)
                done(pool, s_qk, n)
                if not k.first_two:
                    pool.wait_ge(s_rope, n - 1)
                for e in range(2):
                    s = sin[:, ds(k.t, 1), e::2].broadcast_to([P, 2 * H, HD // 2])
                    last = pool.tensor_tensor(heads(rope_s[:, k.u])[:, :, e::2], heads(qk[:, k.u])[:, :, 1 - e::2], s, ALU.mult)
                last.then_inc(s_rs, 1)

            def projections_and_output(ob, pb):
                def step(k, after, before, older):
                    if pb is not None and after:
                        deviation(pb * T + after.t, 0, after.u, s_ve, s_rstd)
                    if ob is not None:
                        pool.wait_ge(s_xr[k.u], (ob * (PAIRS + 1) + k.i + 1) * 16)
                        pool.tensor_tensor(x_res[:, k.u], x_res[:, k.u], bo_all[:], ALU.add).then_inc(s_xrb, 1)
                    if pb is not None:
                        sin_products(pb, k)
                    if ob is not None:
                        n = ob * T + k.t
                        deviation(n, 1, k.u, s_ve2, s_rstd2)
                        if not k.first_two:
                            pool.wait_ge(s_y, n - 1)
                        pool.tensor_tensor(x1b[:, k.u], x1[:, k.u], bias_all[:], ALU.add).then_inc(s_x1b, 1)

                if pb is not None:
                    deviation(pb * T, 0, 0, s_ve, s_rstd)
                over_tiles(pool, step)

            def attention(b):
                with pool.Fori(0, T) as t:
                    for c in range(NU):
                        k = (b * T + t) * NU + c
                        done(pool, s_exp, k * 3 + 1)
                        pool.tensor_tensor(csp_parts[:, c % 2, 1, :], p_cs[:, c % 2, :], csp_parts[:, c % 2, 0, :], ALU.subtract).then_inc(s_low_cs, 1)

            pool.wait_ge(s_const, 16 * len(loads))
            pool.wait_ge(s_w, 1)
            projections_and_output(None, 0)
            with pool.Fori(0, B - 1) as b:
                attention(b)
                projections_and_output(b, b + 1)
            attention(B - 1)
            projections_and_output(B - 1, None)


INS = ["L0_attn_x", "L0_attn_Wq", "L0_attn_Wk", "L0_attn_Wv", "L0_attn_Wo", "L0_attn_bo", "L0_attn_wk_comp",
       "L0_attn_wv_comp", "L0_attn_pe", "L0_attn_Wg", "L0_attn_bg", "L0_ffn_CB", "L0_ffn_SCB", "L0_ffn_bias"]


def kernel(**inputs):
    import numpy as _np
    import concourse.bacc as _bacc
    from concourse import mybir as _mybir
    from concourse.bass_utils import run_bass_kernel_spmd as _run

    nc = _bacc.Bacc("TRN2", target_bir_lowering=False, num_devices=1)
    arrays, args = {}, []
    for name in INS:
        a = _np.ascontiguousarray(inputs[name])
        arrays[f"in_{name}"] = a
        args.append(nc.dram_tensor(f"in_{name}", a.shape, _mybir.dt.from_np(a.dtype), kind="ExternalInput").ap())
    consts = {}
    for group in shape_constants():
        for name, a in group.items():
            arrays[f"const_{name}"] = a
            consts[name] = nc.dram_tensor(f"const_{name}", a.shape, _mybir.dt.from_np(a.dtype), kind="ExternalInput").ap()
    out = nc.dram_tensor("out", (B, S, D), _mybir.dt.float32, kind="ExternalOutput").ap()
    build(nc, *args, consts, out)
    r = _run(nc, [arrays], core_ids=[0])
    return r.results[0]["out"]
```
